# Optimizing a Trainium2 kernel written in Bass

```python
import numpy as np
import jax
import jax.numpy as jnp

def _softmax(x, axis=-1):
    return jax.nn.softmax(x, axis=axis)

def _gelu(x):
    return jax.nn.gelu(x, approximate=True)

def _silu(x):
    return jax.nn.silu(x)

def _sigmoid(x):
    return jax.nn.sigmoid(x)

def _layernorm(x, axis=-1, eps=1e-05):
    m = jnp.mean(x, axis=axis, keepdims=True)
    v = jnp.var(x, axis=axis, keepdims=True)
    return (x - m) / jnp.sqrt(v + eps)

def _scatter_add(tgt, idx, src, axis=0):
    return tgt.at[idx].add(src)

def _segment_sum(src, seg, n):
    return jax.ops.segment_sum(src, seg, n)
kernel_name = 'mk_hybrid_d1_jaxref_r8_e2a445'

def setup_inputs(seed: int=0):
    np.random.seed(seed)
    _w = jnp.asarray

    def _L0_attn_a_setup():
        import jax, jax.numpy as jnp
        import numpy as np
        import math
        B, T, D_MODEL = (2, 256, 128)
        H_Q, H_KV, D_HEAD = (16, 4, 64)
        N_REP = H_Q // H_KV
        MAX_SEQ_LEN = 256
        ROPE_THETA = 10000.0
        NEG = -1000000000.0

        def _rope(x, position_offset=0):
            Bx, Hx, Tx, Dx = x.shape
            half = Dx // 2
            inv_freq = 1.0 / ROPE_THETA ** (jnp.arange(0, half, dtype=jnp.float32) / half)
            pos = jnp.arange(position_offset, position_offset + Tx, dtype=jnp.float32)
            ang = pos[:, None] * inv_freq[None, :]
            cos, sin = (jnp.cos(ang), jnp.sin(ang))
            x1, x2 = (x[..., :half], x[..., half:])
            return jnp.concatenate([x1 * cos - x2 * sin, x2 * cos + x1 * sin], axis=-1)
        key = jax.random.key(seed)
        ks = jax.random.split(key, 7)
        s = 0.02
        return {'x': jax.random.normal(ks[0], (B, T, D_MODEL), dtype=jnp.float32), 'Wq': jax.random.normal(ks[1], (D_MODEL, H_Q * D_HEAD), dtype=jnp.float32) * s, 'Wk': jax.random.normal(ks[2], (D_MODEL, H_KV * D_HEAD), dtype=jnp.float32) * s, 'Wv': jax.random.normal(ks[3], (D_MODEL, H_KV * D_HEAD), dtype=jnp.float32) * s, 'Wo': jax.random.normal(ks[4], (H_Q * D_HEAD, D_MODEL), dtype=jnp.float32) * s, 'polarity_direction': jax.random.normal(ks[5], (H_Q,), dtype=jnp.float32) * 0.5, 'gtp_gamma': jax.random.uniform(ks[6], (H_Q,), dtype=jnp.float32, minval=0.001, maxval=0.02)}
    _L0_attn_a_in = _L0_attn_a_setup()

    def _L0_attn_b_setup():
        import jax, jax.numpy as jnp
        import numpy as np
        B, S, D = (16, 64, 128)
        H, NQ = (16, 8)
        HD = D // H
        key = jax.random.key(seed)
        ks = jax.random.split(key, 8)

        def lin(k, fi, fo):
            return (jax.random.normal(k, (fi, fo), jnp.float32) / np.sqrt(fi)).astype(jnp.float32)
        x = jax.random.normal(ks[0], (B, S, D), jnp.float32)
        wq, wk, wv, wo = (lin(ks[1], D, D), lin(ks[2], D, D), lin(ks[3], D, D), lin(ks[4], D, D))
        bq = jnp.zeros((D,), jnp.float32)
        bk = jnp.zeros((D,), jnp.float32)
        bv = jnp.zeros((D,), jnp.float32)
        bo = jnp.zeros((D,), jnp.float32)
        w1 = lin(ks[5], HD, D)
        b1 = jnp.zeros((D,), jnp.float32)
        w2 = lin(ks[6], D, 2 * NQ)
        b2 = jnp.zeros((2 * NQ,), jnp.float32)
        i = jnp.arange(NQ, dtype=jnp.float32)
        hadamard = jnp.ones((NQ, NQ), jnp.float32) / np.sqrt(NQ) * jnp.cos(2 * np.pi * i / NQ)[:, None]
        rot = jax.random.uniform(ks[7], (H, NQ, 3), jnp.float32, -np.pi, np.pi)
        return dict(x=x, wq=wq, bq=bq, wk=wk, bk=bk, wv=wv, bv=bv, wo=wo, bo=bo, w1=w1, b1=b1, w2=w2, b2=b2, hadamard=hadamard, rot=rot)
    _L0_attn_b_in = _L0_attn_b_setup()

    def _L0_ffn_setup():
        import jax, jax.numpy as jnp
        import numpy as np
        DIM = 128
        DEPTH = 2
        HEADS = 8
        DIM_HEAD = 64
        WINDOW = 64
        INNER = HEADS * DIM_HEAD
        HID = int(DIM * 4 * 2 / 3)
        B, N = (2, 1024)
        QK_SCALE = 8.0

        def shift_token(t):
            t1, t2 = jnp.split(t, 2, axis=-1)
            t2 = jnp.pad(t2, ((0, 0), (1, 0), (0, 0)))[:, :-1]
            return jnp.concatenate([t1, t2], axis=-1)

        def l2norm(t):
            return t / jnp.clip(jnp.linalg.norm(t, axis=-1, keepdims=True), 1e-12)

        def rotate_half(x):
            x1, x2 = jnp.split(x, 2, axis=-1)
            return jnp.concatenate([-x2, x1], axis=-1)

        def rotary_xpos(q, k):
            n = q.shape[-2]
            half_idx = jnp.arange(0, DIM_HEAD, 2, dtype=jnp.float32)
            inv_freq = 1.0 / 10000.0 ** (half_idx / DIM_HEAD)
            t = jnp.arange(n, dtype=jnp.float32)
            freqs = t[:, None] * inv_freq[None, :]
            freqs = jnp.concatenate([freqs, freqs], axis=-1)
            base = (half_idx + 0.4 * DIM_HEAD) / (1.4 * DIM_HEAD)
            power = (t - n // 2) / float(WINDOW // 2)
            scale = base[None, :] ** power[:, None]
            scale = jnp.concatenate([scale, scale], axis=-1)
            cos, sin = (jnp.cos(freqs), jnp.sin(freqs))
            q = q * cos * scale + rotate_half(q) * sin * scale
            k = k * cos / scale + rotate_half(k) * sin / scale
            return (q, k)

        def local_attention(q, k, v):
            b, h, n, d = q.shape
            w = n // WINDOW
            bq = q.reshape(b, h, w, WINDOW, d) * QK_SCALE
            bk = k.reshape(b, h, w, WINDOW, d)
            bv = v.reshape(b, h, w, WINDOW, d)

            def look_around(t):
                p = jnp.pad(t, ((0, 0), (0, 0), (1, 0), (0, 0), (0, 0)))
                return jnp.concatenate([p[:, :, :w], p[:, :, 1:]], axis=3)
            bk, bv = (look_around(bk), look_around(bv))
            bt = jnp.arange(n).reshape(w, WINDOW)
            btp = jnp.pad(bt, ((1, 0), (0, 0)), constant_values=-1)
            btk = jnp.concatenate([btp[:w], btp[1:]], axis=1)
            sim = jnp.einsum('bhwid,bhwjd->bhwij', bq, bk)
            i = bt[:, :, None]
            j = btk[:, None, :]
            mask = (i < j) | (i > j + WINDOW) | (j == -1)
            sim = jnp.where(mask, -jnp.finfo(sim.dtype).max, sim)
            attn = jax.nn.softmax(sim, axis=-1)
            out = jnp.einsum('bhwij,bhwjd->bhwid', attn, bv)
            return out.reshape(b, h, n, d)

        def _layer(x, wqkv, qs, ksc, wo, lg, lb, w1, b1, w2, b2):
            b, n, _ = x.shape
            h = shift_token(x)
            qkv = h @ wqkv
            q, k, v = jnp.split(qkv, 3, axis=-1)
            to_heads = lambda t: t.reshape(b, n, HEADS, DIM_HEAD).transpose(0, 2, 1, 3)
            q, k, v = (to_heads(q), to_heads(k), to_heads(v))
            q = l2norm(q) * qs
            k = l2norm(k) * ksc
            q, k = rotary_xpos(q, k)
            o = local_attention(q, k, v)
            o = o.transpose(0, 2, 1, 3).reshape(b, n, INNER)
            x = x + o @ wo
            h = shift_token(x)
            mu = h.mean(-1, keepdims=True)
            var = h.var(-1, keepdims=True)
            h = (h - mu) / jnp.sqrt(var + 1e-05) * lg + lb
            h = h @ w1 + b1
            a, g = jnp.split(h, 2, axis=-1)
            h = a * jax.nn.gelu(g, approximate=False)
            x = x + h @ w2 + b2
            return x
        key = jax.random.key(seed)
        ks = jax.random.split(key, 6)
        return {'x': jax.random.normal(ks[0], (B, N, DIM), jnp.float32), 'wqkv': jax.random.normal(ks[1], (DEPTH, DIM, 3 * INNER), jnp.float32) * 0.02, 'q_scale': jnp.ones((DEPTH, DIM_HEAD), jnp.float32), 'k_scale': jnp.ones((DEPTH, DIM_HEAD), jnp.float32), 'wo': jax.random.normal(ks[2], (DEPTH, INNER, DIM), jnp.float32) * 0.02, 'ln_g': jnp.ones((DEPTH, DIM), jnp.float32), 'ln_b': jnp.zeros((DEPTH, DIM), jnp.float32), 'w1': jax.random.normal(ks[3], (DEPTH, DIM, 2 * HID), jnp.float32) * 0.02, 'b1': jnp.zeros((DEPTH, 2 * HID), jnp.float32), 'w2': jax.random.normal(ks[4], (DEPTH, HID, DIM), jnp.float32) * 0.02, 'b2': jnp.zeros((DEPTH, DIM), jnp.float32)}
    _L0_ffn_in = _L0_ffn_setup()
    _d = {'L0_attn_a_x': _L0_attn_a_in['x'], 'L0_attn_a_Wq': _L0_attn_a_in['Wq'], 'L0_attn_a_Wk': _L0_attn_a_in['Wk'], 'L0_attn_a_Wv': _L0_attn_a_in['Wv'], 'L0_attn_a_Wo': _L0_attn_a_in['Wo'], 'L0_attn_a_polarity_direction': _L0_attn_a_in['polarity_direction'], 'L0_attn_a_gtp_gamma': _L0_attn_a_in['gtp_gamma'], 'L0_attn_b_wq': _L0_attn_b_in['wq'], 'L0_attn_b_bq': _L0_attn_b_in['bq'], 'L0_attn_b_wk': _L0_attn_b_in['wk'], 'L0_attn_b_bk': _L0_attn_b_in['bk'], 'L0_attn_b_wv': _L0_attn_b_in['wv'], 'L0_attn_b_bv': _L0_attn_b_in['bv'], 'L0_attn_b_wo': _L0_attn_b_in['wo'], 'L0_attn_b_bo': _L0_attn_b_in['bo'], 'L0_attn_b_w1': _L0_attn_b_in['w1'], 'L0_attn_b_b1': _L0_attn_b_in['b1'], 'L0_attn_b_w2': _L0_attn_b_in['w2'], 'L0_attn_b_b2': _L0_attn_b_in['b2'], 'L0_attn_b_hadamard': _L0_attn_b_in['hadamard'], 'L0_attn_b_rot': _L0_attn_b_in['rot'], 'L0_ffn_wqkv': _L0_ffn_in['wqkv'], 'L0_ffn_q_scale': _L0_ffn_in['q_scale'], 'L0_ffn_k_scale': _L0_ffn_in['k_scale'], 'L0_ffn_wo': _L0_ffn_in['wo'], 'L0_ffn_ln_g': _L0_ffn_in['ln_g'], 'L0_ffn_ln_b': _L0_ffn_in['ln_b'], 'L0_ffn_w1': _L0_ffn_in['w1'], 'L0_ffn_b1': _L0_ffn_in['b1'], 'L0_ffn_w2': _L0_ffn_in['w2'], 'L0_ffn_b2': _L0_ffn_in['b2']}
    _x0 = _d['L0_attn_a_x']
    _d['L0_attn_a_x'] = jax.random.normal(jax.random.fold_in(jax.random.key(seed), 1), (16, 256, 128), dtype=_x0.dtype)
    del _x0
    return _d

def reference(L0_attn_a_x, L0_attn_a_Wq, L0_attn_a_Wk, L0_attn_a_Wv, L0_attn_a_Wo, L0_attn_a_polarity_direction, L0_attn_a_gtp_gamma, L0_attn_b_wq, L0_attn_b_bq, L0_attn_b_wk, L0_attn_b_bk, L0_attn_b_wv, L0_attn_b_bv, L0_attn_b_wo, L0_attn_b_bo, L0_attn_b_w1, L0_attn_b_b1, L0_attn_b_w2, L0_attn_b_b2, L0_attn_b_hadamard, L0_attn_b_rot, L0_ffn_wqkv, L0_ffn_q_scale, L0_ffn_k_scale, L0_ffn_wo, L0_ffn_ln_g, L0_ffn_ln_b, L0_ffn_w1, L0_ffn_b1, L0_ffn_w2, L0_ffn_b2):

    def _L0_attn_a_ref(x, Wq, Wk, Wv, Wo, polarity_direction, gtp_gamma):
        import jax, jax.numpy as jnp
        import numpy as np
        import math
        B, T, D_MODEL = (2, 256, 128)
        H_Q, H_KV, D_HEAD = (16, 4, 64)
        N_REP = H_Q // H_KV
        MAX_SEQ_LEN = 256
        ROPE_THETA = 10000.0
        NEG = -1000000000.0

        def _rope(x, position_offset=0):
            Bx, Hx, Tx, Dx = x.shape
            half = Dx // 2
            inv_freq = 1.0 / ROPE_THETA ** (jnp.arange(0, half, dtype=jnp.float32) / half)
            pos = jnp.arange(position_offset, position_offset + Tx, dtype=jnp.float32)
            ang = pos[:, None] * inv_freq[None, :]
            cos, sin = (jnp.cos(ang), jnp.sin(ang))
            x1, x2 = (x[..., :half], x[..., half:])
            return jnp.concatenate([x1 * cos - x2 * sin, x2 * cos + x1 * sin], axis=-1)
        Bx, Tx, _ = x.shape
        scale = math.sqrt(D_HEAD)
        Q = (x @ Wq).reshape(Bx, Tx, H_Q, D_HEAD).transpose(0, 2, 1, 3)
        K = (x @ Wk).reshape(Bx, Tx, H_KV, D_HEAD).transpose(0, 2, 1, 3)
        V = (x @ Wv).reshape(Bx, Tx, H_KV, D_HEAD).transpose(0, 2, 1, 3)
        Q = _rope(Q)
        K = _rope(K)
        K_rep = jnp.repeat(K, N_REP, axis=1)
        V_rep = jnp.repeat(V, N_REP, axis=1)
        scores = jnp.einsum('bhqd,bhkd->bhqk', Q, K_rep) / scale
        q_pos = jnp.arange(Tx, dtype=jnp.float32)
        k_pos = jnp.arange(Tx, dtype=jnp.float32)
        causal = (k_pos[None, :] <= q_pos[:, None]).astype(jnp.float32)
        dist_pol = (k_pos[None, :] - q_pos[:, None]) / float(MAX_SEQ_LEN) * causal
        pol = jnp.clip(polarity_direction, -1.0, 1.0)
        polarity_bias = pol[:, None, None] * dist_pol[None, :, :]
        dist_gtp = jnp.maximum(q_pos[:, None] - k_pos[None, :], 0.0)
        gamma = jnp.clip(gtp_gamma, 0.0001, None)
        gtp = jnp.exp(-gamma[:, None, None] * dist_gtp[None, :, :]) * causal[None, :, :]
        scores = scores + polarity_bias[None] + (1.0 - gtp[None]) * NEG
        attn = jax.nn.softmax(scores, axis=-1)
        out = jnp.einsum('bhqk,bhkd->bhqd', attn, V_rep)
        out = out.transpose(0, 2, 1, 3).reshape(Bx, Tx, H_Q * D_HEAD)
        return out @ Wo

    def _L0_attn_b_ref(x, wq, bq, wk, bk, wv, bv, wo, bo, w1, b1, w2, b2, hadamard, rot):
        import jax, jax.numpy as jnp
        import numpy as np
        B, S, D = (16, 64, 128)
        H, NQ = (16, 8)
        HD = D // H
        Bn, Sn, Dn = x.shape
        Hn = rot.shape[0]
        nq = hadamard.shape[0]
        hd = Dn // Hn
        Q = (x @ wq + bq).reshape(Bn, Sn, Hn, hd)
        K = (x @ wk + bk).reshape(Bn, Sn, Hn, hd)
        V = (x @ wv + bv).reshape(Bn, Sn, Hn, hd)

        def prep(t):
            h1 = jnp.tanh(jnp.einsum('bshd,do->bsho', t, w1) + b1)
            return jnp.einsum('bsho,on->bshn', h1, w2) + b2
        qp, kp = (prep(Q), prep(K))
        qc = (qp[..., :nq] + 1j * qp[..., nq:]).astype(jnp.complex64)
        kc = (kp[..., :nq] + 1j * kp[..., nq:]).astype(jnp.complex64)
        Hc = hadamard.astype(jnp.complex64)
        q1 = jnp.einsum('bshn,nm->bshm', qc, Hc)
        k1 = jnp.einsum('bshn,nm->bshm', kc, Hc)
        cos = jnp.cos(rot[:, :nq // 2, 0] / 2).astype(jnp.complex64)
        sin = jnp.sin(rot[:, :nq // 2, 0] / 2).astype(jnp.complex64)
        R = jnp.zeros((Hn, Bn, Bn), jnp.complex64) + jnp.eye(Bn, dtype=jnp.complex64)
        for i in range(nq // 2):
            a, b = (2 * i, 2 * i + 1)
            R = R.at[:, a, a].set(cos[:, i])
            R = R.at[:, a, b].set(-1j * sin[:, i])
            R = R.at[:, b, a].set(-1j * sin[:, i])
            R = R.at[:, b, b].set(cos[:, i])
        qe = jnp.real(jnp.einsum('hcb,bshn->cshn', R, q1))
        ke = jnp.real(jnp.einsum('hcb,bshn->cshn', R, k1))
        qq = jnp.sum(qe ** 2, -1)
        kk = jnp.sum(ke ** 2, -1)
        s = qq[:, :, None, :] * kk[:, None, :, :]
        attn = jax.nn.softmax(s / s, axis=2)
        out = jnp.einsum('bijh,bjhd->bihd', attn, V).reshape(Bn, Sn, Dn)
        return out @ wo + bo

    def _L0_ffn_ref(x, wqkv, q_scale, k_scale, wo, ln_g, ln_b, w1, b1, w2, b2):
        import jax, jax.numpy as jnp
        import numpy as np
        DIM = 128
        DEPTH = 2
        HEADS = 8
        DIM_HEAD = 64
        WINDOW = 64
        INNER = HEADS * DIM_HEAD
        HID = int(DIM * 4 * 2 / 3)
        B, N = (2, 1024)
        QK_SCALE = 8.0

        def shift_token(t):
            t1, t2 = jnp.split(t, 2, axis=-1)
            t2 = jnp.pad(t2, ((0, 0), (1, 0), (0, 0)))[:, :-1]
            return jnp.concatenate([t1, t2], axis=-1)

        def l2norm(t):
            return t / jnp.clip(jnp.linalg.norm(t, axis=-1, keepdims=True), 1e-12)

        def rotate_half(x):
            x1, x2 = jnp.split(x, 2, axis=-1)
            return jnp.concatenate([-x2, x1], axis=-1)

        def rotary_xpos(q, k):
            n = q.shape[-2]
            half_idx = jnp.arange(0, DIM_HEAD, 2, dtype=jnp.float32)
            inv_freq = 1.0 / 10000.0 ** (half_idx / DIM_HEAD)
            t = jnp.arange(n, dtype=jnp.float32)
            freqs = t[:, None] * inv_freq[None, :]
            freqs = jnp.concatenate([freqs, freqs], axis=-1)
            base = (half_idx + 0.4 * DIM_HEAD) / (1.4 * DIM_HEAD)
            power = (t - n // 2) / float(WINDOW // 2)
            scale = base[None, :] ** power[:, None]
            scale = jnp.concatenate([scale, scale], axis=-1)
            cos, sin = (jnp.cos(freqs), jnp.sin(freqs))
            q = q * cos * scale + rotate_half(q) * sin * scale
            k = k * cos / scale + rotate_half(k) * sin / scale
            return (q, k)

        def local_attention(q, k, v):
            b, h, n, d = q.shape
            w = n // WINDOW
            bq = q.reshape(b, h, w, WINDOW, d) * QK_SCALE
            bk = k.reshape(b, h, w, WINDOW, d)
            bv = v.reshape(b, h, w, WINDOW, d)

            def look_around(t):
                p = jnp.pad(t, ((0, 0), (0, 0), (1, 0), (0, 0), (0, 0)))
                return jnp.concatenate([p[:, :, :w], p[:, :, 1:]], axis=3)
            bk, bv = (look_around(bk), look_around(bv))
            bt = jnp.arange(n).reshape(w, WINDOW)
            btp = jnp.pad(bt, ((1, 0), (0, 0)), constant_values=-1)
            btk = jnp.concatenate([btp[:w], btp[1:]], axis=1)
            sim = jnp.einsum('bhwid,bhwjd->bhwij', bq, bk)
            i = bt[:, :, None]
            j = btk[:, None, :]
            mask = (i < j) | (i > j + WINDOW) | (j == -1)
            sim = jnp.where(mask, -jnp.finfo(sim.dtype).max, sim)
            attn = jax.nn.softmax(sim, axis=-1)
            out = jnp.einsum('bhwij,bhwjd->bhwid', attn, bv)
            return out.reshape(b, h, n, d)

        def _layer(x, wqkv, qs, ksc, wo, lg, lb, w1, b1, w2, b2):
            b, n, _ = x.shape
            h = shift_token(x)
            qkv = h @ wqkv
            q, k, v = jnp.split(qkv, 3, axis=-1)
            to_heads = lambda t: t.reshape(b, n, HEADS, DIM_HEAD).transpose(0, 2, 1, 3)
            q, k, v = (to_heads(q), to_heads(k), to_heads(v))
            q = l2norm(q) * qs
            k = l2norm(k) * ksc
            q, k = rotary_xpos(q, k)
            o = local_attention(q, k, v)
            o = o.transpose(0, 2, 1, 3).reshape(b, n, INNER)
            x = x + o @ wo
            h = shift_token(x)
            mu = h.mean(-1, keepdims=True)
            var = h.var(-1, keepdims=True)
            h = (h - mu) / jnp.sqrt(var + 1e-05) * lg + lb
            h = h @ w1 + b1
            a, g = jnp.split(h, 2, axis=-1)
            h = a * jax.nn.gelu(g, approximate=False)
            x = x + h @ w2 + b2
            return x
        for l in range(DEPTH):
            x = _layer(x, wqkv[l], q_scale[l], k_scale[l], wo[l], ln_g[l], ln_b[l], w1[l], b1[l], w2[l], b2[l])
        return x
    x = L0_attn_a_x
    x = x + _L0_attn_a_ref(_layernorm(x, axis=-1), L0_attn_a_Wq, L0_attn_a_Wk, L0_attn_a_Wv, L0_attn_a_Wo, L0_attn_a_polarity_direction, L0_attn_a_gtp_gamma)
    x = x + _L0_ffn_ref(_layernorm(x, axis=-1), L0_ffn_wqkv, L0_ffn_q_scale, L0_ffn_k_scale, L0_ffn_wo, L0_ffn_ln_g, L0_ffn_ln_b, L0_ffn_w1, L0_ffn_b1, L0_ffn_w2, L0_ffn_b2)
    x = x + _L0_attn_b_ref(_layernorm(x, axis=-1), L0_attn_b_wq, L0_attn_b_bq, L0_attn_b_wk, L0_attn_b_bk, L0_attn_b_wv, L0_attn_b_bv, L0_attn_b_wo, L0_attn_b_bo, L0_attn_b_w1, L0_attn_b_b1, L0_attn_b_w2, L0_attn_b_b2, L0_attn_b_hadamard, L0_attn_b_rot)
    x = x + _L0_ffn_ref(_layernorm(x, axis=-1), L0_ffn_wqkv, L0_ffn_q_scale, L0_ffn_k_scale, L0_ffn_wo, L0_ffn_ln_g, L0_ffn_ln_b, L0_ffn_w1, L0_ffn_b1, L0_ffn_w2, L0_ffn_b2)
    return x

_drawn_inputs = setup_inputs


def setup_inputs(seed=0):
    import zlib

    import numpy as np

    out = dict(_drawn_inputs(seed))
    spreads = {'L0_attn_b_bq': (0.0, 0.1),
     'L0_attn_b_bk': (0.0, 0.1),
     'L0_attn_b_bv': (0.0, 0.368),
     'L0_attn_b_bo': (0.0, 0.334),
     'L0_attn_b_b1': (0.0, 0.1),
     'L0_attn_b_b2': (0.0, 0.1),
     'L0_ffn_q_scale': (1.0, 0.6),
     'L0_ffn_k_scale': (1.0, 0.6),
     'L0_ffn_ln_g': (1.0, 0.6),
     'L0_ffn_ln_b': (0.0, 0.8),
     'L0_ffn_b1': (0.0, 0.8),
     'L0_ffn_b2': (0.0, 0.1)}
    factors = {'L0_ffn_w1': 3.75, 'L0_ffn_w2': 3.693}
    for name, (base, spread) in spreads.items():
        noise = np.random.default_rng([zlib.crc32(name.encode()), seed]).standard_normal(out[name].shape)
        drawn = base * np.exp(spread * noise) if base else spread * noise
        out[name] = jnp.asarray(drawn.astype(out[name].dtype))
    for name, factor in factors.items():
        out[name] = (out[name] * factor).astype(out[name].dtype)
    return out
```

```python
from contextlib import ExitStack

import numpy as np

import concourse.bass as bass
from concourse import mybir

ALU = mybir.AluOpType
ACT = mybir.ActivationFunctionType
AX = mybir.AxisListType
F32 = mybir.dt.float32

P = 128
BATCH, T, D = 16, 256, 128
NB = 2
PAIRS = BATCH // NB
TPB = T // P
NT = NB * TPB
HALF = D // 2
DH = 64
HQ, HKV = 16, 4
QW, KW = HQ * DH, HKV * DH
NEG = -1e9
SLOTS = HQ // 2
STEPS_BEHIND = 5
DEPTH, HL = 2, 8
INNER = HL * DH
WIN = 64
HID = int(D * 4 * 2 / 3)
HIDT = 3
PAIRH = HL // 2
VSETS = 3
MASKED = 1e24
HB, NQ = 16, 8
HD = D // HB
EPS = 1e-5
TWO_PI = 2.0 * np.pi


class Memory:
    pass


def signals(nc, ctx, prefix, names):
    return {name: ctx.enter_context(nc.semaphore(f"{prefix}_{name}")) for name in names.split()}


class Steps:

    def __init__(self, engine, semaphore):
        self.engine, self.semaphore, self.n = engine, semaphore, 0

    def did(self, instruction):
        self.n += 1
        instruction.then_inc(self.semaphore, 1)
        return self.n

    def wait(self, n):
        self.engine.wait_ge(self.semaphore, n)


def clear(nc, s):
    with nc.Block() as block:
        @block.sync
        def _(sp):
            numbers = sorted(x.num for x in s.values())
            start = numbers[0]
            for a, b in zip(numbers, numbers[1:] + [None]):
                if b != a + 1:
                    sp.sem_clear(range(start, a + 1))
                    start = b


def shape_constants():
    c = {}
    c["identity"] = np.eye(P, dtype=np.float32)
    c["shift_down"] = np.eye(P, k=1, dtype=np.float32)
    edge = np.zeros((P, P), np.float32)
    edge[P - 1, 0] = 1
    c["edge"] = edge
    half = DH // 2
    pos = np.arange(T, dtype=np.float32)
    inv = (1.0 / np.float32(10000.0) ** (np.arange(half, dtype=np.float32) / np.float32(half))).astype(np.float32)
    ang = pos[:, None] * inv[None, :]
    cos, sin = np.cos(ang), np.sin(ang)
    rope = np.stack([np.concatenate([cos, cos], 1), np.concatenate([-sin, sin], 1)], 1)
    c["rope_a"] = np.ascontiguousarray(rope.reshape(TPB, P, 2, DH).transpose(1, 0, 2, 3)).astype(np.float32)
    hi = np.arange(0, DH, 2, dtype=np.float32)
    inv = (1.0 / np.float32(10000.0) ** (hi / np.float32(DH))).astype(np.float32)
    ang = pos[:, None] * inv[None, :]
    base = ((hi + 0.4 * DH) / (1.4 * DH)).astype(np.float32)
    power = (pos - T // 2) / np.float32(WIN // 2)
    scale = base[None, :] ** power[:, None]
    scale = np.concatenate([scale, scale], 1)
    cos, sin = np.cos(ang), np.sin(ang)
    cos, sin = np.concatenate([cos, cos], 1), np.concatenate([-sin, sin], 1)
    xpos = np.stack([np.stack([-8.0 * cos * scale, -8.0 * sin * scale], 1),
                     np.stack([cos / scale, sin / scale], 1)], 1)
    c["rope_l"] = np.ascontiguousarray(
        xpos.reshape(TPB, P, 2, 2, DH).transpose(1, 2, 0, 3, 4)).astype(np.float32)
    mask = np.zeros((P, TPB, P), np.float32)
    for tile in range(TPB):
        for p in range(P):
            i = tile * P + p
            for j in range(P):
                key = first_key(tile, p // WIN) + j
                if i < key or i > key + WIN:
                    mask[p, tile, j] = MASKED
    c["mask_l"] = mask
    q = np.arange(T, dtype=np.float32)
    causal = (q[None, :] <= q[:, None]).astype(np.float32)
    for name, table in (("signed_a", (q[None, :] - q[:, None]) / np.float32(T) * causal),
                        ("dist_a", np.maximum(q[:, None] - q[None, :], 0.0)),
                        ("causal_a", causal)):
        c[name] = np.ascontiguousarray(table.reshape(TPB, P, T).transpose(1, 0, 2)).astype(np.float32)
    c["head_of"] = np.repeat(np.eye(HB, dtype=np.float32), HD, 0)
    return c


def first_key(tile, half):
    window = 2 * tile + half
    return max(window - 1, 0) * WIN


def build(nc, a, consts, out):
    with ExitStack() as ctx:
        def sb(name, shape):
            return ctx.enter_context(nc.sbuf_tensor(name, shape, F32))

        w = Memory()
        w.ident = sb("ident", [P, P])
        w.shift_m = sb("shift_m", [P, P])
        w.edge_m = sb("edge_m", [P, P])
        w.rope_a = sb("rope_a", [P, TPB, 2, DH])
        w.rope_l = sb("rope_l", [P, 2, TPB, 2, DH])
        w.mask_l = sb("mask_l", [P, TPB, P])
        w.head_of = sb("head_of", [P, HB])
        w.eps_t = sb("eps_t", [P, 1])
        w.ones_t = sb("ones_t", [P, P])
        w.wqkv_a = sb("wqkv_a", [P, QW + 2 * KW])
        w.wo_a = sb("wo_a", [P, SLOTS, D])
        w.bias_a = sb("bias_a", [P, TPB, HQ, T])
        w.wqkv_l = sb("wqkv_l", [P, DEPTH, 3 * INNER])
        w.wo_l = sb("wo_l", [P, DEPTH, PAIRH, D])
        w.w1_l = sb("w1_l", [P, DEPTH, 2 * HID])
        w.w2_l = sb("w2_l", [P, DEPTH, HIDT, D])
        w.b1_l = sb("b1_l", [P, DEPTH, 2 * HID])
        w.b2_l = sb("b2_l", [P, DEPTH, D])
        w.ln_gb = sb("ln_gb", [P, 2, DEPTH])
        w.rot_l = sb("rot_l", [P, DEPTH, 2, TPB, 2, DH])
        w.wqkv_b = sb("wqkv_b", [P, 3, D])
        w.wo_b = sb("wo_b", [P, D])
        w.bqkv_b = sb("bqkv_b", [P, 3])
        w.w1_b = sb("w1_b", [P, HB, D])
        w.b1_b = sb("b1_b", [P, 1])
        w.w2_b = sb("w2_b", [P, 2 * NQ])
        w.b2_b = sb("b2_b", [P, 2 * NQ])
        w.bo_b = sb("bo_b", [P, D])
        w.mix_b = sb("mix_b", [P, PAIRS, 2, HB])
        w.x = sb("x", [P, NT, D])
        w.y = sb("y", [P, NT, D])
        w.stats = sb("stats", [P, NT, 2, 6])
        w.mean_var = sb("mean_var", [P, NT, 2])
        w.std = sb("std", [P, NT])
        w.rstd = sb("rstd", [P, NT])

        setup(nc, a, consts, w)
        with nc.Fori(0, PAIRS) as pair:
            attention_a(nc, a, w, pair)
            with nc.Fori(0, DEPTH) as layer:
                local_layer(nc, w, layer, "l")
            attention_b(nc, w, pair)
            with nc.Fori(0, DEPTH) as layer:
                local_layer(nc, w, layer, "m")
            store(nc, w, pair, out)


def setup(nc, a, consts, w):
    with ExitStack() as ctx:
        def sb(name, shape):
            return ctx.enter_context(nc.sbuf_tensor("setup_" + name, shape, F32))

        s = signals(nc, ctx, "setup", "zeroed small loaded exp_a dve done pe act pool placed trig")
        signed, dist, causal = (sb(n, [P, TPB, T]) for n in ("signed", "dist", "causal"))
        pol, gam = sb("pol", [P, HQ]), sb("gam", [P, HQ])
        e = sb("e", [P, 2, TPB, T])
        u = sb("u", [P, 2, TPB, T])
        v = sb("v", [P, 2, TPB, T])
        qs = sb("qs", [P, DEPTH, 2, DH])
        rot = sb("rot", [P, NQ // 2, HB])
        ang, turns, angr = sb("ang", [P, NQ // 2, 2, HB]), sb("turns", [P, NQ // 2, 2, HB]), sb("angr", [P, NQ // 2, 2, HB])
        had = sb("had", [2 * NQ, 2 * NQ])
        w2T, b2col, b2rep = sb("w2T", [2 * NQ, P]), sb("b2col", [2 * NQ, 1]), sb("b2rep", [2 * NQ, P])
        ps = ctx.enter_context(nc.psum_tensor("setup_ps", [P, 512], F32))

        plain = [
            (w.ident[:], consts["identity"]), (w.shift_m[:], consts["shift_down"]), (w.edge_m[:], consts["edge"]),
            (w.rope_a[:], consts["rope_a"]), (w.mask_l[:], consts["mask_l"]), (w.head_of[:], consts["head_of"]),
            (w.wqkv_a[:, 0:QW], a["L0_attn_a_Wq"]), (w.wqkv_a[:, QW:QW + KW], a["L0_attn_a_Wk"]),
            (w.wqkv_a[:, QW + KW:], a["L0_attn_a_Wv"]),
            (w.wo_a[:], a["L0_attn_a_Wo"].rearrange("(k p) n -> p k n", p=P)),
            (w.wqkv_l[:], a["L0_ffn_wqkv"].rearrange("l p n -> p l n")),
            (w.wo_l[:], a["L0_ffn_wo"].rearrange("l (k p) n -> p l k n", p=P)),
            (w.w1_l[:], a["L0_ffn_w1"].rearrange("l p n -> p l n")),
            (w.ln_gb[:, 0, :], a["ln_g_by_feature"]),
            (w.ln_gb[:, 1, :], a["ln_b_by_feature"]),
            (w.b1_l[:], a["L0_ffn_b1"].rearrange("(o l) n -> o l n", o=1).broadcast_to((P, DEPTH, 2 * HID))),
            (w.b2_l[:], a["L0_ffn_b2"].rearrange("(o l) n -> o l n", o=1).broadcast_to((P, DEPTH, D))),
            (w.wqkv_b[:, 0, :], a["L0_attn_b_wq"]), (w.wqkv_b[:, 1, :], a["L0_attn_b_wk"]),
            (w.wqkv_b[:, 2, :], a["L0_attn_b_wv"]), (w.wo_b[:], a["L0_attn_b_wo"]),
            (w.bqkv_b[:, 0:1], a["L0_attn_b_bq"].rearrange("(p o) -> p o", o=1)),
            (w.bqkv_b[:, 1:2], a["L0_attn_b_bk"].rearrange("(p o) -> p o", o=1)),
            (w.bqkv_b[:, 2:3], a["L0_attn_b_bv"].rearrange("(p o) -> p o", o=1)),
            (w.b1_b[:], a["L0_attn_b_b1"].rearrange("(p o) -> p o", o=1)),
            (w.bo_b[:], a["L0_attn_b_bo"].rearrange("(o n) -> o n", o=1).broadcast_to((P, D))),
        ]
        small = [
            (signed[:], consts["signed_a"]), (dist[:], consts["dist_a"]), (causal[:], consts["causal_a"]),
            (pol[:], a["L0_attn_a_polarity_direction"].rearrange("(o h) -> o h", o=1).broadcast_to((P, HQ))),
            (gam[:], a["L0_attn_a_gtp_gamma"].rearrange("(o h) -> o h", o=1).broadcast_to((P, HQ))),
            (w.rope_l[:], consts["rope_l"]),
            (qs[:, :, 0, :], a["L0_ffn_q_scale"].rearrange("(o l) n -> o l n", o=1).broadcast_to((P, DEPTH, DH))),
            (qs[:, :, 1, :], a["L0_ffn_k_scale"].rearrange("(o l) n -> o l n", o=1).broadcast_to((P, DEPTH, DH))),
            (rot[:], a["angles_by_pair"].rearrange("(o n) h -> o n h", o=1).broadcast_to((P, NQ // 2, HB))),
            (w2T[:], a["w2_transposed"]),
            (b2col[:], a["L0_attn_b_b2"].rearrange("(p o) -> p o", o=1)),
        ]
        placed = [(w.w1_b[HD * h:HD * (h + 1), h, :], a["L0_attn_b_w1"]) for h in range(HB)]
        placed += [(had[NQ * i:NQ * (i + 1), NQ * i:NQ * (i + 1)], a["L0_attn_b_hadamard"]) for i in range(2)]
        last = HID - (HIDT - 1) * P
        placed += [(w.w2_l[0:P, l, 0:HIDT - 1, :],
                    a["L0_ffn_w2"][l, 0:(HIDT - 1) * P, :].rearrange("(k p) n -> p k n", p=P)) for l in range(DEPTH)]
        placed += [(w.w2_l[0:last, l, HIDT - 1, :], a["L0_ffn_w2"][l, (HIDT - 1) * P:HID, :]) for l in range(DEPTH)]

        with nc.Block() as block:
            @block.sync
            def _(sp):
                for dst, src in small:
                    sp.dma_start(dst, src).then_inc(s["small"], 16)
                sp.wait_ge(s["zeroed"], 3)
                for dst, src in placed:
                    sp.dma_start(dst, src).then_inc(s["placed"], 16)
                sp.wait_ge(s["placed"], 16 * len(placed))

            @block.gpsimd
            def _(pool):
                nc.gpsimd.memset(w.w1_b[:], 0.0).then_inc(s["zeroed"], 1)
                nc.gpsimd.memset(had[:], 0.0).then_inc(s["zeroed"], 1)
                nc.gpsimd.memset(w.w2_l[:], 0.0).then_inc(s["zeroed"], 1)
                nc.gpsimd.memset(w.eps_t[:], EPS).then_inc(s["pool"], 1)
                nc.gpsimd.memset(w.ones_t[:], 1.0).then_inc(s["pool"], 1)
                nc.gpsimd.memset(w.mix_b[:, NQ // 2:, 0, :], 1.0).then_inc(s["pool"], 1)
                nc.gpsimd.memset(w.mix_b[:, NQ // 2:, 1, :], 0.0).then_inc(s["pool"], 1)

            @block.scalar
            def _(act):
                for dst, src in plain:
                    act.dma_start(dst, src).then_inc(s["loaded"], 16)
                for h in range(HQ):
                    act.wait_ge(s["done"], 1 + max(h - 1, 0))
                    nc.scalar.activation(e[:, h % 2], dist[:], ACT.Exp,
                                         scale=gam[:, h:h + 1]).then_inc(s["exp_a"], 1)
                act.wait_ge(s["trig"], 1)
                nc.scalar.activation(w.mix_b[:, 0:NQ // 2, :, :], angr[:], ACT.Sin).then_inc(s["act"], 1)
                act.wait_ge(s["loaded"], 16 * len(plain))

            @block.vector
            def _(dve):
                st = Steps(dve, s["dve"])
                dve.wait_ge(s["small"], 16 * len(small))
                n = st.did(nc.vector.tensor_scalar(pol[:], pol[:], -1.0, 1.0, ALU.max, ALU.min))
                m = st.did(nc.vector.tensor_scalar(gam[:], gam[:], 1e-4, None, ALU.max))
                st.wait(m)
                nc.vector.tensor_scalar(gam[:], gam[:], -1.0, None, ALU.mult).then_inc(s["done"], 1)
                st.did(nc.vector.tensor_scalar(ang[:, :, 0, :], rot[:], 0.5, float(np.pi / 2), ALU.mult, ALU.add))
                k = st.did(nc.vector.tensor_scalar(ang[:, :, 1, :], rot[:], 0.5, None, ALU.mult))
                st.wait(k)
                big = float(1.5 * 2 ** 23)
                k = st.did(nc.vector.tensor_scalar(turns[:], ang[:], 1.0 / TWO_PI, big, ALU.mult, ALU.add))
                st.wait(k)
                k = st.did(nc.vector.tensor_scalar(turns[:], turns[:], big, -TWO_PI, ALU.subtract, ALU.mult))
                st.wait(k)
                k = st.did(nc.vector.tensor_tensor(angr[:], ang[:], turns[:], ALU.add))
                st.wait(k)
                k = st.did(nc.vector.tensor_scalar(angr[:], angr[:], float(np.pi), float(-np.pi), ALU.min, ALU.max))
                st.wait(k)
                nc.vector.tensor_copy(ang[:], angr[:]).then_inc(s["trig"], 1)
                for l in range(DEPTH):
                    for i in range(2):
                        for t in range(TPB):
                            st.did(nc.vector.tensor_tensor(w.rot_l[:, l, i, t, 0, :], w.rope_l[:, i, t, 0, :],
                                                           qs[:, l, i, :], ALU.mult))
                            for hf in range(2):
                                lo, ot = hf * DH // 2, (1 - hf) * DH // 2
                                st.did(nc.vector.tensor_tensor(
                                    w.rot_l[:, l, i, t, 1, lo:lo + DH // 2], w.rope_l[:, i, t, 1, lo:lo + DH // 2],
                                    qs[:, l, i, ot:ot + DH // 2], ALU.mult))
                st.did(nc.vector.tensor_scalar(b2rep[:], w2T[:], 0.0, b2col[:, 0:1], ALU.mult, ALU.add))
                k = st.n
                dve.wait_ge(s["done"], 1)
                for h in range(HQ):
                    dve.wait_ge(s["exp_a"], h + 1)
                    i = h % 2
                    k1 = st.did(nc.vector.tensor_tensor(u[:, i], e[:, i], causal[:], ALU.mult))
                    k2 = st.did(nc.vector.tensor_scalar(v[:, i], signed[:], pol[:, h:h + 1], 8.0, ALU.mult, ALU.mult))
                    st.wait(k1)
                    k3 = st.did(nc.vector.tensor_scalar(u[:, i], u[:, i], -1.0, 1.0, ALU.mult, ALU.add))
                    st.wait(k3)
                    nc.vector.scalar_tensor_tensor(out=w.bias_a[:, :, h, :], in0=u[:, i], scalar=8.0 * NEG, in1=v[:, i],
                                                   op0=ALU.mult, op1=ALU.add).then_inc(s["done"], 1)
                    dve.wait_ge(s["done"], h + 2)
                dve.wait_ge(s["pe"], 1)
                nc.vector.tensor_copy(w.w2_b[:], ps[:, 0:2 * NQ]).then_inc(s["dve"], 1)
                nc.vector.tensor_copy(w.b2_b[:], ps[:, 2 * NQ:4 * NQ]).then_inc(s["dve"], 1)

            @block.tensor
            def _(pe):
                pe.wait_ge(s["placed"], 16 * len(placed))
                pe.wait_ge(s["small"], 16 * len(small))
                pe.wait_ge(s["done"], 2)
                pe.matmul(ps[:, 0:2 * NQ], w2T[:], had[:], start=True, stop=True)
                pe.matmul(ps[:, 2 * NQ:4 * NQ], b2rep[:], had[:], start=True, stop=True).then_inc(s["pe"], 1)
        clear(nc, s)


def layer_norm_stats(nc, dve, st, w, tiles, src, s, done):
    for t in tiles:
        k = st.did(nc.vector.bn_stats(w.stats[:, t, 0, :], src[:, t, :]))
    st.wait(k)
    for t in tiles:
        nc.vector.bn_aggr(w.mean_var[:, t, :], w.stats[:, t, 0, :]).then_inc(done, 1)


def attention_a(nc, a, w, pair):
    with ExitStack() as ctx:
        def sb(name, shape):
            return ctx.enter_context(nc.sbuf_tensor("a_" + name, shape, F32))

        s = signals(nc, ctx, "a", "x_loaded dve act var_ready std_ready normed xT_ps xT proj v_sb rot_dve rot_pool "
                                  "qkT_ps qkT scored shifted_scores probs pT_ps pT_d pT_a pv o_sb oT_ps oT wo x_new "
                                  "var2 std2")
        xn = sb("xn", [P, NT, D])
        xT = sb("xT", [P, NT, P])
        r1, r2 = sb("r1", [P, 2, QW + KW]), sb("r2", [P, 2, QW + KW])
        qk = sb("qk", [P, 2, QW + KW])
        qT = sb("qT", [P, NT, SLOTS, P])
        kT = sb("kT", [P, NB, HKV // 2, T])
        v = sb("v", [P, NT, HKV, DH + 1])
        sc = sb("sc", [P, 2, 2, T])
        neg_max = sb("neg_max", [P, NT * SLOTS, 2])
        pr = sb("pr", [P, 2, 2, T])
        pT = sb("pT", [P, 2, 2, TPB, P])
        rsum = sb("rsum", [P, NT * SLOTS // 2, 4])
        o = sb("o", [P, NT, HQ, DH])
        oT = sb("oT", [P, SLOTS, P])
        bank = [ctx.enter_context(nc.psum_tensor(f"a_bank{i}", [P, 512], F32)) for i in range(8)]
        NU = NT * SLOTS
        slot_head = lambda j, e: 8 * (j // 4) + 4 * e + j % 4

        with nc.Block() as block:
            @block.sync
            def _(sp):
                src = a["L0_attn_a_x"].rearrange("(g b) (c p) d -> p g (b c) d", b=NB, p=P)
                sp.dma_start(w.x[:], src[:, bass.ds(pair, 1), :, :]).then_inc(s["x_loaded"], 16)

            @block.tensor
            def _(pe):
                pe.wait_ge(s["normed"], NT)
                for t in range(NT):
                    pe.transpose(bank[6][:, t * P:(t + 1) * P], xn[:, t, :], w.ident[:]).then_inc(s["xT_ps"], 1)

                def project(t):
                    if t >= 2:
                        pe.wait_ge(s["rot_dve"], t - 1)
                        pe.wait_ge(s["v_sb"], t - 1)
                    for c in range(3):
                        pe.matmul(bank[3 * (t % 2) + c][:], xT[:, t, :], w.wqkv_a[:, 512 * c:512 * (c + 1)],
                                  start=True, stop=True).then_inc(s["proj"], 1)

                def turn(t):
                    for c in range(3):
                        r = 3 * t + c
                        if r >= 2:
                            pe.wait_ge(s["qkT"], r - 1)
                        if c == 0:
                            pe.wait_ge(s["rot_pool"], 3 * (t + 1))
                        if c < 2:
                            for i in range(4):
                                j = 4 * c + i
                                ins = pe.transpose(bank[6 + r % 2][:, i * P:(i + 1) * P],
                                                   qk[:, t % 2, j * P:(j + 1) * P], w.ident[:])
                        else:
                            for g in range(2):
                                ins = pe.transpose(bank[6 + r % 2][:, g * P:(g + 1) * P],
                                                   qk[:, t % 2, QW + g * P:QW + (g + 1) * P], w.ident[:])
                        ins.then_inc(s["qkT_ps"], 1)

                def scores(u):
                    t, j = divmod(u, SLOTS)
                    b = t // TPB
                    if u == 0:
                        pe.wait_ge(s["rot_dve"], NT)
                        pe.wait_ge(s["v_sb"], NT)
                        pe.wait_ge(s["qkT"], 3 * NT)
                    for e in range(2):
                        r = 2 * u + e
                        if r >= 3:
                            pe.wait_ge(s["shifted_scores"], r - 2)
                        rows = slice(64 * e, 64 * e + 64)
                        pe.matmul(bank[r % 3][:, 0:T], qT[rows, t, j, :], kT[rows, b, j // 4, :],
                                  start=True, stop=True).then_inc(s["scored"], 1)

                def turn_probs(u):
                    pe.wait_ge(s["probs"], 2 * (u + 1))
                    if u >= 2:
                        pe.wait_ge(s["pT_d"] if u % 2 == 0 else s["pT_a"], u // 2)
                    for e in range(2):
                        for k in range(TPB):
                            ins = pe.transpose(bank[3 + u % 2][:, (2 * e + k) * P:(2 * e + k + 1) * P],
                                               pr[:, u % 2, e, k * P:(k + 1) * P], w.ident[:])
                    ins.then_inc(s["pT_ps"], 1)

                def weigh_values(u):
                    t, j = divmod(u, SLOTS)
                    b = t // TPB
                    pe.wait_ge(s["pT_d"] if u % 2 == 0 else s["pT_a"], u // 2 + 1)
                    g = u // 2
                    if u % 2 == 0 and g >= 2:
                        pe.wait_ge(s["o_sb"], g - 1)
                    for e in range(2):
                        c = (2 * (u % 2) + e) * (DH + 1)
                        for k in range(TPB):
                            ins = pe.matmul(bank[5 + g % 2][:, c:c + DH + 1], pT[:, u % 2, e, k, :],
                                            v[:, b * TPB + k, 2 * (j // 4) + e, :], start=(k == 0), stop=(k == 1))
                    ins.then_inc(s["pv"], 1)

                def turn_out(t, c):
                    if c == 0:
                        pe.wait_ge(s["o_sb"], 4 * (t + 1))
                    else:
                        pe.wait_ge(s["oT"], 2 * t + 1)
                    if t >= 1:
                        pe.wait_ge(s["x_new"], t)
                    for i in range(4):
                        kt = 4 * c + i
                        ins = pe.transpose(bank[7][:, i * P:(i + 1) * P],
                                           o[:, t, 2 * kt:2 * kt + 2, :].rearrange("p h d -> p (h d)"), w.ident[:])
                    ins.then_inc(s["oT_ps"], 1)

                def project_out(t):
                    pe.wait_ge(s["oT"], 2 * (t + 1))
                    for kt in range(SLOTS):
                        ins = pe.matmul(bank[7][:, 0:D], oT[:, kt, :], w.wo_a[:, kt, :],
                                        start=(kt == 0), stop=(kt == SLOTS - 1))
                    ins.then_inc(s["wo"], 1)

                pe.wait_ge(s["xT"], 1)
                project(0)
                project(1)
                for t in range(NT):
                    turn(t)
                    if t + 2 < NT:
                        project(t + 2)
                for i in range(NU + STEPS_BEHIND):
                    if i < NU:
                        scores(i)
                    if 1 <= i <= NU:
                        turn_probs(i - 1)
                    if 2 <= i <= NU + 1:
                        weigh_values(i - 2)
                    for c in range(2):
                        if i >= 10 + c and (i - 10 - c) % SLOTS == 0:
                            turn_out((i - 10 - c) // SLOTS, c)
                    if i >= 12 and (i - 12) % SLOTS == 0:
                        project_out((i - 12) // SLOTS)

            @block.scalar
            def _(act):
                act.wait_ge(s["var_ready"], NT)
                nc.scalar.activation(w.std[:], w.mean_var[:, :, 1], ACT.Sqrt, bias=w.eps_t[:, 0:1]).then_inc(s["std_ready"], 1)
                act.wait_ge(s["xT_ps"], NT)
                nc.scalar.copy(xT[:].rearrange("p t k -> p (t k)"), bank[6][:]).then_inc(s["xT"], 1)

                def values(t):
                    act.wait_ge(s["proj"], 3 * t + 3)
                    act.wait_ge(s["rot_dve"], t + 1)
                    nc.scalar.copy(v[:, t, :, 0:DH],
                                   bank[3 * (t % 2) + 2][:, KW:2 * KW].rearrange("p (h d) -> p h d", h=HKV)
                                   ).then_inc(s["v_sb"], 1)

                def turned(t):
                    for c in range(3):
                        r = 3 * t + c
                        act.wait_ge(s["qkT_ps"], r + 1)
                        if c < 2:
                            nc.scalar.copy(qT[:, t, 4 * c:4 * c + 4, :].rearrange("p j k -> p (j k)"),
                                           bank[6 + r % 2][:]).then_inc(s["qkT"], 1)
                        else:
                            nc.scalar.copy(kT[:, t // TPB, :, (t % TPB) * P:(t % TPB + 1) * P],
                                           bank[6 + r % 2][:, 0:2 * P].rearrange("p (g k) -> p g k", g=2)
                                           ).then_inc(s["qkT"], 1)

                values(0)
                values(1)
                for t in range(NT):
                    turned(t)
                    if t + 2 < NT:
                        values(t + 2)

                def exps(u):
                    if u >= 2:
                        act.wait_ge(s["pT_ps"], u - 1)
                    for e in range(2):
                        act.wait_ge(s["shifted_scores"], 2 * u + e + 1)
                        nc.scalar.activation(pr[:, u % 2, e, :], sc[:, u % 2, e, :], ACT.Exp,
                                             bias=neg_max[:, u, e:e + 1], scale=-1.0).then_inc(s["probs"], 1)

                def turned_probs(u):
                    act.wait_ge(s["pT_ps"], u + 1)
                    if u >= 2:
                        act.wait_ge(s["pv"], u - 1)
                    nc.scalar.copy(pT[:, u % 2].rearrange("p e k q -> p (e k q)"), bank[3 + u % 2][:]).then_inc(s["pT_a"], 1)

                def turned_out(t, c):
                    act.wait_ge(s["oT_ps"], 2 * t + c + 1)
                    if c == 0 and t >= 1:
                        act.wait_ge(s["wo"], t)
                    nc.scalar.copy(oT[:, 4 * c:4 * c + 4, :].rearrange("p j k -> p (j k)"), bank[7][:]).then_inc(s["oT"], 1)

                for i in range(NU + STEPS_BEHIND):
                    if i < NU:
                        exps(i)
                    if 1 <= i <= NU and (i - 1) % 2 == 1:
                        turned_probs(i - 1)
                    for c in range(2):
                        if i >= 10 + c and (i - 10 - c) % SLOTS == 0:
                            turned_out((i - 10 - c) // SLOTS, c)
                act.wait_ge(s["var2"], NT)
                nc.scalar.activation(w.std[:], w.mean_var[:, :, 1], ACT.Sqrt, bias=w.eps_t[:, 0:1]).then_inc(s["std2"], 1)

            @block.vector
            def _(dve):
                st = Steps(dve, s["dve"])
                dve.wait_ge(s["x_loaded"], 16)
                layer_norm_stats(nc, dve, st, w, range(NT), w.x, s, s["var_ready"])
                dve.wait_ge(s["std_ready"], 1)
                k = st.did(nc.vector.reciprocal(w.rstd[:], w.std[:]))
                st.wait(k)
                for t in range(NT):
                    nc.vector.tensor_scalar(xn[:, t, :], w.x[:, t, :], w.mean_var[:, t, 0:1], w.rstd[:, t:t + 1],
                                            ALU.subtract, ALU.mult).then_inc(s["normed"], 1)

                def rotate(t):
                    if t >= 2:
                        dve.wait_ge(s["rot_pool"], 3 * (t - 1))
                    for c, heads in ((0, 8), (1, 8), (2, 4)):
                        n = heads * DH
                        dve.wait_ge(s["proj"], 3 * t + c + 1)
                        src = bank[3 * (t % 2) + c][:, 0:n].rearrange("p (h d) -> p h d", h=heads)
                        swapped = bank[3 * (t % 2) + c][:, 0:n].rearrange("p (h s d) -> p h s d", h=heads, s=2)[:, :, ::-1, :]
                        cos = w.rope_a[:, t % TPB, 0, :].unsqueeze(1).broadcast_to((P, heads, DH))
                        sin = w.rope_a[:, t % TPB, 1, :].rearrange("p (s d) -> p s d", s=2).unsqueeze(1)\
                            .broadcast_to((P, heads, 2, DH // 2))
                        st.did(nc.vector.tensor_tensor(
                            r1[:, t % 2, 512 * c:512 * c + n].rearrange("p (h d) -> p h d", h=heads), src, cos, ALU.mult))
                        ins = nc.vector.tensor_tensor(
                            r2[:, t % 2, 512 * c:512 * c + n].rearrange("p (h s d) -> p h s d", h=heads, s=2),
                            swapped, sin, ALU.mult)
                        if c < 2:
                            st.did(ins)
                    ins.then_inc(s["rot_dve"], 1)

                for t in range(NT):
                    rotate(t)

                def shift_scores(u):
                    t, j = divmod(u, SLOTS)
                    if u >= 2:
                        dve.wait_ge(s["probs"], 2 * (u - 1))
                    for e in range(2):
                        dve.wait_ge(s["scored"], 2 * u + e + 1)
                        nc.vector.tensor_tensor_reduce(
                            out=sc[:, u % 2, e, :], in0=bank[(2 * u + e) % 3][:, 0:T],
                            in1=w.bias_a[:, t % TPB, slot_head(j, e), :], scale=-1.0 / 8.0, scalar=3e38,
                            op0=ALU.add, op1=ALU.min, accum_out=neg_max[:, u, e:e + 1]).then_inc(s["shifted_scores"], 1)

                def turned_probs(u):
                    dve.wait_ge(s["pT_ps"], u + 1)
                    if u >= 2:
                        dve.wait_ge(s["pv"], u - 1)
                    nc.vector.tensor_copy(pT[:, u % 2].rearrange("p e k q -> p (e k q)"), bank[3 + u % 2][:]).then_inc(s["pT_d"], 1)

                def normalise(g):
                    t, gg = divmod(g, SLOTS // 2)
                    dve.wait_ge(s["pv"], 2 * g + 2)
                    src = bank[5 + g % 2][:, 0:4 * (DH + 1)].rearrange("p (r e c) -> p r e c", r=2, e=2)
                    k = st.did(nc.vector.reciprocal(rsum[:, g, :].rearrange("p (r e) -> p r e", r=2), src[:, :, :, DH]))
                    st.wait(k)
                    dst = o[:, t].rearrange("p (g e r) d -> p g r e d", g=2, e=2)[:, gg // 2, 2 * (gg % 2):2 * (gg % 2) + 2]
                    nc.vector.tensor_tensor(
                        dst, src[:, :, :, 0:DH],
                        rsum[:, g, :].rearrange("p (r e) -> p r e", r=2).unsqueeze(3).broadcast_to((P, 2, 2, DH)),
                        ALU.mult).then_inc(s["o_sb"], 1)

                def residual(t):
                    dve.wait_ge(s["wo"], t + 1)
                    nc.vector.tensor_tensor(w.x[:, t, :], w.x[:, t, :], bank[7][:, 0:D], ALU.add).then_inc(s["x_new"], 1)

                for i in range(NU + STEPS_BEHIND):
                    if i < NU:
                        shift_scores(i)
                    if 1 <= i <= NU and (i - 1) % 2 == 0:
                        turned_probs(i - 1)
                    if 3 <= i <= NU + 1 and i % 2 == 1:
                        normalise((i - 3) // 2)
                    if i >= 12 and (i - 12) % SLOTS == 0:
                        residual((i - 12) // SLOTS)
                dve.wait_ge(s["x_new"], NT)
                layer_norm_stats(nc, dve, st, w, range(NT), w.x, s, s["var2"])
                dve.wait_ge(s["std2"], 1)
                k = st.did(nc.vector.reciprocal(w.rstd[:], w.std[:]))
                st.wait(k)
                for t in range(NT):
                    st.did(nc.vector.tensor_scalar(w.y[:, t, :], w.x[:, t, :], w.mean_var[:, t, 0:1], w.rstd[:, t:t + 1],
                                                   ALU.subtract, ALU.mult))

            @block.gpsimd
            def _(pool):
                nc.gpsimd.memset(v[:, :, :, DH:DH + 1], 1.0).then_inc(s["act"], 1)
                for t in range(NT):
                    pool.wait_ge(s["rot_dve"], t + 1)
                    if t >= 2:
                        pool.wait_ge(s["qkT_ps"], 3 * (t - 1))
                    for c in range(3):
                        lo, hi = 512 * c, min(512 * (c + 1), QW + KW)
                        dst, one, two = qk[:, t % 2, lo:hi], r1[:, t % 2, lo:hi], r2[:, t % 2, lo:hi]
                        if c < 2:
                            dst = dst.rearrange("p (r e d) -> p r e d", r=4, e=2)
                            one, two = (z.rearrange("p (e r d) -> p r e d", r=4, e=2) for z in (one, two))
                        nc.gpsimd.tensor_tensor(dst, one, two, ALU.add).then_inc(s["rot_pool"], 1)
        clear(nc, s)


def local_layer(nc, w, layer, name):
    with ExitStack() as ctx:
        def sb(n, shape):
            return ctx.enter_context(nc.sbuf_tensor(f"{name}_{n}", shape, F32))

        s = signals(nc, ctx, name, "dve pool yT_ps hT_a hT_d edge_zero qk_proj v_proj squared summed norm rn rot_dve "
                                   "rot_pool qT_ps kT_ps qT kT v_sb ones scored shifted_scores probs pT_ps pT pv o_sb "
                                   "oT_ps oT wo y_attn shifted var_ready std_ready normed nT_ps hnT w1 gated_in "
                                   "gelu gated gT_ps gT w2 y_new y_bias pad")
        hT = sb("hT", [P, NB, T])
        sq = sb("sq", [P, 2, 2, INNER])
        ss, norm, rn = sb("ss", [P, NT, 2, HL]), sb("norm", [P, NT, 2, HL]), sb("rn", [P, NT, 2, HL])
        r1, r2 = sb("r1", [P, 2, 2, INNER]), sb("r2", [P, 2, 2, INNER])
        qk = sb("qk", [P, 2, 2, INNER])
        kr = sb("kr", [P, 2, INNER])
        qT = sb("qT", [P, NT, PAIRH, P])
        kT = sb("kT", [P, NB, PAIRH, T])
        v = sb("v", [P, NB, VSETS, HL, DH + 1])
        NU = NT * 2
        sc, pr, pT = sb("sc", [P, 2, 4, P]), sb("pr", [P, 2, 4, P]), sb("pT", [P, 2, 4, P])
        neg_max, rsum = sb("neg_max", [P, NU, 4]), sb("rsum", [P, NU, 4])
        o = sb("o", [P, NT, INNER])
        oT = sb("oT", [P, 2, PAIRH, P])
        old1, old2 = (z[:].rearrange("p a b c -> p (a b c)") for z in (r1, r2))
        gin, ain, gel = (old1[:, 2 * HID * i:2 * HID * (i + 1)].rearrange("p (a b) -> p a b", a=2) for i in range(3))
        n = old2[:, 0:NT * D].rearrange("p (t d) -> p t d", t=NT)
        hnT = old2[:, NT * D:2 * NT * D].rearrange("p (t d) -> p t d", t=NT)
        gT = old2[:, 2 * NT * D:2 * NT * D + 2 * HIDT * P].rearrange("p (a k q) -> p a k q", a=2, k=HIDT)
        gated = sb("gated", [P, 2, HIDT * P])
        yb = sb("yb", [P, NT, D])
        lgb = sb("lgb", [P, 2, 1])
        lg, lb = lgb[:, 0, :], lgb[:, 1, :]
        tab = sb("tab", [P, 2, TPB, 2, DH])
        b1 = sb("b1", [P, 2 * HID])
        bank = [ctx.enter_context(nc.psum_tensor(f"{name}_bank{i}", [P, 512], F32)) for i in range(8)]

        with nc.Block() as block:
            @block.tensor
            def _(pe):
                for b in range(NB):
                    for i in range(TPB):
                        ins = pe.transpose(bank[6 + b][:, i * P:(i + 1) * P], w.y[:, b * TPB + i, :], w.ident[:])
                    ins.then_inc(s["yT_ps"], 1)

                def project(t):
                    b, i = divmod(t, TPB)
                    if i == 0:
                        pe.wait_ge(s["hT_a"], b + 1)
                        pe.wait_ge(s["hT_d"], b + 1)
                        pe.wait_ge(s["edge_zero"], 1)
                    if t >= 2:
                        pe.wait_ge(s["rot_dve"], 2 * (t - 1))
                        pe.wait_ge(s["squared"], 2 * (t - 1))
                    for c in range(2):
                        pe.matmul(bank[2 * (t % 2) + c][:], hT[:, b, i * P:(i + 1) * P],
                                  w.wqkv_l[:, bass.ds(layer, 1), INNER * c:INNER * (c + 1)],
                                  start=True, stop=True).then_inc(s["qk_proj"], 1)

                def project_values(r):
                    b, i = divmod(r, VSETS)
                    if r >= 2:
                        pe.wait_ge(s["v_sb"], r - 1)
                    pe.matmul(bank[4 + r % 2][:], hT[:, b, i * WIN:i * WIN + P],
                              w.wqkv_l[:, bass.ds(layer, 1), 2 * INNER:3 * INNER],
                              start=True, stop=True).then_inc(s["v_proj"], 1)

                def turn(t):
                    if t == 0:
                        pe.wait_ge(s["hT_a"], NB)
                        pe.wait_ge(s["hT_d"], NB)
                    for c, ready, copied, ps in ((0, s["rot_pool"], s["qT"], s["qT_ps"]), (1, s["rot_pool"], s["kT"], s["kT_ps"])):
                        pe.wait_ge(ready, 2 * t + c + 1)
                        if t >= 1:
                            pe.wait_ge(copied, t)
                        for i in range(PAIRH):
                            ins = pe.transpose(bank[6 + c][:, i * P:(i + 1) * P],
                                               qk[:, t % 2, c, i * P:(i + 1) * P], w.ident[:])
                        ins.then_inc(ps, 1)

                def scores(u):
                    t, e = divmod(u, 2)
                    b, i = divmod(t, TPB)
                    if u == 0:
                        pe.wait_ge(s["rot_dve"], 2 * (NT - 1))
                        pe.wait_ge(s["squared"], 2 * (NT - 1))
                    if u >= 2:
                        pe.wait_ge(s["shifted_scores"], 4 * (u - 1))
                    pe.wait_ge(s["qT"], t + 1)
                    pe.wait_ge(s["kT"], t + 1)
                    for c in range(4):
                        h = 2 * c + e
                        rows = slice(64 * e, 64 * e + 64)
                        for half in range(2):
                            k0 = first_key(i, half)
                            ins = pe.matmul(bank[u % 2][64 * half:64 * half + 64, c * P:(c + 1) * P],
                                            qT[rows, t, h // 2, 64 * half:64 * half + 64],
                                            kT[rows, b, h // 2, k0:k0 + P], start=True, stop=True)
                    ins.then_inc(s["scored"], 1)

                def turn_probs(u):
                    if u == 0:
                        pe.wait_ge(s["rot_dve"], 2 * NT)
                        pe.wait_ge(s["squared"], 2 * NT)
                    pe.wait_ge(s["probs"], 4 * (u + 1))
                    if u >= 2:
                        pe.wait_ge(s["pT"], u - 1)
                    for c in range(4):
                        ins = pe.transpose(bank[2 + u % 2][:, c * P:(c + 1) * P], pr[:, u % 2, c, :], w.ident[:])
                    ins.then_inc(s["pT_ps"], 1)

                def weigh_values(u):
                    t, e = divmod(u, 2)
                    b, i = divmod(t, TPB)
                    if u == 0:
                        pe.wait_ge(s["v_sb"], NB * VSETS)
                        pe.wait_ge(s["ones"], 1)
                    pe.wait_ge(s["pT"], u + 1)
                    if u >= 2:
                        pe.wait_ge(s["o_sb"], u - 1)
                    for c in range(4):
                        h = 2 * c + e
                        for half in range(2):
                            ins = pe.matmul(bank[4 + u % 2][64 * half:64 * half + 64, c * (DH + 1):(c + 1) * (DH + 1)],
                                            pT[:, u % 2, c, 64 * half:64 * half + 64],
                                            v[:, b, first_key(i, half) // WIN, h, :], start=True, stop=True)
                    ins.then_inc(s["pv"], 1)

                def turn_out(t):
                    pe.wait_ge(s["o_sb"], 2 * t + 2)
                    if t == 0:
                        pe.wait_ge(s["qT"], NT)
                        pe.wait_ge(s["kT"], NT)
                    if t >= 1:
                        pe.wait_ge(s["oT"], t)
                    for i in range(PAIRH):
                        ins = pe.transpose(bank[6][:, i * P:(i + 1) * P], o[:, t, i * P:(i + 1) * P], w.ident[:])
                    ins.then_inc(s["oT_ps"], 1)

                def project_out(t):
                    pe.wait_ge(s["oT"], t + 1)
                    if t >= 1:
                        pe.wait_ge(s["y_attn"], t)
                    for i in range(PAIRH):
                        ins = pe.matmul(bank[7][:, 0:D], oT[:, t % 2, i, :], w.wo_l[:, bass.ds(layer, 1), i, :],
                                        start=(i == 0), stop=(i == PAIRH - 1))
                    ins.then_inc(s["wo"], 1)

                project(0)
                project(1)
                for r in range(3):
                    project_values(r)
                turn(0)
                project(2)
                turn(1)
                project(3)
                for r in range(3, 6):
                    project_values(r)
                turn(2)
                for i in range(NU + 4):
                    if i == 3:
                        turn(3)
                    if i < NU:
                        scores(i)
                    if 1 <= i <= NU:
                        turn_probs(i - 1)
                    if 2 <= i <= NU + 1:
                        weigh_values(i - 2)
                    if i >= 4 and i % 2 == 0:
                        turn_out((i - 4) // 2)
                    if i >= 5 and i % 2 == 1:
                        project_out((i - 5) // 2)

                def shift(b):
                    t = b * TPB
                    pe.wait_ge(s["y_attn"], t + 2)
                    if b == 0:
                        pe.wait_ge(s["shifted_scores"], 4 * NU)
                    dst = bank[b][:, 0:TPB * HALF].rearrange("p (i d) -> p i d", i=TPB)
                    pe.matmul(dst, w.shift_m[:], w.y[:, t:t + TPB, HALF:D], start=True, stop=False)
                    pe.matmul(dst[:, 1], w.edge_m[:], w.y[:, t, HALF:D], start=False, stop=True).then_inc(s["shifted"], 1)

                def turn_normed(b):
                    pe.wait_ge(s["normed"], 4 * (b + 1))
                    if b == 0:
                        pe.wait_ge(s["oT"], NT)
                    if b == 1:
                        pe.wait_ge(s["y_attn"], NT)
                    for i in range(TPB):
                        ins = pe.transpose(bank[6 + b][:, i * P:(i + 1) * P], n[:, b * TPB + i, :], w.ident[:])
                    ins.then_inc(s["nT_ps"], 1)

                def widen(t):
                    pe.wait_ge(s["hnT"], t // TPB + 1)
                    if t == 0:
                        pe.wait_ge(s["pT"], NU)
                        pe.wait_ge(s["o_sb"], NU)
                    if t >= 2:
                        pe.wait_ge(s["gated_in"], 2 * (t - 1))
                    for c in (1, 0):
                        pe.matmul(bank[2 + 2 * (t % 2) + c][:, 0:HID], hnT[:, t, :],
                                  w.w1_l[:, bass.ds(layer, 1), HID * c:HID * (c + 1)],
                                  start=True, stop=True).then_inc(s["w1"], 1)

                def turn_gated(t):
                    pe.wait_ge(s["gated"], t + 1)
                    if t == 0:
                        pe.wait_ge(s["pad"], 2)
                        pe.wait_ge(s["normed"], 4 * NB)
                    if t >= 2:
                        pe.wait_ge(s["gT"], t - 1)
                    for i in range(HIDT):
                        ins = pe.transpose(bank[t % 2][:, i * P:(i + 1) * P], gated[:, t % 2, i * P:(i + 1) * P], w.ident[:])
                    ins.then_inc(s["gT_ps"], 1)

                def narrow(t):
                    pe.wait_ge(s["gT"], t + 1)
                    if t == 0:
                        pe.wait_ge(s["hnT"], NB)
                    if t >= 1:
                        pe.wait_ge(s["y_new"], t)
                    for i in range(HIDT):
                        ins = pe.matmul(bank[7][:, 0:D], gT[:, t % 2, i, :], w.w2_l[:, bass.ds(layer, 1), i, :],
                                        start=(i == 0), stop=(i == HIDT - 1))
                    ins.then_inc(s["w2"], 1)

                shift(0)
                shift(1)
                turn_normed(0)
                widen(0)
                turn_normed(1)
                widen(1)
                turn_gated(0)
                widen(2)
                narrow(0)
                turn_gated(1)
                widen(3)
                narrow(1)
                turn_gated(2)
                narrow(2)
                turn_gated(3)
                narrow(3)

            @block.scalar
            def _(act):
                for b in range(NB):
                    act.wait_ge(s["yT_ps"], b + 1)
                    nc.scalar.copy(hT[0:HALF, b, :], bank[6 + b][0:HALF, 0:T]).then_inc(s["hT_a"], 1)

                def squares(t):
                    if t >= 2:
                        act.wait_ge(s["summed"], 2 * (t - 1))
                    for c in range(2):
                        act.wait_ge(s["qk_proj"], 2 * t + c + 1)
                        nc.scalar.activation(sq[:, t % 2, c, :], bank[2 * (t % 2) + c][:], ACT.Square).then_inc(s["squared"], 1)

                def root(t):
                    act.wait_ge(s["summed"], 2 * (t + 1))
                    nc.scalar.activation(norm[:, t], ss[:, t], ACT.Sqrt).then_inc(s["norm"], 1)

                def values(r):
                    b, i = divmod(r, VSETS)
                    act.wait_ge(s["v_proj"], r + 1)
                    nc.scalar.copy(v[:, b, i, :, 0:DH], bank[4 + r % 2][:].rearrange("p (h d) -> p h d", h=HL)
                                   ).then_inc(s["v_sb"], 1)

                def turned(t):
                    b, i = divmod(t, TPB)
                    act.wait_ge(s["qT_ps"], t + 1)
                    nc.scalar.copy(qT[:, t].rearrange("p j k -> p (j k)"), bank[6][:]).then_inc(s["qT"], 1)
                    act.wait_ge(s["kT_ps"], t + 1)
                    nc.scalar.copy(kT[:, b, :, i * P:(i + 1) * P], bank[7][:].rearrange("p (j k) -> p j k", j=PAIRH)
                                   ).then_inc(s["kT"], 1)

                def exps(u):
                    if u >= 2:
                        act.wait_ge(s["pT_ps"], u - 1)
                    for c in range(4):
                        act.wait_ge(s["shifted_scores"], 4 * u + c + 1)
                        nc.scalar.activation(pr[:, u % 2, c, :], sc[:, u % 2, c, :], ACT.Exp,
                                             bias=neg_max[:, u, c:c + 1], scale=-1.0).then_inc(s["probs"], 1)

                def turned_out(t):
                    act.wait_ge(s["oT_ps"], t + 1)
                    if t >= 2:
                        act.wait_ge(s["wo"], t - 1)
                    nc.scalar.copy(oT[:, t % 2].rearrange("p j k -> p (j k)"), bank[6][:]).then_inc(s["oT"], 1)

                squares(0)
                squares(1)
                root(0)
                values(0)
                values(1)
                root(1)
                values(2)
                turned(0)
                squares(2)
                root(2)
                turned(1)
                squares(3)
                values(3)
                root(3)
                values(4)
                values(5)
                turned(2)
                for i in range(NU + 4):
                    if i == 3:
                        turned(3)
                    if i < NU:
                        exps(i)
                    if i >= 4 and i % 2 == 0:
                        turned_out((i - 4) // 2)

                for b in range(NB):
                    act.wait_ge(s["var_ready"], TPB * (b + 1))
                    ts = slice(b * TPB, (b + 1) * TPB)
                    nc.scalar.activation(w.std[:, ts], w.mean_var[:, ts, 1], ACT.Sqrt,
                                         bias=w.eps_t[:, 0:1]).then_inc(s["std_ready"], 1)

                def affine(b):
                    act.wait_ge(s["nT_ps"], b + 1)
                    nc.scalar.activation(hnT[:, b * TPB:(b + 1) * TPB, :].rearrange("p t k -> p (t k)"),
                                         bank[6 + b][:, 0:T], ACT.Identity, bias=lb[:, 0:1],
                                         scale=lg[:, 0:1]).then_inc(s["hnT"], 1)

                def gelu(t):
                    act.wait_ge(s["gated_in"], 2 * t + 1)
                    if t >= 2:
                        act.wait_ge(s["gated"], t - 1)
                    nc.scalar.activation(gel[:, t % 2, :], gin[:, t % 2, :], ACT.Gelu).then_inc(s["gelu"], 1)

                def turned_gated(t):
                    act.wait_ge(s["gT_ps"], t + 1)
                    if t >= 2:
                        act.wait_ge(s["w2"], t - 1)
                    nc.scalar.copy(gT[:, t % 2].rearrange("p j k -> p (j k)"), bank[t % 2][:, 0:HIDT * P]).then_inc(s["gT"], 1)

                act.wait_ge(s["pad"], 2)
                affine(0)
                affine(1)
                gelu(0)
                gelu(1)
                turned_gated(0)
                gelu(2)
                turned_gated(1)
                gelu(3)
                turned_gated(2)
                turned_gated(3)

            @block.vector
            def _(dve):
                st = Steps(dve, s["dve"])
                k0 = st.did(nc.vector.tensor_copy(tab[:].rearrange("p i t c d -> p (i t c d)"),
                                                  w.rot_l[:, bass.ds(layer, 1)].rearrange("p l i t c d -> p (l i t c d)")))
                for b in range(NB):
                    dve.wait_ge(s["yT_ps"], b + 1)
                    nc.vector.tensor_copy(hT[HALF:P, b, 1:T], bank[6 + b][HALF:P, 0:T - 1]).then_inc(s["hT_d"], 1)
                st.wait(k0)

                def rotate(t):
                    i = t % TPB
                    if t >= 2:
                        dve.wait_ge(s["rot_pool"], 2 * (t - 1))
                    for c in range(2):
                        dve.wait_ge(s["squared"], 2 * t + c + 1)
                        nc.vector.tensor_reduce(ss[:, t, c, :], sq[:, t % 2, c, :].rearrange("p (h d) -> p h d", h=HL),
                                                AX.X, ALU.add).then_inc(s["summed"], 1)
                    for c in range(2):
                        ps = bank[2 * (t % 2) + c][:]
                        st.did(nc.vector.tensor_tensor(
                            r1[:, t % 2, c, :].rearrange("p (h d) -> p h d", h=HL), ps.rearrange("p (h d) -> p h d", h=HL),
                            tab[:, c, i, 0, :].unsqueeze(1).broadcast_to((P, HL, DH)), ALU.mult))
                        nc.vector.tensor_tensor(
                            r2[:, t % 2, c, :].rearrange("p (h s d) -> p h s d", h=HL, s=2),
                            ps.rearrange("p (h s d) -> p h s d", h=HL, s=2)[:, :, ::-1, :],
                            tab[:, c, i, 1, :].rearrange("p (s d) -> p s d", s=2).unsqueeze(1)
                            .broadcast_to((P, HL, 2, DH // 2)), ALU.mult).then_inc(s["rot_dve"], 1)
                        if c == 0:
                            dve.wait_ge(s["norm"], t + 1)
                            k = st.did(nc.vector.tensor_scalar(norm[:, t], norm[:, t], 1e-12, None, ALU.max))
                            st.wait(k)
                            nc.vector.reciprocal(rn[:, t], norm[:, t]).then_inc(s["rn"], 1)

                for t in range(NT):
                    rotate(t)

                def shift_scores(u):
                    t, e = divmod(u, 2)
                    if u == 0:
                        dve.wait_ge(s["rn"], NT)
                    if u >= 2:
                        dve.wait_ge(s["probs"], 4 * (u - 1))
                    dve.wait_ge(s["scored"], u + 1)
                    for c in range(4):
                        nc.vector.tensor_tensor_reduce(
                            out=sc[:, u % 2, c, :], in0=bank[u % 2][:, c * P:(c + 1) * P], in1=w.mask_l[:, t % TPB, :],
                            scale=rn[:, t, 0, 2 * c + e:2 * c + e + 1], scalar=3e38, op0=ALU.add, op1=ALU.min,
                            accum_out=neg_max[:, u, c:c + 1]).then_inc(s["shifted_scores"], 1)

                def turned_probs(u):
                    dve.wait_ge(s["pT_ps"], u + 1)
                    if u >= 2:
                        dve.wait_ge(s["pv"], u - 1)
                    nc.vector.tensor_copy(pT[:, u % 2].rearrange("p c q -> p (c q)"), bank[2 + u % 2][:]).then_inc(s["pT"], 1)

                def normalise(u):
                    t, e = divmod(u, 2)
                    dve.wait_ge(s["pv"], u + 1)
                    src = bank[4 + u % 2][:, 0:4 * (DH + 1)].rearrange("p (c d) -> p c d", c=4)
                    k = st.did(nc.vector.reciprocal(rsum[:, u, :], src[:, :, DH]))
                    st.wait(k)
                    nc.vector.tensor_tensor(
                        o[:, t, :].rearrange("p (c e d) -> p c e d", c=4, e=2)[:, :, e, :], src[:, :, 0:DH],
                        rsum[:, u, :].unsqueeze(2).broadcast_to((P, 4, DH)), ALU.mult).then_inc(s["o_sb"], 1)

                def residual(t):
                    dve.wait_ge(s["wo"], t + 1)
                    nc.vector.tensor_tensor(w.y[:, t, :], w.y[:, t, :], bank[7][:, 0:D], ALU.add).then_inc(s["y_attn"], 1)

                for i in range(NU + 4):
                    if i < NU:
                        shift_scores(i)
                    if 1 <= i <= NU:
                        turned_probs(i - 1)
                    if 2 <= i <= NU + 1:
                        normalise(i - 2)
                    if i >= 5 and i % 2 == 1:
                        residual((i - 5) // 2)

                def statistics(b):
                    dve.wait_ge(s["y_attn"], TPB * (b + 1))
                    for i in range(TPB):
                        t = b * TPB + i
                        st.did(nc.vector.bn_stats(w.stats[:, t, 0, :], w.y[:, t, 0:HALF]))
                    dve.wait_ge(s["shifted"], b + 1)
                    for i in range(TPB):
                        t = b * TPB + i
                        k = st.did(nc.vector.bn_stats(w.stats[:, t, 1, :], bank[b][:, i * HALF:(i + 1) * HALF]))
                    st.wait(k)
                    for i in range(TPB):
                        t = b * TPB + i
                        nc.vector.bn_aggr(w.mean_var[:, t, :], w.stats[:, t].rearrange("p a b -> p (a b)")
                                          ).then_inc(s["var_ready"], 1)

                def normed(b):
                    ts = slice(b * TPB, (b + 1) * TPB)
                    dve.wait_ge(s["std_ready"], b + 1)
                    k = st.did(nc.vector.reciprocal(w.rstd[:, ts], w.std[:, ts]))
                    st.wait(k)
                    for i in range(TPB):
                        t = b * TPB + i
                        for c, src in ((0, w.y[:, t, 0:HALF]), (1, bank[b][:, i * HALF:(i + 1) * HALF])):
                            nc.vector.tensor_scalar(n[:, t, c * HALF:(c + 1) * HALF], src, w.mean_var[:, t, 0:1],
                                                    w.rstd[:, t:t + 1], ALU.subtract, ALU.mult).then_inc(s["normed"], 1)

                def gate_in(t):
                    if t == 0:
                        dve.wait_ge(s["pad"], 2)
                    if t >= 2:
                        dve.wait_ge(s["gelu"], t - 1)
                        dve.wait_ge(s["gated"], t - 1)
                    dve.wait_ge(s["w1"], 2 * t + 1)
                    nc.vector.tensor_tensor(gin[:, t % 2, :], bank[3 + 2 * (t % 2)][:, 0:HID], b1[:, HID:2 * HID],
                                            ALU.add).then_inc(s["gated_in"], 1)
                    dve.wait_ge(s["w1"], 2 * t + 2)
                    nc.vector.tensor_tensor(ain[:, t % 2, :], bank[2 + 2 * (t % 2)][:, 0:HID], b1[:, 0:HID],
                                            ALU.add).then_inc(s["gated_in"], 1)

                def gate(t):
                    dve.wait_ge(s["gelu"], t + 1)
                    dve.wait_ge(s["gated_in"], 2 * t + 2)
                    if t >= 2:
                        dve.wait_ge(s["gT_ps"], t - 1)
                    nc.vector.tensor_tensor(gated[:, t % 2, 0:HID], ain[:, t % 2, :], gel[:, t % 2, :],
                                            ALU.mult).then_inc(s["gated"], 1)

                def update(t):
                    if t == 0:
                        dve.wait_ge(s["y_bias"], 1)
                    dve.wait_ge(s["w2"], t + 1)
                    nc.vector.tensor_tensor(w.y[:, t, :], yb[:, t, :], bank[7][:, 0:D], ALU.add).then_inc(s["y_new"], 1)

                statistics(0)
                statistics(1)
                normed(0)
                normed(1)
                gate_in(0)
                gate(0)
                gate_in(1)
                gate(1)
                gate_in(2)
                update(0)
                gate(2)
                gate_in(3)
                update(1)
                gate(3)
                update(2)
                update(3)

            @block.gpsimd
            def _(pool):
                nc.gpsimd.memset(hT[HALF:P, :, 0:1], 0.0).then_inc(s["edge_zero"], 1)
                pool.wait_ge(s["edge_zero"], 1)
                nc.gpsimd.memset(v[:, :, :, :, DH:DH + 1], 1.0).then_inc(s["ones"], 1)
                nc.gpsimd.memset(gated[:, :, HID:], 0.0).then_inc(s["pad"], 1)
                nc.gpsimd.tensor_copy(b1[:], w.b1_l[:, bass.ds(layer, 1), :].rearrange("p l n -> p (l n)")).then_inc(s["pool"], 1)
                nc.gpsimd.tensor_copy(lgb[:], w.ln_gb[:, :, bass.ds(layer, 1)]).then_inc(s["pool"], 1)
                pool.wait_ge(s["pool"], 2)
                nc.gpsimd.memset(yb[:], 0.0).then_inc(s["pad"], 1)
                for t in range(NT):
                    for c in range(2):
                        pool.wait_ge(s["rot_dve"], 2 * t + c + 1)
                        if t >= 2:
                            pool.wait_ge(s["qT_ps"] if c == 0 else s["kT_ps"], t - 1)
                        dst = qk[:, t % 2, 0, :] if c == 0 else kr[:, t % 2, :]
                        ins = nc.gpsimd.tensor_tensor(dst, r1[:, t % 2, c, :], r2[:, t % 2, c, :], ALU.add)
                        if c == 0:
                            ins.then_inc(s["rot_pool"], 1)
                            continue
                        ins.then_inc(s["pool"], 1)
                        pool.wait_ge(s["pool"], 3 + t)
                        pool.wait_ge(s["rn"], t + 1)
                        nc.gpsimd.tensor_tensor(
                            qk[:, t % 2, 1, :].rearrange("p (h d) -> p h d", h=HL),
                            kr[:, t % 2, :].rearrange("p (h d) -> p h d", h=HL),
                            rn[:, t, 1, :].unsqueeze(2).broadcast_to((P, HL, DH)), ALU.mult).then_inc(s["rot_pool"], 1)
                pool.wait_ge(s["y_attn"], NT)
                pool.wait_ge(s["pad"], 2)
                nc.gpsimd.tensor_tensor(yb[:], w.y[:], w.b2_l[:, bass.ds(layer, 1), :].broadcast_to((P, NT, D)),
                                        ALU.add).then_inc(s["y_bias"], 1)
        clear(nc, s)


def attention_b(nc, w, pair):
    with ExitStack() as ctx:
        def sb(name, shape):
            return ctx.enter_context(nc.sbuf_tensor("b_" + name, shape, F32))

        s = signals(nc, ctx, "b", "dve x_new var_ready std_ready normed xT_ps xT proj q_sb k_sb v_sum vd hidden_ps hidden "
                                  "q1 q1_sb norms nT_ps bounds diag spread weights wT_ps wT vw_ps vw out_ps x_out var2 std2 "
                                  "pool xbo")
        xn, xT = sb("xn", [P, NT, D]), sb("xT", [P, NT * P])
        qkT = sb("qkT", [P, 2, NT * P])
        v_sum, v_mean = sb("v_sum", [P, NB]), sb("v_mean", [P, NB])
        vd = sb("vd", [P, NB, HB])
        hidden = sb("hidden", [P, 3, NT * P])
        UN = 2 * HB
        q1 = sb("q1", [P, NT, UN, 2 * NQ])
        e1, e2, e3 = sb("e1", [P, NT, UN, NQ]), sb("e2", [P, NT, UN, NQ]), sb("e3", [P, NT, UN, NQ])
        norms = sb("norms", [P, NT, UN])
        bounds = sb("bounds", [HB, 3, NB])
        kz = sb("kz", [HB, NB, T])
        diag = sb("diag", [HB, 3, NB, HB])
        prod = sb("prod", [P, NT, 2, HB])
        ne, rec, quot = sb("ne", [P, NT, 2, HB]), sb("rec", [P, NT, 2, HB]), sb("quot", [P, NT, 2, HB])
        wgt = sb("wgt", [P, NT, HB])
        wT, vw = sb("wT", [HB, NT, P]), sb("vw", [HB, NB, D])
        mix = sb("mix", [P, 2, HB])
        bank = [ctx.enter_context(nc.psum_tensor(f"b_bank{i}", [P, 512], F32)) for i in range(8)]

        with nc.Block() as block:
            @block.tensor
            def _(pe):
                pe.wait_ge(s["normed"], NT)
                for t in range(NT):
                    pe.transpose(bank[3][:, t * P:(t + 1) * P], xn[:, t, :], w.ident[:]).then_inc(s["xT_ps"], 1)
                pe.wait_ge(s["xT"], 1)
                for c in range(3):
                    pe.matmul(bank[c][:], w.wqkv_b[:, c, :], xT[:], start=True, stop=True).then_inc(s["proj"], 1)

                def hide(v):
                    c, h = divmod(v, HB)
                    if v == 0:
                        pe.wait_ge(s["q_sb"], 1)
                    if v == 1:
                        pe.wait_ge(s["k_sb"], 1)
                    if v == 3:
                        pe.wait_ge(s["v_sum"], 1)
                    if v >= 4:
                        pe.wait_ge(s["hidden"], v - 3)
                    pe.matmul(bank[(v + 3) % 4][:], w.w1_b[:, h, :], qkT[:, c, :], start=True, stop=True)\
                        .then_inc(s["hidden_ps"], 1)

                def encode(v):
                    pe.wait_ge(s["hidden"], v + 1)
                    for t in range(NT):
                        ins = pe.matmul(bank[4 + t][:, 2 * NQ * v:2 * NQ * (v + 1)], hidden[:, v % 3, t * P:(t + 1) * P],
                                        w.w2_b[:], start=True, stop=True)
                    ins.then_inc(s["q1"], 1)

                for v in range(UN + 2):
                    if v < UN:
                        hide(v)
                    if v >= 2:
                        encode(v - 2)
                pe.wait_ge(s["norms"], 1)
                for t in range(NT):
                    ins = pe.transpose(bank[0][0:HB, t * P:(t + 1) * P], norms[:, t, HB:UN], w.ident[:])
                ins.then_inc(s["nT_ps"], 1)
                pe.wait_ge(s["vd"], 1)
                for b in range(NB):
                    ins = pe.matmul(bank[1][0:HB, b * D:(b + 1) * D], vd[:, b, :], w.wo_b[:], start=True, stop=True)
                ins.then_inc(s["vw_ps"], 1)
                pe.wait_ge(s["diag"], 1)
                pe.matmul(bank[2][:, 0:3 * NB * HB], w.ones_t[0:HB, :], diag[:].rearrange("p c b h -> p (c b h)"),
                          start=True, stop=True).then_inc(s["spread"], 1)
                pe.wait_ge(s["weights"], 1)
                for t in range(NT):
                    ins = pe.transpose(bank[3][0:HB, t * P:(t + 1) * P], wgt[:, t, :], w.ident[:])
                ins.then_inc(s["wT_ps"], 1)
                pe.wait_ge(s["wT"], 1)
                pe.wait_ge(s["vw"], 1)
                for t in range(NT):
                    ins = pe.matmul(bank[0][:, t * D:(t + 1) * D], wT[:, t, :], vw[:, t // TPB, :], start=True, stop=True)
                ins.then_inc(s["out_ps"], 1)

            @block.scalar
            def _(act):
                act.wait_ge(s["var_ready"], NT)
                nc.scalar.activation(w.std[:], w.mean_var[:, :, 1], ACT.Sqrt, bias=w.eps_t[:, 0:1]).then_inc(s["std_ready"], 1)
                act.wait_ge(s["xT_ps"], NT)
                nc.scalar.copy(xT[:], bank[3][:]).then_inc(s["xT"], 1)
                act.wait_ge(s["proj"], 1)
                nc.scalar.activation(qkT[:, 0, :], bank[0][:], ACT.Identity, bias=w.bqkv_b[:, 0:1]).then_inc(s["q_sb"], 1)
                for v in range(UN):
                    act.wait_ge(s["hidden_ps"], v + 1)
                    if v >= 3:
                        act.wait_ge(s["q1"], v - 2)
                    nc.scalar.activation(hidden[:, v % 3, :], bank[(v + 3) % 4][:], ACT.Tanh,
                                         bias=w.b1_b[:, 0:1]).then_inc(s["hidden"], 1)
                act.wait_ge(s["vw_ps"], 1)
                nc.scalar.copy(vw[:].rearrange("p b n -> p (b n)"), bank[1][0:HB, 0:NB * D]).then_inc(s["vw"], 1)
                act.wait_ge(s["wT_ps"], 1)
                nc.scalar.copy(wT[:].rearrange("p t k -> p (t k)"), bank[3][0:HB, :]).then_inc(s["wT"], 1)
                act.wait_ge(s["var2"], NT)
                nc.scalar.activation(w.std[:], w.mean_var[:, :, 1], ACT.Sqrt, bias=w.eps_t[:, 0:1]).then_inc(s["std2"], 1)

            @block.gpsimd
            def _(pool):
                nc.gpsimd.tensor_copy(mix[:].rearrange("p c h -> p (c h)"),
                                      w.mix_b[:, bass.ds(pair, 1)].rearrange("p o c h -> p (o c h)")).then_inc(s["pool"], 1)
                pool.wait_ge(s["x_new"], 1)
                pool.wait_ge(s["normed"], NT)
                nc.gpsimd.tensor_tensor(w.x[:], w.x[:], w.bo_b[:].unsqueeze(1).broadcast_to((P, NT, D)),
                                        ALU.add).then_inc(s["xbo"], 1)

            @block.vector
            def _(dve):
                st = Steps(dve, s["dve"])

                def then(instruction):
                    st.wait(st.did(instruction))

                nc.vector.tensor_tensor(w.x[:], w.x[:], w.y[:], ALU.add).then_inc(s["x_new"], 1)
                dve.wait_ge(s["x_new"], 1)
                layer_norm_stats(nc, dve, st, w, range(NT), w.x, s, s["var_ready"])
                dve.wait_ge(s["std_ready"], 1)
                then(nc.vector.reciprocal(w.rstd[:], w.std[:]))
                for t in range(NT):
                    nc.vector.tensor_scalar(xn[:, t, :], w.x[:, t, :], w.mean_var[:, t, 0:1], w.rstd[:, t:t + 1],
                                            ALU.subtract, ALU.mult).then_inc(s["normed"], 1)
                dve.wait_ge(s["proj"], 2)
                nc.vector.tensor_scalar(qkT[:, 1, :], bank[1][:], w.bqkv_b[:, 1:2], None, ALU.add).then_inc(s["k_sb"], 1)
                dve.wait_ge(s["proj"], 3)
                nc.vector.tensor_reduce(v_sum[:], bank[2][:].rearrange("p (b k) -> p b k", b=NB), AX.X, ALU.add)\
                    .then_inc(s["v_sum"], 1)
                dve.wait_ge(s["v_sum"], 1)
                then(nc.vector.tensor_scalar(v_mean[:], v_sum[:], 1.0 / T, w.bqkv_b[:, 2:3], ALU.mult, ALU.add))
                for b in range(NB):
                    ins = nc.vector.tensor_scalar(vd[:, b, :], w.head_of[:], v_mean[:, b:b + 1], None, ALU.mult)
                    if b < NB - 1:
                        st.did(ins)
                ins.then_inc(s["vd"], 1)

                dve.wait_ge(s["q1"], UN)
                b2 = w.b2_b[:].unsqueeze(1).broadcast_to((P, UN, 2 * NQ))
                for t in range(NT):
                    k = st.did(nc.vector.tensor_tensor(q1[:, t], bank[4 + t][:].rearrange("p (v n) -> p v n", v=UN), b2, ALU.add))
                st.wait(k)
                dve.wait_ge(s["pool"], 1)
                for t in range(NT):
                    other = (t + TPB) % NT
                    for dst, src, c in ((e1, q1[:, t, :, 0:NQ], 0), (e2, q1[:, other, :, NQ:2 * NQ], 1)):
                        table = mix[:, c, :].unsqueeze(1).unsqueeze(3).broadcast_to((P, 2, HB, NQ))
                        k = st.did(nc.vector.tensor_tensor(dst[:, t].rearrange("p (c h) n -> p c h n", c=2),
                                                           src.rearrange("p (c h) n -> p c h n", c=2), table, ALU.mult))
                st.wait(k)
                then(nc.vector.tensor_tensor(e3[:], e1[:], e2[:], ALU.add))
                then(nc.vector.tensor_tensor(e1[:], e3[:], e3[:], ALU.mult))
                nc.vector.tensor_reduce(norms[:], e1[:], AX.X, ALU.add).then_inc(s["norms"], 1)
                dve.wait_ge(s["nT_ps"], 1)
                keys = bank[0][0:HB, :].rearrange("p (b k) -> p b k", b=NB)
                st.did(nc.vector.tensor_reduce(bounds[:, 0, :], keys, AX.X, ALU.min))
                st.did(nc.vector.tensor_reduce(bounds[:, 1, :], keys, AX.X, ALU.max))
                then(nc.vector.tensor_scalar(kz[:], keys, 0.0, None, ALU.mult))
                then(nc.vector.tensor_reduce(bounds[:, 2, :], kz[:], AX.X, ALU.add))
                for c in range(3):
                    for b in range(NB):
                        ins = nc.vector.tensor_scalar(diag[:, c, b, :], w.ident[0:HB, 0:HB], bounds[:, c, b:b + 1], None, ALU.mult)
                        if (c, b) != (2, NB - 1):
                            st.did(ins)
                ins.then_inc(s["diag"], 1)
                dve.wait_ge(s["norms"], 1)
                dve.wait_ge(s["spread"], 1)
                spread = bank[2][:, 0:3 * NB * HB].rearrange("p (c b h) -> p c b h", c=3, b=NB)
                for b in range(NB):
                    for c in range(2):
                        queries = norms[:, b * TPB:(b + 1) * TPB, 0:HB]
                        k = st.did(nc.vector.tensor_tensor(prod[:, b * TPB:(b + 1) * TPB, c, :], queries,
                                                           spread[:, c, b, :].unsqueeze(1).broadcast_to((P, TPB, HB)), ALU.mult))
                st.wait(k)
                then(nc.vector.tensor_scalar(ne[:], prod[:], 0.0, None, ALU.not_equal))
                then(nc.vector.reciprocal(rec[:], ne[:]))
                then(nc.vector.tensor_tensor(rec[:], rec[:], ne[:], ALU.mult))
                then(nc.vector.scalar_tensor_tensor(out=quot[:], in0=prod[:], scalar=0.0, in1=rec[:], op0=ALU.mult, op1=ALU.add))
                then(nc.vector.tensor_tensor(wgt[:], quot[:, :, 0, :], quot[:, :, 1, :], ALU.mult))
                for b in range(NB):
                    ts = slice(b * TPB, (b + 1) * TPB)
                    ins = nc.vector.tensor_tensor(wgt[:, ts, :], wgt[:, ts, :],
                                                  spread[:, 2, b, :].unsqueeze(1).broadcast_to((P, TPB, HB)), ALU.add)
                    if b < NB - 1:
                        st.did(ins)
                ins.then_inc(s["weights"], 1)
                dve.wait_ge(s["out_ps"], 1)
                dve.wait_ge(s["xbo"], 1)
                nc.vector.tensor_tensor(w.x[:], w.x[:], bank[0][:].rearrange("p (t n) -> p t n", t=NT), ALU.add).then_inc(s["x_out"], 1)
                dve.wait_ge(s["x_out"], 1)
                layer_norm_stats(nc, dve, st, w, range(NT), w.x, s, s["var2"])
                dve.wait_ge(s["std2"], 1)
                then(nc.vector.reciprocal(w.rstd[:], w.std[:]))
                for t in range(NT):
                    st.did(nc.vector.tensor_scalar(w.y[:, t, :], w.x[:, t, :], w.mean_var[:, t, 0:1], w.rstd[:, t:t + 1],
                                                   ALU.subtract, ALU.mult))
        clear(nc, s)


def store(nc, w, pair, out):
    with ExitStack() as ctx:
        s = signals(nc, ctx, "store", "summed stored")
        with nc.Block() as block:
            @block.vector
            def _(dve):
                nc.vector.tensor_tensor(w.x[:], w.x[:], w.y[:], ALU.add).then_inc(s["summed"], 1)

            @block.sync
            def _(sp):
                sp.wait_ge(s["summed"], 1)
                dst = out.rearrange("(g b) (c p) d -> p g (b c) d", b=NB, p=P)
                sp.dma_start(dst[:, bass.ds(pair, 1), :, :], w.x[:]).then_inc(s["stored"], 16)
                sp.wait_ge(s["stored"], 16)
        clear(nc, s)


def turned_inputs(inputs):
    return {
        "ln_g_by_feature": np.ascontiguousarray(np.asarray(inputs["L0_ffn_ln_g"]).T),
        "ln_b_by_feature": np.ascontiguousarray(np.asarray(inputs["L0_ffn_ln_b"]).T),
        "w2_transposed": np.ascontiguousarray(np.asarray(inputs["L0_attn_b_w2"]).T),
        "angles_by_pair": np.ascontiguousarray(np.asarray(inputs["L0_attn_b_rot"])[:, 0:NQ // 2, 0].T),
    }


INPUTS = ["L0_attn_a_x", "L0_attn_a_Wq", "L0_attn_a_Wk", "L0_attn_a_Wv", "L0_attn_a_Wo",
          "L0_attn_a_polarity_direction", "L0_attn_a_gtp_gamma", "L0_attn_b_wq", "L0_attn_b_bq", "L0_attn_b_wk",
          "L0_attn_b_bk", "L0_attn_b_wv", "L0_attn_b_bv", "L0_attn_b_wo", "L0_attn_b_bo", "L0_attn_b_w1",
          "L0_attn_b_b1", "L0_attn_b_b2", "L0_attn_b_hadamard", "L0_ffn_wqkv",
          "L0_ffn_q_scale", "L0_ffn_k_scale", "L0_ffn_wo", "L0_ffn_w1", "L0_ffn_b1",
          "L0_ffn_w2", "L0_ffn_b2"]


def kernel(**inputs):
    import concourse.bacc as bacc
    from concourse.bass_utils import run_bass_kernel_spmd

    nc = bacc.Bacc("TRN2", target_bir_lowering=False, num_devices=1)
    arrays, a, consts = {}, {}, {}
    for name, array in {**{n: np.ascontiguousarray(inputs[n]) for n in INPUTS}, **turned_inputs(inputs)}.items():
        arrays[f"in_{name}"] = array
        a[name] = nc.dram_tensor(f"in_{name}", array.shape, mybir.dt.from_np(array.dtype), kind="ExternalInput").ap()
    for name, array in shape_constants().items():
        arrays[f"const_{name}"] = array
        consts[name] = nc.dram_tensor(f"const_{name}", array.shape, F32, kind="ExternalInput").ap()
    out = nc.dram_tensor("out_0", (BATCH, T, D), F32, kind="ExternalOutput").ap()
    build(nc, a, consts, out)
    result = run_bass_kernel_spmd(nc, [arrays], core_ids=[0])
    return result.results[0]["out_0"]
```

```python
from contextlib import ExitStack

import numpy as np

import concourse.bass as bass
from concourse import mybir

ALU = mybir.AluOpType
ACT = mybir.ActivationFunctionType
AX = mybir.AxisListType
F32 = mybir.dt.float32

P = 128
BATCH, T, D = 16, 256, 128
NB = 2
PAIRS = BATCH // NB
TPB = T // P
NT = NB * TPB
HALF = D // 2
DH = 64
HQ, HKV = 16, 4
QW, KW = HQ * DH, HKV * DH
NEG = -1e9
SLOTS = HQ // 2
BLK = 4
STEPS_BEHIND = 5
DEPTH, HL = 2, 8
INNER = HL * DH
WIN = 64
HID = int(D * 4 * 2 / 3)
HIDT = 3
PAIRH = HL // 2
VSETS = 3
MASKED = 1e24
HB, NQ = 16, 8
HD = D // HB
EPS = 1e-5
TWO_PI = 2.0 * np.pi


class Memory:
    pass


def signals(nc, ctx, prefix, names):
    return {name: ctx.enter_context(nc.semaphore(f"{prefix}_{name}")) for name in names.split()}


class Steps:

    def __init__(self, engine, semaphore):
        self.engine, self.semaphore, self.n = engine, semaphore, 0

    def did(self, instruction):
        self.n += 1
        instruction.then_inc(self.semaphore, 1)
        return self.n

    def wait(self, n):
        self.engine.wait_ge(self.semaphore, n)


def clear(nc, s):
    with nc.Block() as block:
        @block.sync
        def _(sp):
            numbers = sorted(x.num for x in s.values())
            start = numbers[0]
            for a, b in zip(numbers, numbers[1:] + [None]):
                if b != a + 1:
                    sp.sem_clear(range(start, a + 1))
                    start = b


def shape_constants():
    c = {}
    c["identity"] = np.eye(P, dtype=np.float32)
    c["shift_down"] = np.eye(P, k=1, dtype=np.float32)
    edge = np.zeros((P, P), np.float32)
    edge[P - 1, 0] = 1
    c["edge"] = edge
    half = DH // 2
    pos = np.arange(T, dtype=np.float32)
    inv = (1.0 / np.float32(10000.0) ** (np.arange(half, dtype=np.float32) / np.float32(half))).astype(np.float32)
    ang = pos[:, None] * inv[None, :]
    cos, sin = np.cos(ang), np.sin(ang)
    rope = np.stack([np.concatenate([cos, cos], 1), np.concatenate([-sin, sin], 1)], 1)
    c["rope_a"] = np.ascontiguousarray(rope.reshape(TPB, P, 2, DH).transpose(1, 0, 2, 3)).astype(np.float32)
    hi = np.arange(0, DH, 2, dtype=np.float32)
    inv = (1.0 / np.float32(10000.0) ** (hi / np.float32(DH))).astype(np.float32)
    ang = pos[:, None] * inv[None, :]
    base = ((hi + 0.4 * DH) / (1.4 * DH)).astype(np.float32)
    power = (pos - T // 2) / np.float32(WIN // 2)
    scale = base[None, :] ** power[:, None]
    scale = np.concatenate([scale, scale], 1)
    cos, sin = np.cos(ang), np.sin(ang)
    cos, sin = np.concatenate([cos, cos], 1), np.concatenate([-sin, sin], 1)
    xpos = np.stack([np.stack([-8.0 * cos * scale, -8.0 * sin * scale], 1),
                     np.stack([cos / scale, sin / scale], 1)], 1)
    c["rope_l"] = np.ascontiguousarray(
        xpos.reshape(TPB, P, 2, 2, DH).transpose(1, 2, 0, 3, 4)).astype(np.float32)
    mask = np.zeros((P, TPB, P), np.float32)
    for tile in range(TPB):
        for p in range(P):
            i = tile * P + p
            for j in range(P):
                key = first_key(tile, p // WIN) + j
                if i < key or i > key + WIN:
                    mask[p, tile, j] = MASKED
    c["mask_l"] = mask
    q = np.arange(T, dtype=np.float32)
    causal = (q[None, :] <= q[:, None]).astype(np.float32)
    for name, table in (("signed_a", (q[None, :] - q[:, None]) / np.float32(T) * causal),
                        ("dist_a", np.maximum(q[:, None] - q[None, :], 0.0)),
                        ("causal_a", causal)):
        c[name] = np.ascontiguousarray(table.reshape(TPB, P, T).transpose(1, 0, 2)).astype(np.float32)
    c["head_of"] = np.repeat(np.eye(HB, dtype=np.float32), HD, 0)
    return c


def first_key(tile, half):
    window = 2 * tile + half
    return max(window - 1, 0) * WIN


def build(nc, a, consts, out):
    with ExitStack() as ctx:
        def sb(name, shape):
            return ctx.enter_context(nc.sbuf_tensor(name, shape, F32))

        w = Memory()
        w.ident = sb("ident", [P, P])
        w.shift_m = sb("shift_m", [P, P])
        w.edge_m = sb("edge_m", [P, P])
        w.rope_a = sb("rope_a", [P, TPB, 2, DH])
        w.rope_l = sb("rope_l", [P, 2, TPB, 2, DH])
        w.mask_l = sb("mask_l", [P, TPB, P])
        w.head_of = sb("head_of", [P, HB])
        w.eps_t = sb("eps_t", [P, 1])
        w.ones_t = sb("ones_t", [P, P])
        w.wqkv_a = sb("wqkv_a", [P, QW + 2 * KW])
        w.wo_a = sb("wo_a", [P, SLOTS, D])
        w.bias_a = sb("bias_a", [P, TPB, HQ, T])
        w.wqkv_l = sb("wqkv_l", [P, DEPTH, 3 * INNER])
        w.wo_l = sb("wo_l", [P, DEPTH, PAIRH, D])
        w.w1_l = sb("w1_l", [P, DEPTH, 2 * HID])
        w.w2_l = sb("w2_l", [P, DEPTH, HIDT, D])
        w.b1_l = sb("b1_l", [P, DEPTH, 2 * HID])
        w.b2_l = sb("b2_l", [P, DEPTH, D])
        w.ln_gb = sb("ln_gb", [P, 2, DEPTH])
        w.rot_l = sb("rot_l", [P, DEPTH, 2, TPB, 2, DH])
        w.wqkv_b = sb("wqkv_b", [P, 3, D])
        w.wo_b = sb("wo_b", [P, D])
        w.bqkv_b = sb("bqkv_b", [P, 3])
        w.w1_b = sb("w1_b", [P, HB, D])
        w.b1_b = sb("b1_b", [P, 1])
        w.w2_b = sb("w2_b", [P, 2 * NQ])
        w.b2_b = sb("b2_b", [P, 2 * NQ])
        w.bo_b = sb("bo_b", [P, D])
        w.mix_b = sb("mix_b", [P, PAIRS, 2, HB])
        w.x = sb("x", [P, NT, D])
        w.y = sb("y", [P, NT, D])
        w.stats = sb("stats", [P, NT, 2, 6])
        w.mean_var = sb("mean_var", [P, NT, 2])
        w.std = sb("std", [P, NT])
        w.rstd = sb("rstd", [P, NT])

        setup(nc, a, consts, w)
        with nc.Fori(0, PAIRS) as pair:
            attention_a(nc, a, w, pair)
            with nc.Fori(0, DEPTH) as layer:
                local_layer(nc, w, layer, "l")
            attention_b(nc, w, pair)
            with nc.Fori(0, DEPTH) as layer:
                local_layer(nc, w, layer, "m")
            store(nc, w, pair, out)


def setup(nc, a, consts, w):
    with ExitStack() as ctx:
        def sb(name, shape):
            return ctx.enter_context(nc.sbuf_tensor("setup_" + name, shape, F32))

        s = signals(nc, ctx, "setup", "zeroed small loaded exp_a dve done pe act pool placed trig")
        signed, dist, causal = (sb(n, [P, TPB, T]) for n in ("signed", "dist", "causal"))
        pol, gam = sb("pol", [P, HQ]), sb("gam", [P, HQ])
        e = sb("e", [P, 2, TPB, T])
        u = sb("u", [P, 2, TPB, T])
        v = sb("v", [P, 2, TPB, T])
        qs = sb("qs", [P, DEPTH, 2, DH])
        rot = sb("rot", [P, NQ // 2, HB])
        ang, turns, angr = sb("ang", [P, NQ // 2, 2, HB]), sb("turns", [P, NQ // 2, 2, HB]), sb("angr", [P, NQ // 2, 2, HB])
        had = sb("had", [2 * NQ, 2 * NQ])
        w2T, b2col, b2rep = sb("w2T", [2 * NQ, P]), sb("b2col", [2 * NQ, 1]), sb("b2rep", [2 * NQ, P])
        ps = ctx.enter_context(nc.psum_tensor("setup_ps", [P, 512], F32))

        plain = [
            (w.ident[:], consts["identity"]), (w.shift_m[:], consts["shift_down"]), (w.edge_m[:], consts["edge"]),
            (w.rope_a[:], consts["rope_a"]), (w.mask_l[:], consts["mask_l"]), (w.head_of[:], consts["head_of"]),
            (w.wqkv_a[:, 0:QW], a["L0_attn_a_Wq"]), (w.wqkv_a[:, QW:QW + KW], a["L0_attn_a_Wk"]),
            (w.wqkv_a[:, QW + KW:], a["L0_attn_a_Wv"]),
            (w.wqkv_l[:], a["L0_ffn_wqkv"].rearrange("l p n -> p l n")),
            (w.wo_l[:], a["L0_ffn_wo"].rearrange("l (k p) n -> p l k n", p=P)),
            (w.w1_l[:], a["L0_ffn_w1"].rearrange("l p n -> p l n")),
            (w.ln_gb[:, 0, :], a["ln_g_by_feature"]),
            (w.ln_gb[:, 1, :], a["ln_b_by_feature"]),
            (w.b1_l[:], a["L0_ffn_b1"].rearrange("(o l) n -> o l n", o=1).broadcast_to((P, DEPTH, 2 * HID))),
            (w.b2_l[:], a["L0_ffn_b2"].rearrange("(o l) n -> o l n", o=1).broadcast_to((P, DEPTH, D))),
            (w.wqkv_b[:, 0, :], a["L0_attn_b_wq"]), (w.wqkv_b[:, 1, :], a["L0_attn_b_wk"]),
            (w.wqkv_b[:, 2, :], a["L0_attn_b_wv"]), (w.wo_b[:], a["L0_attn_b_wo"]),
            (w.bqkv_b[:, 0:1], a["L0_attn_b_bq"].rearrange("(p o) -> p o", o=1)),
            (w.bqkv_b[:, 1:2], a["L0_attn_b_bk"].rearrange("(p o) -> p o", o=1)),
            (w.bqkv_b[:, 2:3], a["L0_attn_b_bv"].rearrange("(p o) -> p o", o=1)),
            (w.b1_b[:], a["L0_attn_b_b1"].rearrange("(p o) -> p o", o=1)),
            (w.bo_b[:], a["L0_attn_b_bo"].rearrange("(o n) -> o n", o=1).broadcast_to((P, D))),
        ]
        wo_rows = a["L0_attn_a_Wo"].rearrange("(b e r d) n -> b e d r n", b=SLOTS // BLK, e=2, r=BLK)
        plain += [(w.wo_a[64 * e:64 * e + 64, BLK * b:BLK * (b + 1), :], wo_rows[b, e])
                  for b in range(SLOTS // BLK) for e in range(2)]
        small = [
            (signed[:], consts["signed_a"]), (dist[:], consts["dist_a"]), (causal[:], consts["causal_a"]),
            (pol[:], a["L0_attn_a_polarity_direction"].rearrange("(o h) -> o h", o=1).broadcast_to((P, HQ))),
            (gam[:], a["L0_attn_a_gtp_gamma"].rearrange("(o h) -> o h", o=1).broadcast_to((P, HQ))),
            (w.rope_l[:], consts["rope_l"]),
            (qs[:, :, 0, :], a["L0_ffn_q_scale"].rearrange("(o l) n -> o l n", o=1).broadcast_to((P, DEPTH, DH))),
            (qs[:, :, 1, :], a["L0_ffn_k_scale"].rearrange("(o l) n -> o l n", o=1).broadcast_to((P, DEPTH, DH))),
            (rot[:], a["angles_by_pair"].rearrange("(o n) h -> o n h", o=1).broadcast_to((P, NQ // 2, HB))),
            (w2T[:], a["w2_transposed"]),
            (b2col[:], a["L0_attn_b_b2"].rearrange("(p o) -> p o", o=1)),
        ]
        placed = [(w.w1_b[HD * h:HD * (h + 1), h, :], a["L0_attn_b_w1"]) for h in range(HB)]
        placed += [(had[NQ * i:NQ * (i + 1), NQ * i:NQ * (i + 1)], a["L0_attn_b_hadamard"]) for i in range(2)]
        last = HID - (HIDT - 1) * P
        placed += [(w.w2_l[0:P, l, 0:HIDT - 1, :],
                    a["L0_ffn_w2"][l, 0:(HIDT - 1) * P, :].rearrange("(k p) n -> p k n", p=P)) for l in range(DEPTH)]
        placed += [(w.w2_l[0:last, l, HIDT - 1, :], a["L0_ffn_w2"][l, (HIDT - 1) * P:HID, :]) for l in range(DEPTH)]

        with nc.Block() as block:
            @block.sync
            def _(sp):
                for dst, src in small:
                    sp.dma_start(dst, src).then_inc(s["small"], 16)
                sp.wait_ge(s["zeroed"], 3)
                for dst, src in placed:
                    sp.dma_start(dst, src).then_inc(s["placed"], 16)
                sp.wait_ge(s["placed"], 16 * len(placed))

            @block.gpsimd
            def _(pool):
                nc.gpsimd.memset(w.w1_b[:], 0.0).then_inc(s["zeroed"], 1)
                nc.gpsimd.memset(had[:], 0.0).then_inc(s["zeroed"], 1)
                nc.gpsimd.memset(w.w2_l[:], 0.0).then_inc(s["zeroed"], 1)
                nc.gpsimd.memset(w.eps_t[:], EPS).then_inc(s["pool"], 1)
                nc.gpsimd.memset(w.ones_t[:], 1.0).then_inc(s["pool"], 1)
                nc.gpsimd.memset(w.mix_b[:, NQ // 2:, 0, :], 1.0).then_inc(s["pool"], 1)
                nc.gpsimd.memset(w.mix_b[:, NQ // 2:, 1, :], 0.0).then_inc(s["pool"], 1)

            @block.scalar
            def _(act):
                for dst, src in plain:
                    act.dma_start(dst, src).then_inc(s["loaded"], 16)
                for h in range(HQ):
                    act.wait_ge(s["done"], 1 + max(h - 1, 0))
                    nc.scalar.activation(e[:, h % 2], dist[:], ACT.Exp,
                                         scale=gam[:, h:h + 1]).then_inc(s["exp_a"], 1)
                act.wait_ge(s["trig"], 1)
                nc.scalar.activation(w.mix_b[:, 0:NQ // 2, :, :], angr[:], ACT.Sin).then_inc(s["act"], 1)
                act.wait_ge(s["loaded"], 16 * len(plain))

            @block.vector
            def _(dve):
                st = Steps(dve, s["dve"])
                dve.wait_ge(s["small"], 16 * len(small))
                n = st.did(nc.vector.tensor_scalar(pol[:], pol[:], -1.0, 1.0, ALU.max, ALU.min))
                m = st.did(nc.vector.tensor_scalar(gam[:], gam[:], 1e-4, None, ALU.max))
                st.wait(m)
                nc.vector.tensor_scalar(gam[:], gam[:], -1.0, None, ALU.mult).then_inc(s["done"], 1)
                st.did(nc.vector.tensor_scalar(ang[:, :, 0, :], rot[:], 0.5, float(np.pi / 2), ALU.mult, ALU.add))
                k = st.did(nc.vector.tensor_scalar(ang[:, :, 1, :], rot[:], 0.5, None, ALU.mult))
                st.wait(k)
                big = float(1.5 * 2 ** 23)
                k = st.did(nc.vector.tensor_scalar(turns[:], ang[:], 1.0 / TWO_PI, big, ALU.mult, ALU.add))
                st.wait(k)
                k = st.did(nc.vector.tensor_scalar(turns[:], turns[:], big, -TWO_PI, ALU.subtract, ALU.mult))
                st.wait(k)
                k = st.did(nc.vector.tensor_tensor(angr[:], ang[:], turns[:], ALU.add))
                st.wait(k)
                k = st.did(nc.vector.tensor_scalar(angr[:], angr[:], float(np.pi), float(-np.pi), ALU.min, ALU.max))
                st.wait(k)
                nc.vector.tensor_copy(ang[:], angr[:]).then_inc(s["trig"], 1)
                for l in range(DEPTH):
                    for i in range(2):
                        for t in range(TPB):
                            st.did(nc.vector.tensor_tensor(w.rot_l[:, l, i, t, 0, :], w.rope_l[:, i, t, 0, :],
                                                           qs[:, l, i, :], ALU.mult))
                            for hf in range(2):
                                lo, ot = hf * DH // 2, (1 - hf) * DH // 2
                                st.did(nc.vector.tensor_tensor(
                                    w.rot_l[:, l, i, t, 1, lo:lo + DH // 2], w.rope_l[:, i, t, 1, lo:lo + DH // 2],
                                    qs[:, l, i, ot:ot + DH // 2], ALU.mult))
                st.did(nc.vector.tensor_scalar(b2rep[:], w2T[:], 0.0, b2col[:, 0:1], ALU.mult, ALU.add))
                k = st.n
                dve.wait_ge(s["done"], 1)
                for h in range(HQ):
                    dve.wait_ge(s["exp_a"], h + 1)
                    i = h % 2
                    k1 = st.did(nc.vector.tensor_tensor(u[:, i], e[:, i], causal[:], ALU.mult))
                    k2 = st.did(nc.vector.tensor_scalar(v[:, i], signed[:], pol[:, h:h + 1], 8.0, ALU.mult, ALU.mult))
                    st.wait(k1)
                    k3 = st.did(nc.vector.tensor_scalar(u[:, i], u[:, i], -1.0, 1.0, ALU.mult, ALU.add))
                    st.wait(k3)
                    nc.vector.scalar_tensor_tensor(out=w.bias_a[:, :, h, :], in0=u[:, i], scalar=8.0 * NEG, in1=v[:, i],
                                                   op0=ALU.mult, op1=ALU.add).then_inc(s["done"], 1)
                    dve.wait_ge(s["done"], h + 2)
                dve.wait_ge(s["pe"], 1)
                nc.vector.tensor_copy(w.w2_b[:], ps[:, 0:2 * NQ]).then_inc(s["dve"], 1)
                nc.vector.tensor_copy(w.b2_b[:], ps[:, 2 * NQ:4 * NQ]).then_inc(s["dve"], 1)

            @block.tensor
            def _(pe):
                pe.wait_ge(s["placed"], 16 * len(placed))
                pe.wait_ge(s["small"], 16 * len(small))
                pe.wait_ge(s["done"], 2)
                pe.matmul(ps[:, 0:2 * NQ], w2T[:], had[:], start=True, stop=True)
                pe.matmul(ps[:, 2 * NQ:4 * NQ], b2rep[:], had[:], start=True, stop=True).then_inc(s["pe"], 1)
        clear(nc, s)


def layer_norm_stats(nc, dve, st, w, tiles, src, s, done):
    for t in tiles:
        k = st.did(nc.vector.bn_stats(w.stats[:, t, 0, :], src[:, t, :]))
    st.wait(k)
    for t in tiles:
        nc.vector.bn_aggr(w.mean_var[:, t, :], w.stats[:, t, 0, :]).then_inc(done, 1)


def attention_a(nc, a, w, pair):
    with ExitStack() as ctx:
        def sb(name, shape):
            return ctx.enter_context(nc.sbuf_tensor("a_" + name, shape, F32))

        s = signals(nc, ctx, "a", "x_loaded dve var_ready std_ready normed xT_ps xT proj v_ps v_sb rot_dve rot_pool "
                                  "turned_ps turned scored shifted_scores exps inverse probs pT_ps pT_d pT_a pv oT wo "
                                  "x_new var2 std2")
        CH = QW // 2
        xn = sb("xn", [P, NT, D])
        xT = sb("xT", [P, NT, P])
        r1, r2 = sb("r1", [P, 2, CH]), sb("r2", [P, 2, CH])
        qk = sb("qk", [P, 2, CH])
        qT = sb("qT", [P, 2, SLOTS, P])
        kT = sb("kT", [P, NB, HKV // 2, T])
        v = sb("v", [P, NT, HKV, DH])
        sc = sb("sc", [P, 2, 2, T])
        neg_max = sb("neg_max", [P, NT * SLOTS, 2])
        ex = sb("ex", [P, 2, 2, T])
        total, inv = sb("total", [P, NT * SLOTS, 2]), sb("inv", [P, NT * SLOTS, 2])
        pr = sb("pr", [P, 3, 2, T])
        pT = sb("pT", [P, 2, 2, TPB, BLK, P])
        oT = sb("oT", [P, SLOTS, P])
        bank = [ctx.enter_context(nc.psum_tensor(f"a_bank{i}", [P, 512], F32)) for i in range(8)]
        NU = NT * SLOTS
        NJOBS = 2 + 2 * NT
        STEPS = NU + 9
        slot_head = lambda j, e: 8 * (j // BLK) + 4 * e + j % BLK
        proj_bank = lambda n: bank[(0, 1, 4, 5)[n]] if n < 4 else bank[7]
        turn_bank = lambda n: bank[6 + n % 2] if n < 4 else bank[7]
        PROJECT_AT, TURN_AT = {1: 0, 3: 1}, {4: 0, 6: 1}

        def job_at(i, when):
            t, at = divmod(i, SLOTS)
            return 2 + 2 * (t + 1) + when[at] if t + 1 < NT and at in when else None

        with nc.Block() as block:
            @block.sync
            def _(sp):
                src = a["L0_attn_a_x"].rearrange("(g b) (c p) d -> p g (b c) d", b=NB, p=P)
                sp.dma_start(w.x[:], src[:, bass.ds(pair, 1), :, :]).then_inc(s["x_loaded"], 16)

            @block.tensor
            def _(pe):
                pe.wait_ge(s["normed"], NT)
                for t in range(NT):
                    pe.transpose(bank[6][:, t * P:(t + 1) * P], xn[:, t, :], w.ident[:]).then_inc(s["xT_ps"], 1)

                def project_keys(n):
                    for i in range(TPB):
                        ins = pe.matmul(proj_bank(n)[:, i * KW:(i + 1) * KW], xT[:, n * TPB + i, :],
                                        w.wqkv_a[:, QW:QW + KW], start=True, stop=True)
                    ins.then_inc(s["proj"], 1)

                def project_values(b):
                    for i in range(TPB):
                        ins = pe.matmul(bank[2 + b][:, i * KW:(i + 1) * KW], xT[:, b * TPB + i, :],
                                        w.wqkv_a[:, QW + KW:], start=True, stop=True)
                    ins.then_inc(s["v_ps"], 1)

                def project(n):
                    t, c = divmod(n - 2, 2)
                    if t >= 1 and c == 0:
                        pe.wait_ge(s["turned"], n)
                    if t >= 3 and c == 0:
                        pe.wait_ge(s["x_new"], t - 2)
                    if t >= 1 and c == 1:
                        pe.wait_ge(s["rot_dve"], n)
                    pe.matmul(proj_bank(n)[:], xT[:, t, :], w.wqkv_a[:, CH * c:CH * (c + 1)],
                              start=True, stop=True).then_inc(s["proj"], 1)

                def turn(n):
                    t, c = divmod(n - 2, 2)
                    pe.wait_ge(s["rot_pool"], n + 1)
                    if n < 4:
                        pe.wait_ge(s["xT"], 1)
                        if n >= 2:
                            pe.wait_ge(s["turned"], n - 1)
                    elif c == 0:
                        pe.wait_ge(s["rot_dve"], n + 2)
                    else:
                        pe.wait_ge(s["turned"], n)
                    for i in range(CH // P):
                        ins = pe.transpose(turn_bank(n)[:, i * P:(i + 1) * P], qk[:, n % 2, i * P:(i + 1) * P], w.ident[:])
                    ins.then_inc(s["turned_ps"], 1)

                def scores(u):
                    t, j = divmod(u, SLOTS)
                    b = t // TPB
                    if u == 0:
                        pe.wait_ge(s["rot_dve"], 4)
                        pe.wait_ge(s["v_sb"], NB)
                    if j % BLK == 0:
                        pe.wait_ge(s["turned"], 2 + 2 * t + j // BLK + 1)
                    for e in range(2):
                        r = 2 * u + e
                        if r >= 3:
                            pe.wait_ge(s["shifted_scores"], r - 2)
                        rows = slice(64 * e, 64 * e + 64)
                        pe.matmul(bank[r % 3][:, 0:T], qT[rows, t % 2, j, :], kT[rows, b, j // BLK, :],
                                  start=True, stop=True).then_inc(s["scored"], 1)

                def turn_probs(u):
                    pe.wait_ge(s["probs"], u + 1)
                    if u >= 2:
                        pe.wait_ge(s["pT_d"] if u % 2 == 0 else s["pT_a"], u // 2)
                    for e in range(2):
                        for k in range(TPB):
                            ins = pe.transpose(bank[3 + u % 2][:, (2 * e + k) * P:(2 * e + k + 1) * P],
                                               pr[:, u % 3, e, k * P:(k + 1) * P], w.ident[:])
                    ins.then_inc(s["pT_ps"], 1)

                def weigh_values(g, m):
                    e, k = divmod(m, TPB)
                    t, blk = divmod(g, SLOTS // BLK)
                    if m == 0:
                        pe.wait_ge(s["pT_d"], 2 * (g + 1))
                        pe.wait_ge(s["pT_a"], 2 * (g + 1))
                        if g == 1:
                            pe.wait_ge(s["turned"], 4)
                        if g >= 2:
                            pe.wait_ge(s["oT"], g - 1)
                    ins = pe.matmul(bank[5 + g % 2][64 * e:64 * e + 64, :], v[:, t // TPB * TPB + k, 2 * blk + e, :],
                                    pT[:, g % 2, e, k].rearrange("p r q -> p (r q)"), start=(k == 0), stop=(k == TPB - 1))
                    if m == 2 * TPB - 1:
                        ins.then_inc(s["pv"], 1)

                def project_out(t):
                    pe.wait_ge(s["oT"], 2 * (t + 1))
                    pe.wait_ge(s["turned"], min(NJOBS, 2 * (t + 4)))
                    if t >= 1:
                        pe.wait_ge(s["x_new"], t)
                    for j in range(SLOTS):
                        ins = pe.matmul(bank[7][:, 0:D], oT[:, j, :], w.wo_a[:, j, :],
                                        start=(j == 0), stop=(j == SLOTS - 1))
                    ins.then_inc(s["wo"], 1)

                pe.wait_ge(s["xT"], 1)
                project_keys(0)
                project_keys(1)
                project(2)
                project(3)
                project_values(0)
                project_values(1)
                for n in range(4):
                    turn(n)
                for i in range(STEPS):
                    if i < NU:
                        scores(i)
                    if i >= 7 and (i - 7) // 4 < NU // BLK:
                        weigh_values((i - 7) // 4, (i - 7) % 4)
                    if 3 <= i < NU + 3:
                        turn_probs(i - 3)
                    if i >= 16 and i % SLOTS == 0:
                        project_out(i // SLOTS - 2)
                    if job_at(i, PROJECT_AT) is not None:
                        project(job_at(i, PROJECT_AT))
                    if job_at(i, TURN_AT) is not None:
                        turn(job_at(i, TURN_AT))

            @block.scalar
            def _(act):
                act.wait_ge(s["var_ready"], NT)
                nc.scalar.activation(w.std[:], w.mean_var[:, :, 1], ACT.Sqrt, bias=w.eps_t[:, 0:1]).then_inc(s["std_ready"], 1)
                act.wait_ge(s["xT_ps"], NT)
                nc.scalar.copy(xT[:].rearrange("p t k -> p (t k)"), bank[6][:]).then_inc(s["xT"], 1)

                def values(b):
                    act.wait_ge(s["v_ps"], b + 1)
                    nc.scalar.copy(v[:, b * TPB:(b + 1) * TPB].rearrange("p t h d -> p (t h d)"),
                                   bank[2 + b][:]).then_inc(s["v_sb"], 1)

                def turned(n):
                    t, c = divmod(n - 2, 2)
                    act.wait_ge(s["turned_ps"], n + 1)
                    if n < 2:
                        nc.scalar.copy(kT[:, n].rearrange("p g (t k) -> p t g k", t=TPB),
                                       turn_bank(n)[:].rearrange("p (t g k) -> p t g k", t=TPB, g=2)).then_inc(s["turned"], 1)
                        return
                    if t >= 2:
                        act.wait_ge(s["scored"], 2 * SLOTS * (t - 1))
                    nc.scalar.copy(qT[:, t % 2, BLK * c:BLK * (c + 1), :].rearrange("p j k -> p (j k)"),
                                   turn_bank(n)[:]).then_inc(s["turned"], 1)

                values(0)
                values(1)
                for n in range(4):
                    turned(n)

                def exps(u):
                    if u >= 2:
                        act.wait_ge(s["probs"], u - 1)
                    for e in range(2):
                        act.wait_ge(s["shifted_scores"], 2 * u + e + 1)
                        nc.scalar.activation(ex[:, u % 2, e, :], sc[:, u % 2, e, :], ACT.Exp, bias=neg_max[:, u, e:e + 1],
                                             scale=-1.0, accum_out=total[:, u, e:e + 1]).then_inc(s["exps"], 1)

                def turned_probs(u):
                    act.wait_ge(s["pT_ps"], u + 1)
                    if u // BLK >= 2:
                        act.wait_ge(s["pv"], u // BLK - 1)
                    nc.scalar.copy(pT[:, u // BLK % 2, :, :, u % BLK, :],
                                   bank[3 + u % 2][:].rearrange("p (e k q) -> p e k q", e=2, k=TPB)).then_inc(s["pT_a"], 1)

                def turned_out(g):
                    t, blk = divmod(g, SLOTS // BLK)
                    act.wait_ge(s["pv"], g + 1)
                    if t >= 1:
                        act.wait_ge(s["wo"], t)
                    nc.scalar.copy(oT[:, BLK * blk:BLK * (blk + 1), :].rearrange("p j k -> p (j k)"),
                                   bank[5 + g % 2][:]).then_inc(s["oT"], 1)

                for i in range(STEPS):
                    if i >= 11 and (i - 11) % BLK == 0:
                        turned_out((i - 11) // BLK)
                    if i < NU:
                        exps(i)
                    if 3 <= i < NU + 3 and (i - 3) % 2 == 1:
                        turned_probs(i - 3)
                    if job_at(i, TURN_AT) is not None:
                        turned(job_at(i, TURN_AT))
                act.wait_ge(s["var2"], NT)
                nc.scalar.activation(w.std[:], w.mean_var[:, :, 1], ACT.Sqrt, bias=w.eps_t[:, 0:1]).then_inc(s["std2"], 1)

            @block.vector
            def _(dve):
                st = Steps(dve, s["dve"])
                dve.wait_ge(s["x_loaded"], 16)
                layer_norm_stats(nc, dve, st, w, range(NT), w.x, s, s["var_ready"])
                dve.wait_ge(s["std_ready"], 1)
                k = st.did(nc.vector.reciprocal(w.rstd[:], w.std[:]))
                st.wait(k)
                for t in range(NT):
                    nc.vector.tensor_scalar(xn[:, t, :], w.x[:, t, :], w.mean_var[:, t, 0:1], w.rstd[:, t:t + 1],
                                            ALU.subtract, ALU.mult).then_inc(s["normed"], 1)

                def rotate(n):
                    dve.wait_ge(s["proj"], n + 1)
                    if n >= 2:
                        dve.wait_ge(s["rot_pool"], n - 1)
                    parts = [(i, KW * i, HKV) for i in range(TPB)] if n < 2 else [((n - 2) // 2 % TPB, 0, CH // DH)]
                    for at, lo, heads in parts:
                        hi = lo + heads * DH
                        src = proj_bank(n)[:, lo:hi].rearrange("p (h d) -> p h d", h=heads)
                        swapped = proj_bank(n)[:, lo:hi].rearrange("p (h s d) -> p h s d", h=heads, s=2)[:, :, ::-1, :]
                        cos = w.rope_a[:, at, 0, :].unsqueeze(1).broadcast_to((P, heads, DH))
                        sin = w.rope_a[:, at, 1, :].rearrange("p (s d) -> p s d", s=2).unsqueeze(1)\
                            .broadcast_to((P, heads, 2, DH // 2))
                        st.did(nc.vector.tensor_tensor(
                            r1[:, n % 2, lo:hi].rearrange("p (h d) -> p h d", h=heads), src, cos, ALU.mult))
                        ins = nc.vector.tensor_tensor(
                            r2[:, n % 2, lo:hi].rearrange("p (h s d) -> p h s d", h=heads, s=2), swapped, sin, ALU.mult)
                        if hi < CH:
                            st.did(ins)
                    ins.then_inc(s["rot_dve"], 1)

                for n in range(4):
                    rotate(n)

                def shift_scores(u):
                    t, j = divmod(u, SLOTS)
                    if u >= 2:
                        dve.wait_ge(s["exps"], 2 * (u - 1))
                    for e in range(2):
                        dve.wait_ge(s["scored"], 2 * u + e + 1)
                        nc.vector.tensor_tensor_reduce(
                            out=sc[:, u % 2, e, :], in0=bank[(2 * u + e) % 3][:, 0:T],
                            in1=w.bias_a[:, t % TPB, slot_head(j, e), :], scale=-1.0 / 8.0, scalar=3e38,
                            op0=ALU.add, op1=ALU.min, accum_out=neg_max[:, u, e:e + 1]).then_inc(s["shifted_scores"], 1)

                def turned_probs(u):
                    dve.wait_ge(s["pT_ps"], u + 1)
                    if u // BLK >= 2:
                        dve.wait_ge(s["pv"], u // BLK - 1)
                    nc.vector.tensor_copy(pT[:, u // BLK % 2, :, :, u % BLK, :],
                                          bank[3 + u % 2][:].rearrange("p (e k q) -> p e k q", e=2, k=TPB)).then_inc(s["pT_d"], 1)

                def residual(t):
                    dve.wait_ge(s["wo"], t + 1)
                    nc.vector.tensor_tensor(w.x[:, t, :], w.x[:, t, :], bank[7][:, 0:D], ALU.add).then_inc(s["x_new"], 1)

                for i in range(STEPS):
                    if i < NU:
                        shift_scores(i)
                    if 1 <= i <= NU:
                        dve.wait_ge(s["exps"], 2 * i)
                        nc.vector.reciprocal(inv[:, i - 1, :], total[:, i - 1, :]).then_inc(s["inverse"], 1)
                    if 3 <= i < NU + 3 and (i - 3) % 2 == 0:
                        turned_probs(i - 3)
                    if i >= 16 and i % SLOTS == 0:
                        residual(i // SLOTS - 2)
                    if job_at(i, PROJECT_AT) is not None:
                        rotate(job_at(i, PROJECT_AT))
                dve.wait_ge(s["x_new"], NT)
                layer_norm_stats(nc, dve, st, w, range(NT), w.x, s, s["var2"])
                dve.wait_ge(s["std2"], 1)
                k = st.did(nc.vector.reciprocal(w.rstd[:], w.std[:]))
                st.wait(k)
                for t in range(NT):
                    st.did(nc.vector.tensor_scalar(w.y[:, t, :], w.x[:, t, :], w.mean_var[:, t, 0:1], w.rstd[:, t:t + 1],
                                                   ALU.subtract, ALU.mult))

            @block.gpsimd
            def _(pool):
                def rotated(n):
                    pool.wait_ge(s["rot_dve"], n + 1)
                    if n >= 2:
                        pool.wait_ge(s["turned_ps"], n - 1)
                    dst, one, two = qk[:, n % 2, :], r1[:, n % 2, :], r2[:, n % 2, :]
                    if n >= 2:
                        dst = dst.rearrange("p (r e d) -> p r e d", r=BLK, e=2)
                        one, two = (z.rearrange("p (e r d) -> p r e d", r=BLK, e=2) for z in (one, two))
                    nc.gpsimd.tensor_tensor(dst, one, two, ALU.add).then_inc(s["rot_pool"], 1)

                def normalise(u):
                    pool.wait_ge(s["inverse"], u + 1)
                    if u >= 3:
                        pool.wait_ge(s["pT_ps"], u - 2)
                    nc.gpsimd.tensor_tensor(pr[:, u % 3], ex[:, u % 2], inv[:, u, :].unsqueeze(2).broadcast_to((P, 2, T)),
                                            ALU.mult).then_inc(s["probs"], 1)

                for n in range(4):
                    rotated(n)
                for i in range(NU):
                    if i >= 1:
                        normalise(i - 1)
                    if job_at(i, PROJECT_AT) is not None:
                        rotated(job_at(i, PROJECT_AT))
                normalise(NU - 1)
        clear(nc, s)


def local_layer(nc, w, layer, name):
    with ExitStack() as ctx:
        def sb(n, shape):
            return ctx.enter_context(nc.sbuf_tensor(f"{name}_{n}", shape, F32))

        s = signals(nc, ctx, name, "dve pool yT_ps hT_a hT_d edge_zero qk_proj v_proj squared summed norm rn rot_dve "
                                   "rot_pool qT_ps kT_ps qT kT v_sb ones scored shifted_scores probs pT_ps pT pv o_sb "
                                   "oT_ps oT wo y_attn shifted var_ready std_ready normed nT_ps hnT w1 gated_in "
                                   "gelu gated gT_ps gT w2 y_new y_bias pad")
        hT = sb("hT", [P, NB, T])
        sq = sb("sq", [P, 2, 2, INNER])
        ss, norm, rn = sb("ss", [P, NT, 2, HL]), sb("norm", [P, NT, 2, HL]), sb("rn", [P, NT, 2, HL])
        r1, r2 = sb("r1", [P, 2, 2, INNER]), sb("r2", [P, 2, 2, INNER])
        qk = sb("qk", [P, 2, 2, INNER])
        kr = sb("kr", [P, 2, INNER])
        qT = sb("qT", [P, NT, PAIRH, P])
        kT = sb("kT", [P, NB, PAIRH, T])
        v = sb("v", [P, NB, VSETS, HL, DH + 1])
        NU = NT * 2
        sc, pr, pT = sb("sc", [P, 2, 4, P]), sb("pr", [P, 2, 4, P]), sb("pT", [P, 2, 4, P])
        neg_max, rsum = sb("neg_max", [P, NU, 4]), sb("rsum", [P, NU, 4])
        o = sb("o", [P, NT, INNER])
        oT = sb("oT", [P, 2, PAIRH, P])
        old1, old2 = (z[:].rearrange("p a b c -> p (a b c)") for z in (r1, r2))
        gin, ain, gel = (old1[:, 2 * HID * i:2 * HID * (i + 1)].rearrange("p (a b) -> p a b", a=2) for i in range(3))
        n = old2[:, 0:NT * D].rearrange("p (t d) -> p t d", t=NT)
        hnT = old2[:, NT * D:2 * NT * D].rearrange("p (t d) -> p t d", t=NT)
        gT = old2[:, 2 * NT * D:2 * NT * D + 2 * HIDT * P].rearrange("p (a k q) -> p a k q", a=2, k=HIDT)
        gated = sb("gated", [P, 2, HIDT * P])
        yb = sb("yb", [P, NT, D])
        lgb = sb("lgb", [P, 2, 1])
        lg, lb = lgb[:, 0, :], lgb[:, 1, :]
        tab = sb("tab", [P, 2, TPB, 2, DH])
        b1 = sb("b1", [P, 2 * HID])
        bank = [ctx.enter_context(nc.psum_tensor(f"{name}_bank{i}", [P, 512], F32)) for i in range(8)]

        with nc.Block() as block:
            @block.tensor
            def _(pe):
                for b in range(NB):
                    for i in range(TPB):
                        ins = pe.transpose(bank[6 + b][:, i * P:(i + 1) * P], w.y[:, b * TPB + i, :], w.ident[:])
                    ins.then_inc(s["yT_ps"], 1)

                def project(t):
                    b, i = divmod(t, TPB)
                    if i == 0:
                        pe.wait_ge(s["hT_a"], b + 1)
                        pe.wait_ge(s["hT_d"], b + 1)
                        pe.wait_ge(s["edge_zero"], 1)
                    if t >= 2:
                        pe.wait_ge(s["rot_dve"], 2 * (t - 1))
                        pe.wait_ge(s["squared"], 2 * (t - 1))
                    for c in range(2):
                        pe.matmul(bank[2 * (t % 2) + c][:], hT[:, b, i * P:(i + 1) * P],
                                  w.wqkv_l[:, bass.ds(layer, 1), INNER * c:INNER * (c + 1)],
                                  start=True, stop=True).then_inc(s["qk_proj"], 1)

                def project_values(r):
                    b, i = divmod(r, VSETS)
                    if r >= 2:
                        pe.wait_ge(s["v_sb"], r - 1)
                    pe.matmul(bank[4 + r % 2][:], hT[:, b, i * WIN:i * WIN + P],
                              w.wqkv_l[:, bass.ds(layer, 1), 2 * INNER:3 * INNER],
                              start=True, stop=True).then_inc(s["v_proj"], 1)

                def turn(t):
                    if t == 0:
                        pe.wait_ge(s["hT_a"], NB)
                        pe.wait_ge(s["hT_d"], NB)
                    for c, ready, copied, ps in ((0, s["rot_pool"], s["qT"], s["qT_ps"]), (1, s["rot_pool"], s["kT"], s["kT_ps"])):
                        pe.wait_ge(ready, 2 * t + c + 1)
                        if t >= 1:
                            pe.wait_ge(copied, t)
                        for i in range(PAIRH):
                            ins = pe.transpose(bank[6 + c][:, i * P:(i + 1) * P],
                                               qk[:, t % 2, c, i * P:(i + 1) * P], w.ident[:])
                        ins.then_inc(ps, 1)

                def scores(u):
                    t, e = divmod(u, 2)
                    b, i = divmod(t, TPB)
                    if u == 0:
                        pe.wait_ge(s["rot_dve"], 2 * (NT - 1))
                        pe.wait_ge(s["squared"], 2 * (NT - 1))
                    if u >= 2:
                        pe.wait_ge(s["shifted_scores"], 4 * (u - 1))
                    pe.wait_ge(s["qT"], t + 1)
                    pe.wait_ge(s["kT"], t + 1)
                    for c in range(4):
                        h = 2 * c + e
                        rows = slice(64 * e, 64 * e + 64)
                        for half in range(2):
                            k0 = first_key(i, half)
                            ins = pe.matmul(bank[u % 2][64 * half:64 * half + 64, c * P:(c + 1) * P],
                                            qT[rows, t, h // 2, 64 * half:64 * half + 64],
                                            kT[rows, b, h // 2, k0:k0 + P], start=True, stop=True)
                    ins.then_inc(s["scored"], 1)

                def turn_probs(u):
                    if u == 0:
                        pe.wait_ge(s["rot_dve"], 2 * NT)
                        pe.wait_ge(s["squared"], 2 * NT)
                    pe.wait_ge(s["probs"], 4 * (u + 1))
                    if u >= 2:
                        pe.wait_ge(s["pT"], u - 1)
                    for c in range(4):
                        ins = pe.transpose(bank[2 + u % 2][:, c * P:(c + 1) * P], pr[:, u % 2, c, :], w.ident[:])
                    ins.then_inc(s["pT_ps"], 1)

                def weigh_values(u):
                    t, e = divmod(u, 2)
                    b, i = divmod(t, TPB)
                    if u == 0:
                        pe.wait_ge(s["v_sb"], NB * VSETS)
                        pe.wait_ge(s["ones"], 1)
                    pe.wait_ge(s["pT"], u + 1)
                    if u >= 2:
                        pe.wait_ge(s["o_sb"], u - 1)
                    for c in range(4):
                        h = 2 * c + e
                        for half in range(2):
                            ins = pe.matmul(bank[4 + u % 2][64 * half:64 * half + 64, c * (DH + 1):(c + 1) * (DH + 1)],
                                            pT[:, u % 2, c, 64 * half:64 * half + 64],
                                            v[:, b, first_key(i, half) // WIN, h, :], start=True, stop=True)
                    ins.then_inc(s["pv"], 1)

                def turn_out(t):
                    pe.wait_ge(s["o_sb"], 2 * t + 2)
                    if t == 0:
                        pe.wait_ge(s["qT"], NT)
                        pe.wait_ge(s["kT"], NT)
                    if t >= 1:
                        pe.wait_ge(s["oT"], t)
                    for i in range(PAIRH):
                        ins = pe.transpose(bank[6][:, i * P:(i + 1) * P], o[:, t, i * P:(i + 1) * P], w.ident[:])
                    ins.then_inc(s["oT_ps"], 1)

                def project_out(t):
                    pe.wait_ge(s["oT"], t + 1)
                    if t >= 1:
                        pe.wait_ge(s["y_attn"], t)
                    for i in range(PAIRH):
                        ins = pe.matmul(bank[7][:, 0:D], oT[:, t % 2, i, :], w.wo_l[:, bass.ds(layer, 1), i, :],
                                        start=(i == 0), stop=(i == PAIRH - 1))
                    ins.then_inc(s["wo"], 1)

                project(0)
                project(1)
                for r in range(3):
                    project_values(r)
                turn(0)
                project(2)
                turn(1)
                project(3)
                for r in range(3, 6):
                    project_values(r)
                turn(2)
                for i in range(NU + 4):
                    if i == 3:
                        turn(3)
                    if i < NU:
                        scores(i)
                    if 1 <= i <= NU:
                        turn_probs(i - 1)
                    if 2 <= i <= NU + 1:
                        weigh_values(i - 2)
                    if i >= 4 and i % 2 == 0:
                        turn_out((i - 4) // 2)
                    if i >= 5 and i % 2 == 1:
                        project_out((i - 5) // 2)

                def shift(b):
                    t = b * TPB
                    pe.wait_ge(s["y_attn"], t + 2)
                    if b == 0:
                        pe.wait_ge(s["shifted_scores"], 4 * NU)
                    dst = bank[b][:, 0:TPB * HALF].rearrange("p (i d) -> p i d", i=TPB)
                    pe.matmul(dst, w.shift_m[:], w.y[:, t:t + TPB, HALF:D], start=True, stop=False)
                    pe.matmul(dst[:, 1], w.edge_m[:], w.y[:, t, HALF:D], start=False, stop=True).then_inc(s["shifted"], 1)

                def turn_normed(b):
                    pe.wait_ge(s["normed"], 4 * (b + 1))
                    if b == 0:
                        pe.wait_ge(s["oT"], NT)
                    if b == 1:
                        pe.wait_ge(s["y_attn"], NT)
                    for i in range(TPB):
                        ins = pe.transpose(bank[6 + b][:, i * P:(i + 1) * P], n[:, b * TPB + i, :], w.ident[:])
                    ins.then_inc(s["nT_ps"], 1)

                def widen(t):
                    pe.wait_ge(s["hnT"], t // TPB + 1)
                    if t == 0:
                        pe.wait_ge(s["pT"], NU)
                        pe.wait_ge(s["o_sb"], NU)
                    if t >= 2:
                        pe.wait_ge(s["gated_in"], 2 * (t - 1))
                    for c in (1, 0):
                        pe.matmul(bank[2 + 2 * (t % 2) + c][:, 0:HID], hnT[:, t, :],
                                  w.w1_l[:, bass.ds(layer, 1), HID * c:HID * (c + 1)],
                                  start=True, stop=True).then_inc(s["w1"], 1)

                def turn_gated(t):
                    pe.wait_ge(s["gated"], t + 1)
                    if t == 0:
                        pe.wait_ge(s["pad"], 2)
                        pe.wait_ge(s["normed"], 4 * NB)
                    if t >= 2:
                        pe.wait_ge(s["gT"], t - 1)
                    for i in range(HIDT):
                        ins = pe.transpose(bank[t % 2][:, i * P:(i + 1) * P], gated[:, t % 2, i * P:(i + 1) * P], w.ident[:])
                    ins.then_inc(s["gT_ps"], 1)

                def narrow(t):
                    pe.wait_ge(s["gT"], t + 1)
                    if t == 0:
                        pe.wait_ge(s["hnT"], NB)
                    if t >= 1:
                        pe.wait_ge(s["y_new"], t)
                    for i in range(HIDT):
                        ins = pe.matmul(bank[7][:, 0:D], gT[:, t % 2, i, :], w.w2_l[:, bass.ds(layer, 1), i, :],
                                        start=(i == 0), stop=(i == HIDT - 1))
                    ins.then_inc(s["w2"], 1)

                shift(0)
                shift(1)
                turn_normed(0)
                widen(0)
                turn_normed(1)
                widen(1)
                turn_gated(0)
                widen(2)
                narrow(0)
                turn_gated(1)
                widen(3)
                narrow(1)
                turn_gated(2)
                narrow(2)
                turn_gated(3)
                narrow(3)

            @block.scalar
            def _(act):
                for b in range(NB):
                    act.wait_ge(s["yT_ps"], b + 1)
                    nc.scalar.copy(hT[0:HALF, b, :], bank[6 + b][0:HALF, 0:T]).then_inc(s["hT_a"], 1)

                def squares(t):
                    if t >= 2:
                        act.wait_ge(s["summed"], 2 * (t - 1))
                    for c in range(2):
                        act.wait_ge(s["qk_proj"], 2 * t + c + 1)
                        nc.scalar.activation(sq[:, t % 2, c, :], bank[2 * (t % 2) + c][:], ACT.Square).then_inc(s["squared"], 1)

                def root(t):
                    act.wait_ge(s["summed"], 2 * (t + 1))
                    nc.scalar.activation(norm[:, t], ss[:, t], ACT.Sqrt).then_inc(s["norm"], 1)

                def values(r):
                    b, i = divmod(r, VSETS)
                    act.wait_ge(s["v_proj"], r + 1)
                    nc.scalar.copy(v[:, b, i, :, 0:DH], bank[4 + r % 2][:].rearrange("p (h d) -> p h d", h=HL)
                                   ).then_inc(s["v_sb"], 1)

                def turned(t):
                    b, i = divmod(t, TPB)
                    act.wait_ge(s["qT_ps"], t + 1)
                    nc.scalar.copy(qT[:, t].rearrange("p j k -> p (j k)"), bank[6][:]).then_inc(s["qT"], 1)
                    act.wait_ge(s["kT_ps"], t + 1)
                    nc.scalar.copy(kT[:, b, :, i * P:(i + 1) * P], bank[7][:].rearrange("p (j k) -> p j k", j=PAIRH)
                                   ).then_inc(s["kT"], 1)

                def exps(u):
                    if u >= 2:
                        act.wait_ge(s["pT_ps"], u - 1)
                    for c in range(4):
                        act.wait_ge(s["shifted_scores"], 4 * u + c + 1)
                        nc.scalar.activation(pr[:, u % 2, c, :], sc[:, u % 2, c, :], ACT.Exp,
                                             bias=neg_max[:, u, c:c + 1], scale=-1.0).then_inc(s["probs"], 1)

                def turned_out(t):
                    act.wait_ge(s["oT_ps"], t + 1)
                    if t >= 2:
                        act.wait_ge(s["wo"], t - 1)
                    nc.scalar.copy(oT[:, t % 2].rearrange("p j k -> p (j k)"), bank[6][:]).then_inc(s["oT"], 1)

                squares(0)
                squares(1)
                root(0)
                values(0)
                values(1)
                root(1)
                values(2)
                turned(0)
                squares(2)
                root(2)
                turned(1)
                squares(3)
                values(3)
                root(3)
                values(4)
                values(5)
                turned(2)
                for i in range(NU + 4):
                    if i == 3:
                        turned(3)
                    if i < NU:
                        exps(i)
                    if i >= 4 and i % 2 == 0:
                        turned_out((i - 4) // 2)

                for b in range(NB):
                    act.wait_ge(s["var_ready"], TPB * (b + 1))
                    ts = slice(b * TPB, (b + 1) * TPB)
                    nc.scalar.activation(w.std[:, ts], w.mean_var[:, ts, 1], ACT.Sqrt,
                                         bias=w.eps_t[:, 0:1]).then_inc(s["std_ready"], 1)

                def affine(b):
                    act.wait_ge(s["nT_ps"], b + 1)
                    nc.scalar.activation(hnT[:, b * TPB:(b + 1) * TPB, :].rearrange("p t k -> p (t k)"),
                                         bank[6 + b][:, 0:T], ACT.Identity, bias=lb[:, 0:1],
                                         scale=lg[:, 0:1]).then_inc(s["hnT"], 1)

                def gelu(t):
                    act.wait_ge(s["gated_in"], 2 * t + 1)
                    if t >= 2:
                        act.wait_ge(s["gated"], t - 1)
                    nc.scalar.activation(gel[:, t % 2, :], gin[:, t % 2, :], ACT.Gelu).then_inc(s["gelu"], 1)

                def turned_gated(t):
                    act.wait_ge(s["gT_ps"], t + 1)
                    if t >= 2:
                        act.wait_ge(s["w2"], t - 1)
                    nc.scalar.copy(gT[:, t % 2].rearrange("p j k -> p (j k)"), bank[t % 2][:, 0:HIDT * P]).then_inc(s["gT"], 1)

                act.wait_ge(s["pad"], 2)
                affine(0)
                affine(1)
                gelu(0)
                gelu(1)
                turned_gated(0)
                gelu(2)
                turned_gated(1)
                gelu(3)
                turned_gated(2)
                turned_gated(3)

            @block.vector
            def _(dve):
                st = Steps(dve, s["dve"])
                k0 = st.did(nc.vector.tensor_copy(tab[:].rearrange("p i t c d -> p (i t c d)"),
                                                  w.rot_l[:, bass.ds(layer, 1)].rearrange("p l i t c d -> p (l i t c d)")))
                for b in range(NB):
                    dve.wait_ge(s["yT_ps"], b + 1)
                    nc.vector.tensor_copy(hT[HALF:P, b, 1:T], bank[6 + b][HALF:P, 0:T - 1]).then_inc(s["hT_d"], 1)
                st.wait(k0)

                def rotate(t):
                    i = t % TPB
                    if t >= 2:
                        dve.wait_ge(s["rot_pool"], 2 * (t - 1))
                    for c in range(2):
                        dve.wait_ge(s["squared"], 2 * t + c + 1)
                        nc.vector.tensor_reduce(ss[:, t, c, :], sq[:, t % 2, c, :].rearrange("p (h d) -> p h d", h=HL),
                                                AX.X, ALU.add).then_inc(s["summed"], 1)
                    for c in range(2):
                        ps = bank[2 * (t % 2) + c][:]
                        st.did(nc.vector.tensor_tensor(
                            r1[:, t % 2, c, :].rearrange("p (h d) -> p h d", h=HL), ps.rearrange("p (h d) -> p h d", h=HL),
                            tab[:, c, i, 0, :].unsqueeze(1).broadcast_to((P, HL, DH)), ALU.mult))
                        nc.vector.tensor_tensor(
                            r2[:, t % 2, c, :].rearrange("p (h s d) -> p h s d", h=HL, s=2),
                            ps.rearrange("p (h s d) -> p h s d", h=HL, s=2)[:, :, ::-1, :],
                            tab[:, c, i, 1, :].rearrange("p (s d) -> p s d", s=2).unsqueeze(1)
                            .broadcast_to((P, HL, 2, DH // 2)), ALU.mult).then_inc(s["rot_dve"], 1)
                        if c == 0:
                            dve.wait_ge(s["norm"], t + 1)
                            k = st.did(nc.vector.tensor_scalar(norm[:, t], norm[:, t], 1e-12, None, ALU.max))
                            st.wait(k)
                            nc.vector.reciprocal(rn[:, t], norm[:, t]).then_inc(s["rn"], 1)

                for t in range(NT):
                    rotate(t)

                def shift_scores(u):
                    t, e = divmod(u, 2)
                    if u == 0:
                        dve.wait_ge(s["rn"], NT)
                    if u >= 2:
                        dve.wait_ge(s["probs"], 4 * (u - 1))
                    dve.wait_ge(s["scored"], u + 1)
                    for c in range(4):
                        nc.vector.tensor_tensor_reduce(
                            out=sc[:, u % 2, c, :], in0=bank[u % 2][:, c * P:(c + 1) * P], in1=w.mask_l[:, t % TPB, :],
                            scale=rn[:, t, 0, 2 * c + e:2 * c + e + 1], scalar=3e38, op0=ALU.add, op1=ALU.min,
                            accum_out=neg_max[:, u, c:c + 1]).then_inc(s["shifted_scores"], 1)

                def turned_probs(u):
                    dve.wait_ge(s["pT_ps"], u + 1)
                    if u >= 2:
                        dve.wait_ge(s["pv"], u - 1)
                    nc.vector.tensor_copy(pT[:, u % 2].rearrange("p c q -> p (c q)"), bank[2 + u % 2][:]).then_inc(s["pT"], 1)

                def normalise(u):
                    t, e = divmod(u, 2)
                    dve.wait_ge(s["pv"], u + 1)
                    src = bank[4 + u % 2][:, 0:4 * (DH + 1)].rearrange("p (c d) -> p c d", c=4)
                    k = st.did(nc.vector.reciprocal(rsum[:, u, :], src[:, :, DH]))
                    st.wait(k)
                    nc.vector.tensor_tensor(
                        o[:, t, :].rearrange("p (c e d) -> p c e d", c=4, e=2)[:, :, e, :], src[:, :, 0:DH],
                        rsum[:, u, :].unsqueeze(2).broadcast_to((P, 4, DH)), ALU.mult).then_inc(s["o_sb"], 1)

                def residual(t):
                    dve.wait_ge(s["wo"], t + 1)
                    nc.vector.tensor_tensor(w.y[:, t, :], w.y[:, t, :], bank[7][:, 0:D], ALU.add).then_inc(s["y_attn"], 1)

                for i in range(NU + 4):
                    if i < NU:
                        shift_scores(i)
                    if 1 <= i <= NU:
                        turned_probs(i - 1)
                    if 2 <= i <= NU + 1:
                        normalise(i - 2)
                    if i >= 5 and i % 2 == 1:
                        residual((i - 5) // 2)

                def statistics(b):
                    dve.wait_ge(s["y_attn"], TPB * (b + 1))
                    for i in range(TPB):
                        t = b * TPB + i
                        st.did(nc.vector.bn_stats(w.stats[:, t, 0, :], w.y[:, t, 0:HALF]))
                    dve.wait_ge(s["shifted"], b + 1)
                    for i in range(TPB):
                        t = b * TPB + i
                        k = st.did(nc.vector.bn_stats(w.stats[:, t, 1, :], bank[b][:, i * HALF:(i + 1) * HALF]))
                    st.wait(k)
                    for i in range(TPB):
                        t = b * TPB + i
                        nc.vector.bn_aggr(w.mean_var[:, t, :], w.stats[:, t].rearrange("p a b -> p (a b)")
                                          ).then_inc(s["var_ready"], 1)

                def normed(b):
                    ts = slice(b * TPB, (b + 1) * TPB)
                    dve.wait_ge(s["std_ready"], b + 1)
                    k = st.did(nc.vector.reciprocal(w.rstd[:, ts], w.std[:, ts]))
                    st.wait(k)
                    for i in range(TPB):
                        t = b * TPB + i
                        for c, src in ((0, w.y[:, t, 0:HALF]), (1, bank[b][:, i * HALF:(i + 1) * HALF])):
                            nc.vector.tensor_scalar(n[:, t, c * HALF:(c + 1) * HALF], src, w.mean_var[:, t, 0:1],
                                                    w.rstd[:, t:t + 1], ALU.subtract, ALU.mult).then_inc(s["normed"], 1)

                def gate_in(t):
                    if t == 0:
                        dve.wait_ge(s["pad"], 2)
                    if t >= 2:
                        dve.wait_ge(s["gelu"], t - 1)
                        dve.wait_ge(s["gated"], t - 1)
                    dve.wait_ge(s["w1"], 2 * t + 1)
                    nc.vector.tensor_tensor(gin[:, t % 2, :], bank[3 + 2 * (t % 2)][:, 0:HID], b1[:, HID:2 * HID],
                                            ALU.add).then_inc(s["gated_in"], 1)
                    dve.wait_ge(s["w1"], 2 * t + 2)
                    nc.vector.tensor_tensor(ain[:, t % 2, :], bank[2 + 2 * (t % 2)][:, 0:HID], b1[:, 0:HID],
                                            ALU.add).then_inc(s["gated_in"], 1)

                def gate(t):
                    dve.wait_ge(s["gelu"], t + 1)
                    dve.wait_ge(s["gated_in"], 2 * t + 2)
                    if t >= 2:
                        dve.wait_ge(s["gT_ps"], t - 1)
                    nc.vector.tensor_tensor(gated[:, t % 2, 0:HID], ain[:, t % 2, :], gel[:, t % 2, :],
                                            ALU.mult).then_inc(s["gated"], 1)

                def update(t):
                    if t == 0:
                        dve.wait_ge(s["y_bias"], 1)
                    dve.wait_ge(s["w2"], t + 1)
                    nc.vector.tensor_tensor(w.y[:, t, :], yb[:, t, :], bank[7][:, 0:D], ALU.add).then_inc(s["y_new"], 1)

                statistics(0)
                statistics(1)
                normed(0)
                normed(1)
                gate_in(0)
                gate(0)
                gate_in(1)
                gate(1)
                gate_in(2)
                update(0)
                gate(2)
                gate_in(3)
                update(1)
                gate(3)
                update(2)
                update(3)

            @block.gpsimd
            def _(pool):
                nc.gpsimd.memset(hT[HALF:P, :, 0:1], 0.0).then_inc(s["edge_zero"], 1)
                pool.wait_ge(s["edge_zero"], 1)
                nc.gpsimd.memset(v[:, :, :, :, DH:DH + 1], 1.0).then_inc(s["ones"], 1)
                nc.gpsimd.memset(gated[:, :, HID:], 0.0).then_inc(s["pad"], 1)
                nc.gpsimd.tensor_copy(b1[:], w.b1_l[:, bass.ds(layer, 1), :].rearrange("p l n -> p (l n)")).then_inc(s["pool"], 1)
                nc.gpsimd.tensor_copy(lgb[:], w.ln_gb[:, :, bass.ds(layer, 1)]).then_inc(s["pool"], 1)
                pool.wait_ge(s["pool"], 2)
                nc.gpsimd.memset(yb[:], 0.0).then_inc(s["pad"], 1)
                for t in range(NT):
                    for c in range(2):
                        pool.wait_ge(s["rot_dve"], 2 * t + c + 1)
                        if t >= 2:
                            pool.wait_ge(s["qT_ps"] if c == 0 else s["kT_ps"], t - 1)
                        dst = qk[:, t % 2, 0, :] if c == 0 else kr[:, t % 2, :]
                        ins = nc.gpsimd.tensor_tensor(dst, r1[:, t % 2, c, :], r2[:, t % 2, c, :], ALU.add)
                        if c == 0:
                            ins.then_inc(s["rot_pool"], 1)
                            continue
                        ins.then_inc(s["pool"], 1)
                        pool.wait_ge(s["pool"], 3 + t)
                        pool.wait_ge(s["rn"], t + 1)
                        nc.gpsimd.tensor_tensor(
                            qk[:, t % 2, 1, :].rearrange("p (h d) -> p h d", h=HL),
                            kr[:, t % 2, :].rearrange("p (h d) -> p h d", h=HL),
                            rn[:, t, 1, :].unsqueeze(2).broadcast_to((P, HL, DH)), ALU.mult).then_inc(s["rot_pool"], 1)
                pool.wait_ge(s["y_attn"], NT)
                pool.wait_ge(s["pad"], 2)
                nc.gpsimd.tensor_tensor(yb[:], w.y[:], w.b2_l[:, bass.ds(layer, 1), :].broadcast_to((P, NT, D)),
                                        ALU.add).then_inc(s["y_bias"], 1)
        clear(nc, s)


def attention_b(nc, w, pair):
    with ExitStack() as ctx:
        def sb(name, shape):
            return ctx.enter_context(nc.sbuf_tensor("b_" + name, shape, F32))

        s = signals(nc, ctx, "b", "dve x_new var_ready std_ready normed xT_ps xT proj q_sb k_sb v_sum vd hidden_ps hidden "
                                  "q1 q1_sb norms nT_ps bounds diag spread weights wT_ps wT vw_ps vw out_ps x_out var2 std2 "
                                  "pool xbo")
        xn, xT = sb("xn", [P, NT, D]), sb("xT", [P, NT * P])
        qkT = sb("qkT", [P, 2, NT * P])
        v_sum, v_mean = sb("v_sum", [P, NB]), sb("v_mean", [P, NB])
        vd = sb("vd", [P, NB, HB])
        hidden = sb("hidden", [P, 3, NT * P])
        UN = 2 * HB
        q1 = sb("q1", [P, NT, UN, 2 * NQ])
        e1, e2, e3 = sb("e1", [P, NT, UN, NQ]), sb("e2", [P, NT, UN, NQ]), sb("e3", [P, NT, UN, NQ])
        norms = sb("norms", [P, NT, UN])
        bounds = sb("bounds", [HB, 3, NB])
        kz = sb("kz", [HB, NB, T])
        diag = sb("diag", [HB, 3, NB, HB])
        prod = sb("prod", [P, NT, 2, HB])
        ne, rec, quot = sb("ne", [P, NT, 2, HB]), sb("rec", [P, NT, 2, HB]), sb("quot", [P, NT, 2, HB])
        wgt = sb("wgt", [P, NT, HB])
        wT, vw = sb("wT", [HB, NT, P]), sb("vw", [HB, NB, D])
        mix = sb("mix", [P, 2, HB])
        bank = [ctx.enter_context(nc.psum_tensor(f"b_bank{i}", [P, 512], F32)) for i in range(8)]

        with nc.Block() as block:
            @block.tensor
            def _(pe):
                pe.wait_ge(s["normed"], NT)
                for t in range(NT):
                    pe.transpose(bank[3][:, t * P:(t + 1) * P], xn[:, t, :], w.ident[:]).then_inc(s["xT_ps"], 1)
                pe.wait_ge(s["xT"], 1)
                for c in range(3):
                    pe.matmul(bank[c][:], w.wqkv_b[:, c, :], xT[:], start=True, stop=True).then_inc(s["proj"], 1)

                def hide(v):
                    c, h = divmod(v, HB)
                    if v == 0:
                        pe.wait_ge(s["q_sb"], 1)
                    if v == 1:
                        pe.wait_ge(s["k_sb"], 1)
                    if v == 3:
                        pe.wait_ge(s["v_sum"], 1)
                    if v >= 4:
                        pe.wait_ge(s["hidden"], v - 3)
                    pe.matmul(bank[(v + 3) % 4][:], w.w1_b[:, h, :], qkT[:, c, :], start=True, stop=True)\
                        .then_inc(s["hidden_ps"], 1)

                def encode(v):
                    pe.wait_ge(s["hidden"], v + 1)
                    for t in range(NT):
                        ins = pe.matmul(bank[4 + t][:, 2 * NQ * v:2 * NQ * (v + 1)], hidden[:, v % 3, t * P:(t + 1) * P],
                                        w.w2_b[:], start=True, stop=True)
                    ins.then_inc(s["q1"], 1)

                for v in range(UN + 2):
                    if v < UN:
                        hide(v)
                    if v >= 2:
                        encode(v - 2)
                pe.wait_ge(s["norms"], 1)
                for t in range(NT):
                    ins = pe.transpose(bank[0][0:HB, t * P:(t + 1) * P], norms[:, t, HB:UN], w.ident[:])
                ins.then_inc(s["nT_ps"], 1)
                pe.wait_ge(s["vd"], 1)
                for b in range(NB):
                    ins = pe.matmul(bank[1][0:HB, b * D:(b + 1) * D], vd[:, b, :], w.wo_b[:], start=True, stop=True)
                ins.then_inc(s["vw_ps"], 1)
                pe.wait_ge(s["diag"], 1)
                pe.matmul(bank[2][:, 0:3 * NB * HB], w.ones_t[0:HB, :], diag[:].rearrange("p c b h -> p (c b h)"),
                          start=True, stop=True).then_inc(s["spread"], 1)
                pe.wait_ge(s["weights"], 1)
                for t in range(NT):
                    ins = pe.transpose(bank[3][0:HB, t * P:(t + 1) * P], wgt[:, t, :], w.ident[:])
                ins.then_inc(s["wT_ps"], 1)
                pe.wait_ge(s["wT"], 1)
                pe.wait_ge(s["vw"], 1)
                for t in range(NT):
                    ins = pe.matmul(bank[0][:, t * D:(t + 1) * D], wT[:, t, :], vw[:, t // TPB, :], start=True, stop=True)
                ins.then_inc(s["out_ps"], 1)

            @block.scalar
            def _(act):
                act.wait_ge(s["var_ready"], NT)
                nc.scalar.activation(w.std[:], w.mean_var[:, :, 1], ACT.Sqrt, bias=w.eps_t[:, 0:1]).then_inc(s["std_ready"], 1)
                act.wait_ge(s["xT_ps"], NT)
                nc.scalar.copy(xT[:], bank[3][:]).then_inc(s["xT"], 1)
                act.wait_ge(s["proj"], 1)
                nc.scalar.activation(qkT[:, 0, :], bank[0][:], ACT.Identity, bias=w.bqkv_b[:, 0:1]).then_inc(s["q_sb"], 1)
                for v in range(UN):
                    act.wait_ge(s["hidden_ps"], v + 1)
                    if v >= 3:
                        act.wait_ge(s["q1"], v - 2)
                    nc.scalar.activation(hidden[:, v % 3, :], bank[(v + 3) % 4][:], ACT.Tanh,
                                         bias=w.b1_b[:, 0:1]).then_inc(s["hidden"], 1)
                act.wait_ge(s["vw_ps"], 1)
                nc.scalar.copy(vw[:].rearrange("p b n -> p (b n)"), bank[1][0:HB, 0:NB * D]).then_inc(s["vw"], 1)
                act.wait_ge(s["wT_ps"], 1)
                nc.scalar.copy(wT[:].rearrange("p t k -> p (t k)"), bank[3][0:HB, :]).then_inc(s["wT"], 1)
                act.wait_ge(s["var2"], NT)
                nc.scalar.activation(w.std[:], w.mean_var[:, :, 1], ACT.Sqrt, bias=w.eps_t[:, 0:1]).then_inc(s["std2"], 1)

            @block.gpsimd
            def _(pool):
                nc.gpsimd.tensor_copy(mix[:].rearrange("p c h -> p (c h)"),
                                      w.mix_b[:, bass.ds(pair, 1)].rearrange("p o c h -> p (o c h)")).then_inc(s["pool"], 1)
                pool.wait_ge(s["x_new"], 1)
                pool.wait_ge(s["normed"], NT)
                nc.gpsimd.tensor_tensor(w.x[:], w.x[:], w.bo_b[:].unsqueeze(1).broadcast_to((P, NT, D)),
                                        ALU.add).then_inc(s["xbo"], 1)

            @block.vector
            def _(dve):
                st = Steps(dve, s["dve"])

                def then(instruction):
                    st.wait(st.did(instruction))

                nc.vector.tensor_tensor(w.x[:], w.x[:], w.y[:], ALU.add).then_inc(s["x_new"], 1)
                dve.wait_ge(s["x_new"], 1)
                layer_norm_stats(nc, dve, st, w, range(NT), w.x, s, s["var_ready"])
                dve.wait_ge(s["std_ready"], 1)
                then(nc.vector.reciprocal(w.rstd[:], w.std[:]))
                for t in range(NT):
                    nc.vector.tensor_scalar(xn[:, t, :], w.x[:, t, :], w.mean_var[:, t, 0:1], w.rstd[:, t:t + 1],
                                            ALU.subtract, ALU.mult).then_inc(s["normed"], 1)
                dve.wait_ge(s["proj"], 2)
                nc.vector.tensor_scalar(qkT[:, 1, :], bank[1][:], w.bqkv_b[:, 1:2], None, ALU.add).then_inc(s["k_sb"], 1)
                dve.wait_ge(s["proj"], 3)
                nc.vector.tensor_reduce(v_sum[:], bank[2][:].rearrange("p (b k) -> p b k", b=NB), AX.X, ALU.add)\
                    .then_inc(s["v_sum"], 1)
                dve.wait_ge(s["v_sum"], 1)
                then(nc.vector.tensor_scalar(v_mean[:], v_sum[:], 1.0 / T, w.bqkv_b[:, 2:3], ALU.mult, ALU.add))
                for b in range(NB):
                    ins = nc.vector.tensor_scalar(vd[:, b, :], w.head_of[:], v_mean[:, b:b + 1], None, ALU.mult)
                    if b < NB - 1:
                        st.did(ins)
                ins.then_inc(s["vd"], 1)

                dve.wait_ge(s["q1"], UN)
                b2 = w.b2_b[:].unsqueeze(1).broadcast_to((P, UN, 2 * NQ))
                for t in range(NT):
                    k = st.did(nc.vector.tensor_tensor(q1[:, t], bank[4 + t][:].rearrange("p (v n) -> p v n", v=UN), b2, ALU.add))
                st.wait(k)
                dve.wait_ge(s["pool"], 1)
                for t in range(NT):
                    other = (t + TPB) % NT
                    for dst, src, c in ((e1, q1[:, t, :, 0:NQ], 0), (e2, q1[:, other, :, NQ:2 * NQ], 1)):
                        table = mix[:, c, :].unsqueeze(1).unsqueeze(3).broadcast_to((P, 2, HB, NQ))
                        k = st.did(nc.vector.tensor_tensor(dst[:, t].rearrange("p (c h) n -> p c h n", c=2),
                                                           src.rearrange("p (c h) n -> p c h n", c=2), table, ALU.mult))
                st.wait(k)
                then(nc.vector.tensor_tensor(e3[:], e1[:], e2[:], ALU.add))
                then(nc.vector.tensor_tensor(e1[:], e3[:], e3[:], ALU.mult))
                nc.vector.tensor_reduce(norms[:], e1[:], AX.X, ALU.add).then_inc(s["norms"], 1)
                dve.wait_ge(s["nT_ps"], 1)
                keys = bank[0][0:HB, :].rearrange("p (b k) -> p b k", b=NB)
                st.did(nc.vector.tensor_reduce(bounds[:, 0, :], keys, AX.X, ALU.min))
                st.did(nc.vector.tensor_reduce(bounds[:, 1, :], keys, AX.X, ALU.max))
                then(nc.vector.tensor_scalar(kz[:], keys, 0.0, None, ALU.mult))
                then(nc.vector.tensor_reduce(bounds[:, 2, :], kz[:], AX.X, ALU.add))
                for c in range(3):
                    for b in range(NB):
                        ins = nc.vector.tensor_scalar(diag[:, c, b, :], w.ident[0:HB, 0:HB], bounds[:, c, b:b + 1], None, ALU.mult)
                        if (c, b) != (2, NB - 1):
                            st.did(ins)
                ins.then_inc(s["diag"], 1)
                dve.wait_ge(s["norms"], 1)
                dve.wait_ge(s["spread"], 1)
                spread = bank[2][:, 0:3 * NB * HB].rearrange("p (c b h) -> p c b h", c=3, b=NB)
                for b in range(NB):
                    for c in range(2):
                        queries = norms[:, b * TPB:(b + 1) * TPB, 0:HB]
                        k = st.did(nc.vector.tensor_tensor(prod[:, b * TPB:(b + 1) * TPB, c, :], queries,
                                                           spread[:, c, b, :].unsqueeze(1).broadcast_to((P, TPB, HB)), ALU.mult))
                st.wait(k)
                then(nc.vector.tensor_scalar(ne[:], prod[:], 0.0, None, ALU.not_equal))
                then(nc.vector.reciprocal(rec[:], ne[:]))
                then(nc.vector.tensor_tensor(rec[:], rec[:], ne[:], ALU.mult))
                then(nc.vector.scalar_tensor_tensor(out=quot[:], in0=prod[:], scalar=0.0, in1=rec[:], op0=ALU.mult, op1=ALU.add))
                then(nc.vector.tensor_tensor(wgt[:], quot[:, :, 0, :], quot[:, :, 1, :], ALU.mult))
                for b in range(NB):
                    ts = slice(b * TPB, (b + 1) * TPB)
                    ins = nc.vector.tensor_tensor(wgt[:, ts, :], wgt[:, ts, :],
                                                  spread[:, 2, b, :].unsqueeze(1).broadcast_to((P, TPB, HB)), ALU.add)
                    if b < NB - 1:
                        st.did(ins)
                ins.then_inc(s["weights"], 1)
                dve.wait_ge(s["out_ps"], 1)
                dve.wait_ge(s["xbo"], 1)
                nc.vector.tensor_tensor(w.x[:], w.x[:], bank[0][:].rearrange("p (t n) -> p t n", t=NT), ALU.add).then_inc(s["x_out"], 1)
                dve.wait_ge(s["x_out"], 1)
                layer_norm_stats(nc, dve, st, w, range(NT), w.x, s, s["var2"])
                dve.wait_ge(s["std2"], 1)
                then(nc.vector.reciprocal(w.rstd[:], w.std[:]))
                for t in range(NT):
                    st.did(nc.vector.tensor_scalar(w.y[:, t, :], w.x[:, t, :], w.mean_var[:, t, 0:1], w.rstd[:, t:t + 1],
                                                   ALU.subtract, ALU.mult))
        clear(nc, s)


def store(nc, w, pair, out):
    with ExitStack() as ctx:
        s = signals(nc, ctx, "store", "summed stored")
        with nc.Block() as block:
            @block.vector
            def _(dve):
                nc.vector.tensor_tensor(w.x[:], w.x[:], w.y[:], ALU.add).then_inc(s["summed"], 1)

            @block.sync
            def _(sp):
                sp.wait_ge(s["summed"], 1)
                dst = out.rearrange("(g b) (c p) d -> p g (b c) d", b=NB, p=P)
                sp.dma_start(dst[:, bass.ds(pair, 1), :, :], w.x[:]).then_inc(s["stored"], 16)
                sp.wait_ge(s["stored"], 16)
        clear(nc, s)


def turned_inputs(inputs):
    return {
        "ln_g_by_feature": np.ascontiguousarray(np.asarray(inputs["L0_ffn_ln_g"]).T),
        "ln_b_by_feature": np.ascontiguousarray(np.asarray(inputs["L0_ffn_ln_b"]).T),
        "w2_transposed": np.ascontiguousarray(np.asarray(inputs["L0_attn_b_w2"]).T),
        "angles_by_pair": np.ascontiguousarray(np.asarray(inputs["L0_attn_b_rot"])[:, 0:NQ // 2, 0].T),
    }


INPUTS = ["L0_attn_a_x", "L0_attn_a_Wq", "L0_attn_a_Wk", "L0_attn_a_Wv", "L0_attn_a_Wo",
          "L0_attn_a_polarity_direction", "L0_attn_a_gtp_gamma", "L0_attn_b_wq", "L0_attn_b_bq", "L0_attn_b_wk",
          "L0_attn_b_bk", "L0_attn_b_wv", "L0_attn_b_bv", "L0_attn_b_wo", "L0_attn_b_bo", "L0_attn_b_w1",
          "L0_attn_b_b1", "L0_attn_b_b2", "L0_attn_b_hadamard", "L0_ffn_wqkv",
          "L0_ffn_q_scale", "L0_ffn_k_scale", "L0_ffn_wo", "L0_ffn_w1", "L0_ffn_b1",
          "L0_ffn_w2", "L0_ffn_b2"]


def kernel(**inputs):
    import concourse.bacc as bacc
    from concourse.bass_utils import run_bass_kernel_spmd

    nc = bacc.Bacc("TRN2", target_bir_lowering=False, num_devices=1)
    arrays, a, consts = {}, {}, {}
    for name, array in {**{n: np.ascontiguousarray(inputs[n]) for n in INPUTS}, **turned_inputs(inputs)}.items():
        arrays[f"in_{name}"] = array
        a[name] = nc.dram_tensor(f"in_{name}", array.shape, mybir.dt.from_np(array.dtype), kind="ExternalInput").ap()
    for name, array in shape_constants().items():
        arrays[f"const_{name}"] = array
        consts[name] = nc.dram_tensor(f"const_{name}", array.shape, F32, kind="ExternalInput").ap()
    out = nc.dram_tensor("out_0", (BATCH, T, D), F32, kind="ExternalOutput").ap()
    build(nc, a, consts, out)
    result = run_bass_kernel_spmd(nc, [arrays], core_ids=[0])
    return result.results[0]["out_0"]
```

```python
from contextlib import ExitStack

import numpy as np

import concourse.bass as bass
from concourse import mybir

ALU = mybir.AluOpType
ACT = mybir.ActivationFunctionType
AX = mybir.AxisListType
F32 = mybir.dt.float32
F32R = mybir.dt.float32r

P = 128
BATCH, T, D = 16, 256, 128
NB = 2
PAIRS = BATCH // NB
TPB = T // P
NT = NB * TPB
HALF = D // 2
DH = 64
HQ, HKV = 16, 4
QW, KW = HQ * DH, HKV * DH
NEG = -1e9
SLOTS = HQ // 2
BLK = 4
DEPTH, HL = 2, 8
INNER = HL * DH
WIN = 64
HID = int(D * 4 * 2 / 3)
HIDT = 3
PAIRH = HL // 2
VSETS = 3
MASKED = 1e24
HB, NQ = 16, 8
HD = D // HB
GB = 2
EPS = 1e-5
TWO_PI = 2.0 * np.pi


class Memory:
    pass


def signals(nc, ctx, prefix, names):
    return {name: ctx.enter_context(nc.semaphore(f"{prefix}_{name}")) for name in names.split()}


class Steps:

    def __init__(self, engine, semaphore):
        self.engine, self.semaphore, self.n = engine, semaphore, 0

    def did(self, instruction):
        self.n += 1
        instruction.then_inc(self.semaphore, 1)
        return self.n

    def wait(self, n):
        self.engine.wait_ge(self.semaphore, n)


def clear(nc, s):
    with nc.Block() as block:
        @block.sync
        def _(sp):
            numbers = sorted(x.num for x in s.values())
            start = numbers[0]
            for a, b in zip(numbers, numbers[1:] + [None]):
                if b != a + 1:
                    sp.sem_clear(range(start, a + 1))
                    start = b


def shape_constants():
    c = {}
    c["identity"] = np.eye(P, dtype=np.float32)
    c["shift_down"] = np.eye(P, k=1, dtype=np.float32)
    edge = np.zeros((P, P), np.float32)
    edge[P - 1, 0] = 1
    c["edge"] = edge
    half = DH // 2
    pos = np.arange(T, dtype=np.float32)
    inv = (1.0 / np.float32(10000.0) ** (np.arange(half, dtype=np.float32) / np.float32(half))).astype(np.float32)
    ang = pos[:, None] * inv[None, :]
    cos, sin = np.cos(ang), np.sin(ang)
    rope = np.stack([np.concatenate([cos, cos], 1), np.concatenate([-sin, sin], 1)], 1)
    c["rope_a"] = np.ascontiguousarray(rope.reshape(TPB, P, 2, DH).transpose(1, 0, 2, 3)).astype(np.float32)
    hi = np.arange(0, DH, 2, dtype=np.float32)
    inv = (1.0 / np.float32(10000.0) ** (hi / np.float32(DH))).astype(np.float32)
    ang = pos[:, None] * inv[None, :]
    base = ((hi + 0.4 * DH) / (1.4 * DH)).astype(np.float32)
    power = (pos - T // 2) / np.float32(WIN // 2)
    scale = base[None, :] ** power[:, None]
    scale = np.concatenate([scale, scale], 1)
    cos, sin = np.cos(ang), np.sin(ang)
    cos, sin = np.concatenate([cos, cos], 1), np.concatenate([-sin, sin], 1)
    xpos = np.stack([np.stack([-8.0 * cos * scale, -8.0 * sin * scale], 1),
                     np.stack([cos / scale, sin / scale], 1)], 1)
    c["rope_l"] = np.ascontiguousarray(
        xpos.reshape(TPB, P, 2, 2, DH).transpose(1, 2, 0, 3, 4)).astype(np.float32)
    mask = np.zeros((P, TPB, P), np.float32)
    for tile in range(TPB):
        for p in range(P):
            i = tile * P + p
            for j in range(P):
                key = first_key(tile, p // WIN) + j
                if i < key or i > key + WIN:
                    mask[p, tile, j] = MASKED
    c["mask_l"] = mask
    q = np.arange(T, dtype=np.float32)
    causal = (q[None, :] <= q[:, None]).astype(np.float32)
    for name, table in (("signed_a", (q[None, :] - q[:, None]) / np.float32(T) * causal),
                        ("dist_a", np.maximum(q[:, None] - q[None, :], 0.0)),
                        ("causal_a", causal)):
        c[name] = np.ascontiguousarray(table.reshape(TPB, P, T).transpose(1, 0, 2)).astype(np.float32)
    c["head_of"] = np.repeat(np.eye(HB, dtype=np.float32), HD, 0)
    return c


def first_key(tile, half):
    window = 2 * tile + half
    return max(window - 1, 0) * WIN


def build(nc, a, consts, out):
    with ExitStack() as ctx:
        def sb(name, shape):
            return ctx.enter_context(nc.sbuf_tensor(name, shape, F32))

        w = Memory()
        w.ident = sb("ident", [P, P])
        w.shift_m = sb("shift_m", [P, P])
        w.edge_m = sb("edge_m", [P, P])
        w.rope_a = sb("rope_a", [P, TPB, 2, DH])
        w.rope_l = sb("rope_l", [P, 2, TPB, 2, DH])
        w.mask_l = sb("mask_l", [P, TPB, P])
        w.head_of = sb("head_of", [P, HB])
        w.eps_t = sb("eps_t", [P, 1])
        w.ones_t = sb("ones_t", [P, P])
        w.wqkv_a = sb("wqkv_a", [P, QW + 2 * KW])
        w.wo_a = sb("wo_a", [P, SLOTS, D])
        w.bias_a = sb("bias_a", [P, TPB, HQ, T])
        w.wqkv_l = sb("wqkv_l", [P, DEPTH, 3 * INNER])
        w.wo_l = sb("wo_l", [P, DEPTH, PAIRH, D])
        w.w1_l = sb("w1_l", [P, DEPTH, 2 * HID])
        w.w2_l = sb("w2_l", [P, DEPTH, HIDT, D])
        w.b1_l = sb("b1_l", [P, DEPTH, 2 * HID])
        w.b2_l = sb("b2_l", [P, DEPTH, D])
        w.ln_gb = sb("ln_gb", [P, 2, DEPTH])
        w.rot_l = sb("rot_l", [P, DEPTH, 2, TPB, 2, DH])
        w.wqk_b = sb("wqk_b", [P, 2 * GB, 2, D // GB])
        w.wv_b = sb("wv_b", [P, D])
        w.wo_b = sb("wo_b", [P, D])
        w.bqk_b, w.bv_b = sb("bqk_b", [P, 2 * GB]), sb("bv_b", [P, 1])
        w.w1_b = ctx.enter_context(nc.sbuf_tensor("w1_b", [P, 2, HB // GB, D], F32R))
        w.b1_b = sb("b1_b", [P, 1])
        w.w2_b = sb("w2_b", [P, 4 * NQ])
        w.b2_b = sb("b2_b", [P, 2 * NQ])
        w.bo_b = sb("bo_b", [P, D])
        w.mix_b = sb("mix_b", [P, PAIRS, 2, HB])
        w.x = sb("x", [P, NT, D])
        w.y = sb("y", [P, NT, D])
        w.stats = sb("stats", [P, NT, 2, 6])
        w.mean_var = sb("mean_var", [P, NT, 2])
        w.std = sb("std", [P, NT])
        w.rstd = sb("rstd", [P, NT])

        setup(nc, a, consts, w)
        with nc.Fori(0, PAIRS) as pair:
            attention_a(nc, w)
            with nc.Fori(0, DEPTH) as layer:
                local_layer(nc, w, layer, "l")
            attention_b(nc, w, pair)
            with nc.Fori(0, DEPTH) as layer:
                local_layer(nc, w, layer, "m")
            store(nc, w, pair, a["x_and_one_pair_more"], out)


def pairs_of_tiles(x):
    return x.rearrange("(g b) (c p) d -> p g (b c) d", b=NB, p=P)


def setup(nc, a, consts, w):
    with ExitStack() as ctx:
        def sb(name, shape):
            return ctx.enter_context(nc.sbuf_tensor("setup_" + name, shape, F32))

        s = signals(nc, ctx, "setup", "zeroed small loaded exp_a dve done pe act pool placed trig w1_high")
        signed, dist, causal = (sb(n, [P, TPB, T]) for n in ("signed", "dist", "causal"))
        pol, gam = sb("pol", [P, HQ]), sb("gam", [P, HQ])
        e = sb("e", [P, 2, TPB, T])
        u = sb("u", [P, 2, TPB, T])
        v = sb("v", [P, 2, TPB, T])
        qs = sb("qs", [P, DEPTH, 2, DH])
        rot = sb("rot", [P, NQ // 2, HB])
        ang, turns, angr = sb("ang", [P, NQ // 2, 2, HB]), sb("turns", [P, NQ // 2, 2, HB]), sb("angr", [P, NQ // 2, 2, HB])
        had = sb("had", [2 * NQ, 4 * NQ])
        w1 = sb("w1", [P, HB // GB, D])
        w2T, b2col, b2rep = sb("w2T", [2 * NQ, P]), sb("b2col", [2 * NQ, 1]), sb("b2rep", [2 * NQ, P])
        ps = ctx.enter_context(nc.psum_tensor("setup_ps", [P, 512], F32))

        plain = [
            (w.x[:], pairs_of_tiles(a["x_and_one_pair_more"])[:, 0:1]),
            (w.ident[:], consts["identity"]), (w.shift_m[:], consts["shift_down"]), (w.edge_m[:], consts["edge"]),
            (w.rope_a[:], consts["rope_a"]), (w.mask_l[:], consts["mask_l"]), (w.head_of[:], consts["head_of"]),
            (w.wqkv_a[:, 0:QW], a["L0_attn_a_Wq"]), (w.wqkv_a[:, QW:QW + KW], a["L0_attn_a_Wk"]),
            (w.wqkv_a[:, QW + KW:], a["L0_attn_a_Wv"]),
            (w.wqkv_l[:], a["L0_ffn_wqkv"].rearrange("l p n -> p l n")),
            (w.wo_l[:], a["L0_ffn_wo"].rearrange("l (k p) n -> p l k n", p=P)),
            (w.w1_l[:], a["L0_ffn_w1"].rearrange("l p n -> p l n")),
            (w.ln_gb[:, 0, :], a["ln_g_by_feature"]),
            (w.ln_gb[:, 1, :], a["ln_b_by_feature"]),
            (w.b1_l[:], a["L0_ffn_b1"].rearrange("(o l) n -> o l n", o=1).broadcast_to((P, DEPTH, 2 * HID))),
            (w.b2_l[:], a["L0_ffn_b2"].rearrange("(o l) n -> o l n", o=1).broadcast_to((P, DEPTH, D))),
            (w.wv_b[:], a["L0_attn_b_wv"]), (w.wo_b[:], a["L0_attn_b_wo"]),
            (w.bv_b[:], a["L0_attn_b_bv"].rearrange("(p o) -> p o", o=1)),
            (w.b1_b[:], a["L0_attn_b_b1"].rearrange("(p o) -> p o", o=1)),
            (w.bo_b[:], a["L0_attn_b_bo"].rearrange("(o n) -> o n", o=1).broadcast_to((P, D))),
        ]
        for c, name in enumerate(("k", "q")):
            for half in range(2):
                plain.append((w.wqk_b[:, GB * c:GB * (c + 1), half, :],
                              a[f"L0_attn_b_w{name}"].rearrange("p (g n) -> p g n", g=GB)))
                plain.append((w.bqk_b[64 * half:64 * half + 64, GB * c:GB * (c + 1)], a[f"b{name}_by_group"]))
        wo_rows = a["L0_attn_a_Wo"].rearrange("(b e r d) n -> b e d r n", b=SLOTS // BLK, e=2, r=BLK)
        plain += [(w.wo_a[64 * e:64 * e + 64, BLK * b:BLK * (b + 1), :], wo_rows[b, e])
                  for b in range(SLOTS // BLK) for e in range(2)]
        small = [
            (signed[:], consts["signed_a"]), (dist[:], consts["dist_a"]), (causal[:], consts["causal_a"]),
            (pol[:], a["L0_attn_a_polarity_direction"].rearrange("(o h) -> o h", o=1).broadcast_to((P, HQ))),
            (gam[:], a["L0_attn_a_gtp_gamma"].rearrange("(o h) -> o h", o=1).broadcast_to((P, HQ))),
            (w.rope_l[:], consts["rope_l"]),
            (qs[:, :, 0, :], a["L0_ffn_q_scale"].rearrange("(o l) n -> o l n", o=1).broadcast_to((P, DEPTH, DH))),
            (qs[:, :, 1, :], a["L0_ffn_k_scale"].rearrange("(o l) n -> o l n", o=1).broadcast_to((P, DEPTH, DH))),
            (rot[:], a["angles_by_pair"].rearrange("(o n) h -> o n h", o=1).broadcast_to((P, NQ // 2, HB))),
            (w2T[:], a["w2_transposed"]),
            (b2col[:], a["L0_attn_b_b2"].rearrange("(p o) -> p o", o=1)),
        ]
        placed = [(w1[64 * half + HD * h:64 * half + HD * (h + 1), h, :], a["L0_attn_b_w1"])
                  for half in range(2) for h in range(HB // GB)]
        placed += [(had[NQ * i:NQ * (i + 1), NQ * i:NQ * (i + 1)], a["L0_attn_b_hadamard"]) for i in range(2)]
        last = HID - (HIDT - 1) * P
        placed += [(w.w2_l[0:P, l, 0:HIDT - 1, :],
                    a["L0_ffn_w2"][l, 0:(HIDT - 1) * P, :].rearrange("(k p) n -> p k n", p=P)) for l in range(DEPTH)]
        placed += [(w.w2_l[0:last, l, HIDT - 1, :], a["L0_ffn_w2"][l, (HIDT - 1) * P:HID, :]) for l in range(DEPTH)]

        with nc.Block() as block:
            @block.sync
            def _(sp):
                for dst, src in small:
                    sp.dma_start(dst, src).then_inc(s["small"], 16)
                for dst, src in plain:
                    sp.dma_start(dst, src).then_inc(s["loaded"], 16)
                sp.wait_ge(s["zeroed"], 3)
                for dst, src in placed:
                    sp.dma_start(dst, src).then_inc(s["placed"], 16)
                sp.wait_ge(s["placed"], 16 * len(placed))
                sp.wait_ge(s["loaded"], 16 * len(plain))

            @block.gpsimd
            def _(pool):
                nc.gpsimd.memset(w1[:], 0.0).then_inc(s["zeroed"], 1)
                nc.gpsimd.memset(had[:], 0.0).then_inc(s["zeroed"], 1)
                nc.gpsimd.memset(w.w2_l[:], 0.0).then_inc(s["zeroed"], 1)
                nc.gpsimd.memset(w.eps_t[:], EPS).then_inc(s["pool"], 1)
                nc.gpsimd.memset(w.ones_t[:], 1.0).then_inc(s["pool"], 1)
                nc.gpsimd.memset(w.mix_b[:, NQ // 2:, 0, :], 1.0).then_inc(s["pool"], 1)
                nc.gpsimd.memset(w.mix_b[:, NQ // 2:, 1, :], 0.0).then_inc(s["pool"], 1)

            @block.scalar
            def _(act):
                for h in range(HQ):
                    act.wait_ge(s["done"], 1 + max(h - 1, 0))
                    nc.scalar.activation(e[:, h % 2], dist[:], ACT.Exp,
                                         scale=gam[:, h:h + 1]).then_inc(s["exp_a"], 1)
                act.wait_ge(s["trig"], 1)
                nc.scalar.activation(w.mix_b[:, 0:NQ // 2, :, :], angr[:], ACT.Sin).then_inc(s["act"], 1)

            @block.vector
            def _(dve):
                st = Steps(dve, s["dve"])
                dve.wait_ge(s["small"], 16 * len(small))
                n = st.did(nc.vector.tensor_scalar(pol[:], pol[:], -1.0, 1.0, ALU.max, ALU.min))
                m = st.did(nc.vector.tensor_scalar(gam[:], gam[:], 1e-4, None, ALU.max))
                st.wait(m)
                nc.vector.tensor_scalar(gam[:], gam[:], -1.0, None, ALU.mult).then_inc(s["done"], 1)
                st.did(nc.vector.tensor_scalar(ang[:, :, 0, :], rot[:], 0.5, float(np.pi / 2), ALU.mult, ALU.add))
                k = st.did(nc.vector.tensor_scalar(ang[:, :, 1, :], rot[:], 0.5, None, ALU.mult))
                st.wait(k)
                big = float(1.5 * 2 ** 23)
                k = st.did(nc.vector.tensor_scalar(turns[:], ang[:], 1.0 / TWO_PI, big, ALU.mult, ALU.add))
                st.wait(k)
                k = st.did(nc.vector.tensor_scalar(turns[:], turns[:], big, -TWO_PI, ALU.subtract, ALU.mult))
                st.wait(k)
                k = st.did(nc.vector.tensor_tensor(angr[:], ang[:], turns[:], ALU.add))
                st.wait(k)
                k = st.did(nc.vector.tensor_scalar(angr[:], angr[:], float(np.pi), float(-np.pi), ALU.min, ALU.max))
                st.wait(k)
                nc.vector.tensor_copy(ang[:], angr[:]).then_inc(s["trig"], 1)
                for l in range(DEPTH):
                    for i in range(2):
                        for t in range(TPB):
                            st.did(nc.vector.tensor_tensor(w.rot_l[:, l, i, t, 0, :], w.rope_l[:, i, t, 0, :],
                                                           qs[:, l, i, :], ALU.mult))
                            for hf in range(2):
                                lo, ot = hf * DH // 2, (1 - hf) * DH // 2
                                st.did(nc.vector.tensor_tensor(
                                    w.rot_l[:, l, i, t, 1, lo:lo + DH // 2], w.rope_l[:, i, t, 1, lo:lo + DH // 2],
                                    qs[:, l, i, ot:ot + DH // 2], ALU.mult))
                st.did(nc.vector.tensor_scalar(b2rep[:], w2T[:], 0.0, b2col[:, 0:1], ALU.mult, ALU.add))
                k = st.n
                dve.wait_ge(s["done"], 1)
                for h in range(HQ):
                    dve.wait_ge(s["exp_a"], h + 1)
                    i = h % 2
                    k1 = st.did(nc.vector.tensor_tensor(u[:, i], e[:, i], causal[:], ALU.mult))
                    k2 = st.did(nc.vector.tensor_scalar(v[:, i], signed[:], pol[:, h:h + 1], 8.0, ALU.mult, ALU.mult))
                    st.wait(k1)
                    k3 = st.did(nc.vector.tensor_scalar(u[:, i], u[:, i], -1.0, 1.0, ALU.mult, ALU.add))
                    st.wait(k3)
                    nc.vector.scalar_tensor_tensor(out=w.bias_a[:, :, h, :], in0=u[:, i], scalar=8.0 * NEG, in1=v[:, i],
                                                   op0=ALU.mult, op1=ALU.add).then_inc(s["done"], 1)
                    dve.wait_ge(s["done"], h + 2)
                dve.wait_ge(s["pe"], 1)
                nc.vector.tensor_copy(w.w2_b[:], ps[:, 0:4 * NQ]).then_inc(s["dve"], 1)
                nc.vector.tensor_copy(w.b2_b[:], ps[:, 4 * NQ:6 * NQ]).then_inc(s["dve"], 1)
                dve.wait_ge(s["placed"], 16 * len(placed))
                nc.vector.tensor_copy(w.w1_b[:, 0], w1[:]).then_inc(s["w1_high"], 1)
                dve.wait_ge(s["w1_high"], 1)
                nc.vector.tensor_tensor(w.w1_b[:, 1], w1[:], w.w1_b[:, 0].bitcast(F32), ALU.subtract).then_inc(s["dve"], 1)

            @block.tensor
            def _(pe):
                pe.wait_ge(s["placed"], 16 * len(placed))
                pe.wait_ge(s["small"], 16 * len(small))
                pe.wait_ge(s["done"], 2)
                pe.matmul(ps[:, 0:4 * NQ], w2T[:], had[:], start=True, stop=True)
                pe.matmul(ps[:, 4 * NQ:6 * NQ], b2rep[:], had[:, 0:2 * NQ], start=True, stop=True).then_inc(s["pe"], 1)
        clear(nc, s)


def keep_clock(pe, w, bank, n):
    for _ in range(n):
        pe.matmul(bank[:], w.ident[:], w.wqkv_a[:, 0:512], start=True, stop=True)


def layer_norm_stats(nc, dve, st, w, tiles, src, s, done):
    for t in tiles:
        k = st.did(nc.vector.bn_stats(w.stats[:, t, 0, :], src[:, t, :]))
    st.wait(k)
    for t in tiles:
        nc.vector.bn_aggr(w.mean_var[:, t, :], w.stats[:, t, 0, :]).then_inc(done, 1)


def attention_a(nc, w):
    with ExitStack() as ctx:
        def sb(name, shape):
            return ctx.enter_context(nc.sbuf_tensor("a_" + name, shape, F32))

        s = signals(nc, ctx, "a", "dve var_ready std_ready normed xT_ps xT proj v_ps v_sb rot_dve rot_pool "
                                  "turned_ps turned scored shifted_scores exps inverse probs pT_ps pT_d pT_a pv oT wo "
                                  "x_new var2 std2")
        CH = QW // 2
        table = sb("table", [P, 1])
        xn = sb("xn", [P, NT, D])
        xT = sb("xT", [P, NT, P])
        r1, r2 = sb("r1", [P, 2, CH]), sb("r2", [P, 2, CH])
        qk = sb("qk", [P, 2, CH])
        qT = sb("qT", [P, 2, SLOTS, P])
        kT = sb("kT", [P, NB, HKV // 2, T])
        v = sb("v", [P, NT, HKV, DH])
        sc = sb("sc", [P, 2, 2, T])
        neg_max = sb("neg_max", [P, NT * SLOTS, 2])
        ex = sb("ex", [P, 2, 2, T])
        total, inv = sb("total", [P, NT * SLOTS, 2]), sb("inv", [P, NT * SLOTS, 2])
        pr = sb("pr", [P, 3, 2, T])
        pT = sb("pT", [P, 2, 2, TPB, BLK, P])
        oT = sb("oT", [P, SLOTS, P])
        bank = [ctx.enter_context(nc.psum_tensor(f"a_bank{i}", [P, 512], F32)) for i in range(8)]
        NU = NT * SLOTS
        NJOBS = 2 + 2 * NT
        STEPS = NU + 9
        slot_head = lambda j, e: 8 * (j // BLK) + 4 * e + j % BLK
        is_keys = lambda n: n in (0, 3)
        key_sequence = lambda n: n // 3
        queries_of = lambda n: (0, n - 1) if n < 4 else divmod(n - 2, 2)
        proj_bank = lambda n: bank[(0, 4, 1, 5)[n]] if n < 4 else bank[7]
        turn_bank = lambda n: bank[6 + n % 2] if n < 4 else bank[7]
        PROJECT_AT, TURN_AT = {2: 0, 4: 1}, {5: 0, 7: 1}

        def job_at(i, when):
            t, at = divmod(i, SLOTS)
            return 2 + 2 * (t + 1) + when[at] if t + 1 < NT and at in when else None

        with nc.Block() as block:
            @block.tensor
            def _(pe):
                keep_clock(pe, w, bank[0], 3)
                pe.wait_ge(s["normed"], NT)
                for t in range(NT):
                    pe.transpose(bank[6][:, t * P:(t + 1) * P], xn[:, t, :], w.ident[:]).then_inc(s["xT_ps"], 1)

                def project_keys(n):
                    for i in range(TPB):
                        ins = pe.matmul(proj_bank(n)[:, i * KW:(i + 1) * KW], xT[:, key_sequence(n) * TPB + i, :],
                                        w.wqkv_a[:, QW:QW + KW], start=True, stop=True)
                    ins.then_inc(s["proj"], 1)

                def project_values(b):
                    for i in range(TPB):
                        ins = pe.matmul(bank[2 + b][:, i * KW:(i + 1) * KW], xT[:, b * TPB + i, :],
                                        w.wqkv_a[:, QW + KW:], start=True, stop=True)
                    ins.then_inc(s["v_ps"], 1)

                def project(n):
                    t, c = queries_of(n)
                    if t >= 1 and c == 0:
                        pe.wait_ge(s["turned"], n)
                    if t >= 3 and c == 0:
                        pe.wait_ge(s["x_new"], t - 2)
                    if t >= 1 and c == 1:
                        pe.wait_ge(s["rot_dve"], n)
                    pe.matmul(proj_bank(n)[:], xT[:, t, :], w.wqkv_a[:, CH * c:CH * (c + 1)],
                              start=True, stop=True).then_inc(s["proj"], 1)

                def turn(n):
                    t, c = queries_of(n)
                    pe.wait_ge(s["rot_pool"], n + 1)
                    if n < 4:
                        pe.wait_ge(s["xT"], 1)
                        if n >= 2:
                            pe.wait_ge(s["turned"], n - 1)
                    elif c == 0:
                        pe.wait_ge(s["rot_dve"], n + 2)
                    else:
                        pe.wait_ge(s["turned"], n)
                    for i in range(CH // P):
                        ins = pe.transpose(turn_bank(n)[:, i * P:(i + 1) * P], qk[:, n % 2, i * P:(i + 1) * P], w.ident[:])
                    ins.then_inc(s["turned_ps"], 1)

                def scores(u):
                    t, j = divmod(u, SLOTS)
                    b = t // TPB
                    if u == 0:
                        pe.wait_ge(s["rot_dve"], 3)
                        pe.wait_ge(s["v_sb"], NB)
                    if j % BLK == 0:
                        pe.wait_ge(s["turned"], 2 + j // BLK if t == 0 else 3 + 2 * t + j // BLK)
                    for e in range(2):
                        r = 2 * u + e
                        if r >= 3:
                            pe.wait_ge(s["shifted_scores"], r - 2)
                        rows = slice(64 * e, 64 * e + 64)
                        pe.matmul(bank[r % 3][:, 0:T], qT[rows, t % 2, j, :], kT[rows, b, j // BLK, :],
                                  start=True, stop=True).then_inc(s["scored"], 1)

                def turn_probs(u):
                    pe.wait_ge(s["probs"], u + 1)
                    if u >= 2:
                        pe.wait_ge(s["pT_d"] if u % 2 == 0 else s["pT_a"], u // 2)
                    for e in range(2):
                        for k in range(TPB):
                            ins = pe.transpose(bank[3 + u % 2][:, (2 * e + k) * P:(2 * e + k + 1) * P],
                                               pr[:, u % 3, e, k * P:(k + 1) * P], w.ident[:])
                    ins.then_inc(s["pT_ps"], 1)

                def weigh_values(g, k):
                    t, blk = divmod(g, SLOTS // BLK)
                    if k == 0:
                        pe.wait_ge(s["pT_d"], 2 * (g + 1))
                        pe.wait_ge(s["pT_a"], 2 * (g + 1))
                        if g == 0:
                            pe.wait_ge(s["rot_dve"], 4)
                        if g == 1:
                            pe.wait_ge(s["turned"], 4)
                        if g >= 2:
                            pe.wait_ge(s["oT"], g - 1)
                    for e in range(2):
                        ins = pe.matmul(bank[5 + g % 2][64 * e:64 * e + 64, :], v[:, t // TPB * TPB + k, 2 * blk + e, :],
                                        pT[:, g % 2, e, k].rearrange("p r q -> p (r q)"),
                                        start=(k == 0), stop=(k == TPB - 1))
                    if k == TPB - 1:
                        ins.then_inc(s["pv"], 1)

                def project_out(t):
                    pe.wait_ge(s["oT"], 2 * (t + 1))
                    pe.wait_ge(s["turned"], min(NJOBS, 2 * (t + 4)))
                    if t >= 1:
                        pe.wait_ge(s["x_new"], t)
                    for j in range(SLOTS):
                        ins = pe.matmul(bank[7][:, 0:D], oT[:, j, :], w.wo_a[:, j, :],
                                        start=(j == 0), stop=(j == SLOTS - 1))
                    ins.then_inc(s["wo"], 1)

                pe.wait_ge(s["xT"], 1)
                project_keys(0)
                project(1)
                project(2)
                project_keys(3)
                project_values(0)
                project_values(1)
                for n in range(3):
                    turn(n)
                for i in range(STEPS):
                    if i < NU:
                        scores(i)
                    if 3 <= i < NU + 3:
                        turn_probs(i - 3)
                    if i >= 7 and (i - 7) // BLK < NU // BLK and (i - 7) % BLK % 2 == 0:
                        weigh_values((i - 7) // BLK, (i - 7) % BLK // 2)
                    if i >= 16 and i % SLOTS == 0:
                        project_out(i // SLOTS - 2)
                    if i == 1:
                        turn(3)
                    if job_at(i, PROJECT_AT) is not None:
                        project(job_at(i, PROJECT_AT))
                    if job_at(i, TURN_AT) is not None:
                        turn(job_at(i, TURN_AT))
                pe.wait_ge(s["shifted_scores"], 2 * NU)
                keep_clock(pe, w, bank[0], 4)

            @block.scalar
            def _(act):
                act.wait_ge(s["var_ready"], NT)
                nc.scalar.activation(w.std[:], w.mean_var[:, :, 1], ACT.Sqrt, bias=w.eps_t[:, 0:1]).then_inc(s["std_ready"], 1)
                nc.scalar.activation(table[:], w.eps_t[:], ACT.Exp)
                act.wait_ge(s["xT_ps"], NT)
                nc.scalar.copy(xT[:].rearrange("p t k -> p (t k)"), bank[6][:]).then_inc(s["xT"], 1)

                def values(b):
                    act.wait_ge(s["v_ps"], b + 1)
                    nc.scalar.copy(v[:, b * TPB:(b + 1) * TPB].rearrange("p t h d -> p (t h d)"),
                                   bank[2 + b][:]).then_inc(s["v_sb"], 1)

                def turned(n):
                    t, c = queries_of(n)
                    act.wait_ge(s["turned_ps"], n + 1)
                    if is_keys(n):
                        nc.scalar.copy(kT[:, key_sequence(n)].rearrange("p g (t k) -> p t g k", t=TPB),
                                       turn_bank(n)[:].rearrange("p (t g k) -> p t g k", t=TPB, g=2)).then_inc(s["turned"], 1)
                        return
                    if t >= 2:
                        act.wait_ge(s["scored"], 2 * SLOTS * (t - 1))
                    nc.scalar.copy(qT[:, t % 2, BLK * c:BLK * (c + 1), :].rearrange("p j k -> p (j k)"),
                                   turn_bank(n)[:]).then_inc(s["turned"], 1)

                values(0)
                values(1)
                for n in range(3):
                    turned(n)

                def exps(u):
                    if u >= 2:
                        act.wait_ge(s["probs"], u - 1)
                    for e in range(2):
                        act.wait_ge(s["shifted_scores"], 2 * u + e + 1)
                        nc.scalar.activation(ex[:, u % 2, e, :], sc[:, u % 2, e, :], ACT.Exp, bias=neg_max[:, u, e:e + 1],
                                             scale=-1.0, accum_out=total[:, u, e:e + 1]).then_inc(s["exps"], 1)

                def turned_probs(u):
                    act.wait_ge(s["pT_ps"], u + 1)
                    if u // BLK >= 2:
                        act.wait_ge(s["pv"], u // BLK - 1)
                    nc.scalar.copy(pT[:, u // BLK % 2, :, :, u % BLK, :],
                                   bank[3 + u % 2][:].rearrange("p (e k q) -> p e k q", e=2, k=TPB)).then_inc(s["pT_a"], 1)

                def turned_out(g):
                    t, blk = divmod(g, SLOTS // BLK)
                    act.wait_ge(s["pv"], g + 1)
                    if t >= 1:
                        act.wait_ge(s["wo"], t)
                    nc.scalar.copy(oT[:, BLK * blk:BLK * (blk + 1), :].rearrange("p j k -> p (j k)"),
                                   bank[5 + g % 2][:]).then_inc(s["oT"], 1)

                for i in range(STEPS):
                    if i >= 10 and (i - 10) % BLK == 0 and (i - 10) // BLK < NU // BLK:
                        turned_out((i - 10) // BLK)
                    if i < NU:
                        exps(i)
                    if 3 <= i < NU + 3 and (i - 3) % 2 == 1:
                        turned_probs(i - 3)
                    if job_at(i, TURN_AT) is not None:
                        turned(job_at(i, TURN_AT))
                    if i == 1:
                        turned(3)
                act.wait_ge(s["var2"], NT)
                nc.scalar.activation(w.std[:], w.mean_var[:, :, 1], ACT.Sqrt, bias=w.eps_t[:, 0:1]).then_inc(s["std2"], 1)

            @block.vector
            def _(dve):
                st = Steps(dve, s["dve"])
                layer_norm_stats(nc, dve, st, w, range(NT), w.x, s, s["var_ready"])
                dve.wait_ge(s["std_ready"], 1)
                k = st.did(nc.vector.reciprocal(w.rstd[:], w.std[:]))
                st.wait(k)
                for t in range(NT):
                    nc.vector.tensor_scalar(xn[:, t, :], w.x[:, t, :], w.mean_var[:, t, 0:1], w.rstd[:, t:t + 1],
                                            ALU.subtract, ALU.mult).then_inc(s["normed"], 1)

                def rotate(n):
                    dve.wait_ge(s["proj"], n + 1)
                    if n >= 2:
                        dve.wait_ge(s["rot_pool"], n - 1)
                    parts = [(i, KW * i, HKV) for i in range(TPB)] if is_keys(n) \
                        else [(queries_of(n)[0] % TPB, 0, CH // DH)]
                    for at, lo, heads in parts:
                        hi = lo + heads * DH
                        src = proj_bank(n)[:, lo:hi].rearrange("p (h d) -> p h d", h=heads)
                        swapped = proj_bank(n)[:, lo:hi].rearrange("p (h s d) -> p h s d", h=heads, s=2)[:, :, ::-1, :]
                        cos = w.rope_a[:, at, 0, :].unsqueeze(1).broadcast_to((P, heads, DH))
                        sin = w.rope_a[:, at, 1, :].rearrange("p (s d) -> p s d", s=2).unsqueeze(1)\
                            .broadcast_to((P, heads, 2, DH // 2))
                        st.did(nc.vector.tensor_tensor(
                            r1[:, n % 2, lo:hi].rearrange("p (h d) -> p h d", h=heads), src, cos, ALU.mult))
                        ins = nc.vector.tensor_tensor(
                            r2[:, n % 2, lo:hi].rearrange("p (h s d) -> p h s d", h=heads, s=2), swapped, sin, ALU.mult)
                        if hi < CH:
                            st.did(ins)
                    ins.then_inc(s["rot_dve"], 1)

                for n in range(3):
                    rotate(n)

                def shift_scores(u):
                    t, j = divmod(u, SLOTS)
                    if u >= 2:
                        dve.wait_ge(s["exps"], 2 * (u - 1))
                    for e in range(2):
                        dve.wait_ge(s["scored"], 2 * u + e + 1)
                        nc.vector.tensor_tensor_reduce(
                            out=sc[:, u % 2, e, :], in0=bank[(2 * u + e) % 3][:, 0:T],
                            in1=w.bias_a[:, t % TPB, slot_head(j, e), :], scale=-1.0 / 8.0, scalar=3e38,
                            op0=ALU.add, op1=ALU.min, accum_out=neg_max[:, u, e:e + 1]).then_inc(s["shifted_scores"], 1)

                def turned_probs(u):
                    dve.wait_ge(s["pT_ps"], u + 1)
                    if u // BLK >= 2:
                        dve.wait_ge(s["pv"], u // BLK - 1)
                    nc.vector.tensor_copy(pT[:, u // BLK % 2, :, :, u % BLK, :],
                                          bank[3 + u % 2][:].rearrange("p (e k q) -> p e k q", e=2, k=TPB)).then_inc(s["pT_d"], 1)

                def residual(t):
                    dve.wait_ge(s["wo"], t + 1)
                    nc.vector.tensor_tensor(w.x[:, t, :], w.x[:, t, :], bank[7][:, 0:D], ALU.add).then_inc(s["x_new"], 1)
                    dve.wait_ge(s["x_new"], t + 1)
                    return st.did(nc.vector.bn_stats(w.stats[:, t, 0, :], w.x[:, t, :]))

                for i in range(STEPS):
                    if i < NU:
                        shift_scores(i)
                    if 1 <= i <= NU:
                        dve.wait_ge(s["exps"], 2 * i)
                        nc.vector.reciprocal(inv[:, i - 1, :], total[:, i - 1, :]).then_inc(s["inverse"], 1)
                    if 3 <= i < NU + 3 and (i - 3) % 2 == 0:
                        turned_probs(i - 3)
                    if i >= 16 and i % SLOTS == 0:
                        k = residual(i // SLOTS - 2)
                    if job_at(i, PROJECT_AT) is not None:
                        rotate(job_at(i, PROJECT_AT))
                    if i == 0:
                        rotate(3)
                st.wait(k)
                for t in range(NT):
                    nc.vector.bn_aggr(w.mean_var[:, t, :], w.stats[:, t, 0, :]).then_inc(s["var2"], 1)
                dve.wait_ge(s["std2"], 1)
                k = st.did(nc.vector.reciprocal(w.rstd[:], w.std[:]))
                st.wait(k)
                for t in range(NT):
                    st.did(nc.vector.tensor_scalar(w.y[:, t, :], w.x[:, t, :], w.mean_var[:, t, 0:1], w.rstd[:, t:t + 1],
                                                   ALU.subtract, ALU.mult))

            @block.gpsimd
            def _(pool):
                def rotated(n):
                    pool.wait_ge(s["rot_dve"], n + 1)
                    if n >= 2:
                        pool.wait_ge(s["turned_ps"], n - 1)
                    dst, one, two = qk[:, n % 2, :], r1[:, n % 2, :], r2[:, n % 2, :]
                    if not is_keys(n):
                        dst = dst.rearrange("p (r e d) -> p r e d", r=BLK, e=2)
                        one, two = (z.rearrange("p (e r d) -> p r e d", r=BLK, e=2) for z in (one, two))
                    nc.gpsimd.tensor_tensor(dst, one, two, ALU.add).then_inc(s["rot_pool"], 1)

                def normalise(u):
                    pool.wait_ge(s["inverse"], u + 1)
                    if u >= 3:
                        pool.wait_ge(s["pT_ps"], u - 2)
                    nc.gpsimd.tensor_tensor(pr[:, u % 3], ex[:, u % 2], inv[:, u, :].unsqueeze(2).broadcast_to((P, 2, T)),
                                            ALU.mult).then_inc(s["probs"], 1)

                for n in range(3):
                    rotated(n)
                for i in range(NU):
                    if i >= 1:
                        normalise(i - 1)
                    if job_at(i, PROJECT_AT) is not None:
                        rotated(job_at(i, PROJECT_AT))
                    if i == 0:
                        rotated(3)
                normalise(NU - 1)
        clear(nc, s)


def local_layer(nc, w, layer, name):
    with ExitStack() as ctx:
        def sb(n, shape):
            return ctx.enter_context(nc.sbuf_tensor(f"{name}_{n}", shape, F32))

        s = signals(nc, ctx, name, "dve pool yT_ps hT_a hT_d edge_zero qk_proj v_proj squared summed norm rn rot_dve "
                                   "rot_pool qT_ps kT_ps qT kT v_sb ones scored shifted_scores probs pT_ps pT pv o_sb "
                                   "oT_ps oT wo y_attn shifted var_ready std_ready normed nT_ps hnT w1 gated_in "
                                   "gelu gated gT_ps gT w2 y_new y_bias pad")
        table = sb("table", [P, 1])
        hT = sb("hT", [P, NB, T])
        sq = sb("sq", [P, 2, 2, INNER])
        ss, norm, rn = sb("ss", [P, NT, 2, HL]), sb("norm", [P, NT, 2, HL]), sb("rn", [P, NT, 2, HL])
        r1, r2 = sb("r1", [P, 2, 2, INNER]), sb("r2", [P, 2, 2, INNER])
        qk = sb("qk", [P, 2, 2, INNER])
        kr = sb("kr", [P, 2, INNER])
        qT = sb("qT", [P, NT, PAIRH, P])
        kT = sb("kT", [P, NB, PAIRH, T])
        v = sb("v", [P, NB, VSETS, HL, DH + 1])
        NU = NT * 2
        sc, pr, pT = sb("sc", [P, 2, 4, P]), sb("pr", [P, 2, 4, P]), sb("pT", [P, 2, 4, P])
        neg_max, rsum = sb("neg_max", [P, NU, 4]), sb("rsum", [P, NU, 4])
        o = sb("o", [P, NT, INNER])
        oT = sb("oT", [P, 2, PAIRH, P])
        old1, old2 = (z[:].rearrange("p a b c -> p (a b c)") for z in (r1, r2))
        gin, ain, gel = (old1[:, 2 * HID * i:2 * HID * (i + 1)].rearrange("p (a b) -> p a b", a=2) for i in range(3))
        n = old2[:, 0:NT * D].rearrange("p (t d) -> p t d", t=NT)
        hnT = old2[:, NT * D:2 * NT * D].rearrange("p (t d) -> p t d", t=NT)
        gT = old2[:, 2 * NT * D:2 * NT * D + 2 * HIDT * P].rearrange("p (a k q) -> p a k q", a=2, k=HIDT)
        gated = sb("gated", [P, 2, HIDT * P])
        yb = sb("yb", [P, NT, D])
        lgb = sb("lgb", [P, 2, 1])
        lg, lb = lgb[:, 0, :], lgb[:, 1, :]
        tab = sb("tab", [P, 2, TPB, 2, DH])
        b1 = sb("b1", [P, 2 * HID])
        bank = [ctx.enter_context(nc.psum_tensor(f"{name}_bank{i}", [P, 512], F32)) for i in range(8)]

        with nc.Block() as block:
            @block.tensor
            def _(pe):
                for b in range(NB):
                    for i in range(TPB):
                        ins = pe.transpose(bank[6 + b][:, i * P:(i + 1) * P], w.y[:, b * TPB + i, :], w.ident[:])
                    ins.then_inc(s["yT_ps"], 1)
                keep_clock(pe, w, bank[0], 1)

                def project(t):
                    b, i = divmod(t, TPB)
                    if i == 0:
                        pe.wait_ge(s["hT_a"], b + 1)
                        pe.wait_ge(s["hT_d"], b + 1)
                        pe.wait_ge(s["edge_zero"], 1)
                    if t >= 2:
                        pe.wait_ge(s["rot_dve"], 2 * (t - 1))
                        pe.wait_ge(s["squared"], 2 * (t - 1))
                    for c in range(2):
                        pe.matmul(bank[2 * (t % 2) + c][:], hT[:, b, i * P:(i + 1) * P],
                                  w.wqkv_l[:, bass.ds(layer, 1), INNER * c:INNER * (c + 1)],
                                  start=True, stop=True).then_inc(s["qk_proj"], 1)

                def project_values(r):
                    b, i = divmod(r, VSETS)
                    if r >= 2:
                        pe.wait_ge(s["v_sb"], r - 1)
                    pe.matmul(bank[4 + r % 2][:], hT[:, b, i * WIN:i * WIN + P],
                              w.wqkv_l[:, bass.ds(layer, 1), 2 * INNER:3 * INNER],
                              start=True, stop=True).then_inc(s["v_proj"], 1)

                def turn(t):
                    if t == 0:
                        pe.wait_ge(s["hT_a"], NB)
                        pe.wait_ge(s["hT_d"], NB)
                        keep_clock(pe, w, bank[6], 2)
                    for c, ready, copied, ps in ((0, s["rot_pool"], s["qT"], s["qT_ps"]), (1, s["rot_pool"], s["kT"], s["kT_ps"])):
                        pe.wait_ge(ready, 2 * t + c + 1)
                        if t >= 1:
                            pe.wait_ge(copied, t)
                        for i in range(PAIRH):
                            ins = pe.transpose(bank[6 + c][:, i * P:(i + 1) * P],
                                               qk[:, t % 2, c, i * P:(i + 1) * P], w.ident[:])
                        ins.then_inc(ps, 1)

                def scores(u):
                    t, e = divmod(u, 2)
                    b, i = divmod(t, TPB)
                    if u == 0:
                        pe.wait_ge(s["rot_dve"], 2 * (NT - 1))
                        pe.wait_ge(s["squared"], 2 * (NT - 1))
                    if u >= 2:
                        pe.wait_ge(s["shifted_scores"], 4 * (u - 1))
                    pe.wait_ge(s["qT"], t + 1)
                    pe.wait_ge(s["kT"], t + 1)
                    for c in range(4):
                        h = 2 * c + e
                        rows = slice(64 * e, 64 * e + 64)
                        for half in range(2):
                            k0 = first_key(i, half)
                            ins = pe.matmul(bank[u % 2][64 * half:64 * half + 64, c * P:(c + 1) * P],
                                            qT[rows, t, h // 2, 64 * half:64 * half + 64],
                                            kT[rows, b, h // 2, k0:k0 + P], start=True, stop=True)
                    ins.then_inc(s["scored"], 1)

                def turn_probs(u):
                    if u == 0:
                        pe.wait_ge(s["rot_dve"], 2 * NT)
                        pe.wait_ge(s["squared"], 2 * NT)
                    pe.wait_ge(s["probs"], 4 * (u + 1))
                    if u >= 2:
                        pe.wait_ge(s["pT"], u - 1)
                    for c in range(4):
                        ins = pe.transpose(bank[2 + u % 2][:, c * P:(c + 1) * P], pr[:, u % 2, c, :], w.ident[:])
                    ins.then_inc(s["pT_ps"], 1)

                def weigh_values(u):
                    t, e = divmod(u, 2)
                    b, i = divmod(t, TPB)
                    if u == 0:
                        pe.wait_ge(s["v_sb"], NB * VSETS)
                        pe.wait_ge(s["ones"], 1)
                    pe.wait_ge(s["pT"], u + 1)
                    if u >= 2:
                        pe.wait_ge(s["o_sb"], u - 1)
                    for c in range(4):
                        h = 2 * c + e
                        for half in range(2):
                            ins = pe.matmul(bank[4 + u % 2][64 * half:64 * half + 64, c * (DH + 1):(c + 1) * (DH + 1)],
                                            pT[:, u % 2, c, 64 * half:64 * half + 64],
                                            v[:, b, first_key(i, half) // WIN, h, :], start=True, stop=True)
                    ins.then_inc(s["pv"], 1)

                def turn_out(t):
                    pe.wait_ge(s["o_sb"], 2 * t + 2)
                    if t == 0:
                        pe.wait_ge(s["qT"], NT)
                        pe.wait_ge(s["kT"], NT)
                    if t >= 1:
                        pe.wait_ge(s["oT"], t)
                    for i in range(PAIRH):
                        ins = pe.transpose(bank[6][:, i * P:(i + 1) * P], o[:, t, i * P:(i + 1) * P], w.ident[:])
                    ins.then_inc(s["oT_ps"], 1)

                def project_out(t):
                    pe.wait_ge(s["oT"], t + 1)
                    if t >= 1:
                        pe.wait_ge(s["y_attn"], t)
                    for i in range(PAIRH):
                        ins = pe.matmul(bank[7][:, 0:D], oT[:, t % 2, i, :], w.wo_l[:, bass.ds(layer, 1), i, :],
                                        start=(i == 0), stop=(i == PAIRH - 1))
                    ins.then_inc(s["wo"], 1)

                def shift(b):
                    t = b * TPB
                    pe.wait_ge(s["y_attn"], t + 2)
                    pe.wait_ge(s["shifted_scores"], 4 * (NU - 1 + b))
                    dst = bank[b][:, 0:TPB * HALF].rearrange("p (i d) -> p i d", i=TPB)
                    pe.matmul(dst, w.shift_m[:], w.y[:, t:t + TPB, HALF:D], start=True, stop=False)
                    pe.matmul(dst[:, 1], w.edge_m[:], w.y[:, t, HALF:D], start=False, stop=True).then_inc(s["shifted"], 1)

                def turn_normed(b):
                    pe.wait_ge(s["normed"], 4 * (b + 1))
                    if b == 0:
                        pe.wait_ge(s["pT"], NU - 1)
                    else:
                        pe.wait_ge(s["oT"], NT)
                    for i in range(TPB):
                        ins = pe.transpose(bank[2 + 4 * b][:, i * P:(i + 1) * P], n[:, b * TPB + i, :], w.ident[:])
                    ins.then_inc(s["nT_ps"], 1)

                def widen(t):
                    pe.wait_ge(s["hnT"], t // TPB + 1)
                    if t == 0:
                        pe.wait_ge(s["pT"], NU)
                        pe.wait_ge(s["o_sb"], NU)
                    if t >= 2:
                        pe.wait_ge(s["gated_in"], 2 * (t - 1))
                    for c in (1, 0):
                        pe.matmul(bank[2 + 2 * (t % 2) + c][:, 0:HID], hnT[:, t, :],
                                  w.w1_l[:, bass.ds(layer, 1), HID * c:HID * (c + 1)],
                                  start=True, stop=True).then_inc(s["w1"], 1)

                def turn_gated(t):
                    pe.wait_ge(s["gated"], t + 1)
                    if t == 0:
                        pe.wait_ge(s["pad"], 2)
                        pe.wait_ge(s["normed"], 4 * NB)
                    if t >= 2:
                        pe.wait_ge(s["gT"], t - 1)
                    for i in range(HIDT):
                        ins = pe.transpose(bank[t % 2][:, i * P:(i + 1) * P], gated[:, t % 2, i * P:(i + 1) * P], w.ident[:])
                    ins.then_inc(s["gT_ps"], 1)

                def narrow(t):
                    pe.wait_ge(s["gT"], t + 1)
                    if t == 0:
                        pe.wait_ge(s["y_attn"], NT)
                    if t >= 1:
                        pe.wait_ge(s["y_new"], t)
                    for i in range(HIDT):
                        ins = pe.matmul(bank[7][:, 0:D], gT[:, t % 2, i, :], w.w2_l[:, bass.ds(layer, 1), i, :],
                                        start=(i == 0), stop=(i == HIDT - 1))
                    ins.then_inc(s["w2"], 1)

                project(0)
                project(1)
                for r in range(3):
                    project_values(r)
                turn(0)
                project(2)
                turn(1)
                project(3)
                for r in range(3, 6):
                    project_values(r)
                turn(2)
                for i in range(NU + 4):
                    if i == 3:
                        turn(3)
                    if i < NU:
                        scores(i)
                    if i == 1:
                        pe.wait_ge(s["rot_dve"], 2 * NT)
                        pe.wait_ge(s["squared"], 2 * NT)
                        keep_clock(pe, w, bank[3], 2)
                    if 1 <= i <= NU:
                        turn_probs(i - 1)
                    if 2 <= i <= NU + 1:
                        weigh_values(i - 2)
                    if i >= 4 and i % 2 == 0:
                        turn_out((i - 4) // 2)
                    if i >= 5 and i % 2 == 1:
                        project_out((i - 5) // 2)
                    if i == 8:
                        shift(0)
                    if i == 10:
                        turn_normed(0)

                shift(1)
                widen(0)
                widen(1)
                turn_normed(1)
                turn_gated(0)
                widen(2)
                narrow(0)
                turn_gated(1)
                widen(3)
                narrow(1)
                turn_gated(2)
                narrow(2)
                turn_gated(3)
                narrow(3)

            @block.scalar
            def _(act):
                nc.scalar.activation(table[:], w.eps_t[:], ACT.Sqrt)
                for b in range(NB):
                    act.wait_ge(s["yT_ps"], b + 1)
                    nc.scalar.copy(hT[0:HALF, b, :], bank[6 + b][0:HALF, 0:T]).then_inc(s["hT_a"], 1)

                def squares(t):
                    if t >= 2:
                        act.wait_ge(s["summed"], 2 * (t - 1))
                    for c in range(2):
                        act.wait_ge(s["qk_proj"], 2 * t + c + 1)
                        nc.scalar.activation(sq[:, t % 2, c, :], bank[2 * (t % 2) + c][:], ACT.Square).then_inc(s["squared"], 1)

                def root(t):
                    act.wait_ge(s["summed"], 2 * (t + 1))
                    nc.scalar.activation(norm[:, t], ss[:, t], ACT.Sqrt).then_inc(s["norm"], 1)

                def values(r):
                    b, i = divmod(r, VSETS)
                    act.wait_ge(s["v_proj"], r + 1)
                    nc.scalar.copy(v[:, b, i, :, 0:DH], bank[4 + r % 2][:].rearrange("p (h d) -> p h d", h=HL)
                                   ).then_inc(s["v_sb"], 1)

                def turned(t):
                    b, i = divmod(t, TPB)
                    act.wait_ge(s["qT_ps"], t + 1)
                    nc.scalar.copy(qT[:, t].rearrange("p j k -> p (j k)"), bank[6][:]).then_inc(s["qT"], 1)
                    act.wait_ge(s["kT_ps"], t + 1)
                    nc.scalar.copy(kT[:, b, :, i * P:(i + 1) * P], bank[7][:].rearrange("p (j k) -> p j k", j=PAIRH)
                                   ).then_inc(s["kT"], 1)

                def exps(u):
                    if u >= 2:
                        act.wait_ge(s["pT_ps"], u - 1)
                    for c in range(4):
                        act.wait_ge(s["shifted_scores"], 4 * u + c + 1)
                        nc.scalar.activation(pr[:, u % 2, c, :], sc[:, u % 2, c, :], ACT.Exp,
                                             bias=neg_max[:, u, c:c + 1], scale=-1.0).then_inc(s["probs"], 1)

                def turned_out(t):
                    act.wait_ge(s["oT_ps"], t + 1)
                    if t >= 2:
                        act.wait_ge(s["wo"], t - 1)
                    nc.scalar.copy(oT[:, t % 2].rearrange("p j k -> p (j k)"), bank[6][:]).then_inc(s["oT"], 1)

                def deviation(b):
                    act.wait_ge(s["var_ready"], TPB * (b + 1))
                    ts = slice(b * TPB, (b + 1) * TPB)
                    nc.scalar.activation(w.std[:, ts], w.mean_var[:, ts, 1], ACT.Sqrt,
                                         bias=w.eps_t[:, 0:1]).then_inc(s["std_ready"], 1)

                def affine(b):
                    act.wait_ge(s["nT_ps"], b + 1)
                    nc.scalar.activation(hnT[:, b * TPB:(b + 1) * TPB, :].rearrange("p t k -> p (t k)"),
                                         bank[2 + 4 * b][:, 0:T], ACT.Identity, bias=lb[:, 0:1],
                                         scale=lg[:, 0:1]).then_inc(s["hnT"], 1)

                def gelu(t):
                    act.wait_ge(s["gated_in"], 2 * t + 1)
                    if t >= 2:
                        act.wait_ge(s["gated"], t - 1)
                    nc.scalar.activation(gel[:, t % 2, :], gin[:, t % 2, :], ACT.Gelu).then_inc(s["gelu"], 1)

                def turned_gated(t):
                    act.wait_ge(s["gT_ps"], t + 1)
                    if t >= 2:
                        act.wait_ge(s["w2"], t - 1)
                    nc.scalar.copy(gT[:, t % 2].rearrange("p j k -> p (j k)"), bank[t % 2][:, 0:HIDT * P]).then_inc(s["gT"], 1)

                squares(0)
                squares(1)
                root(0)
                values(0)
                values(1)
                root(1)
                values(2)
                turned(0)
                squares(2)
                root(2)
                turned(1)
                squares(3)
                values(3)
                root(3)
                values(4)
                values(5)
                turned(2)
                for i in range(NU + 4):
                    if i == 3:
                        turned(3)
                    if i < NU:
                        exps(i)
                    if i >= 4 and i % 2 == 0:
                        turned_out((i - 4) // 2)
                    if i == 8:
                        deviation(0)
                    if i == 10:
                        act.wait_ge(s["pad"], 2)
                        affine(0)
                deviation(1)
                gelu(0)
                affine(1)
                gelu(1)
                turned_gated(0)
                gelu(2)
                turned_gated(1)
                gelu(3)
                turned_gated(2)
                turned_gated(3)

            @block.vector
            def _(dve):
                st = Steps(dve, s["dve"])
                k0 = st.did(nc.vector.tensor_copy(tab[:].rearrange("p i t c d -> p (i t c d)"),
                                                  w.rot_l[:, bass.ds(layer, 1)].rearrange("p l i t c d -> p (l i t c d)")))
                for b in range(NB):
                    dve.wait_ge(s["yT_ps"], b + 1)
                    nc.vector.tensor_copy(hT[HALF:P, b, 1:T], bank[6 + b][HALF:P, 0:T - 1]).then_inc(s["hT_d"], 1)
                st.wait(k0)

                def rotate(t):
                    i = t % TPB
                    if t >= 2:
                        dve.wait_ge(s["rot_pool"], 2 * (t - 1))
                    for c in range(2):
                        dve.wait_ge(s["squared"], 2 * t + c + 1)
                        nc.vector.tensor_reduce(ss[:, t, c, :], sq[:, t % 2, c, :].rearrange("p (h d) -> p h d", h=HL),
                                                AX.X, ALU.add).then_inc(s["summed"], 1)
                    for c in range(2):
                        ps = bank[2 * (t % 2) + c][:]
                        st.did(nc.vector.tensor_tensor(
                            r1[:, t % 2, c, :].rearrange("p (h d) -> p h d", h=HL), ps.rearrange("p (h d) -> p h d", h=HL),
                            tab[:, c, i, 0, :].unsqueeze(1).broadcast_to((P, HL, DH)), ALU.mult))
                        nc.vector.tensor_tensor(
                            r2[:, t % 2, c, :].rearrange("p (h s d) -> p h s d", h=HL, s=2),
                            ps.rearrange("p (h s d) -> p h s d", h=HL, s=2)[:, :, ::-1, :],
                            tab[:, c, i, 1, :].rearrange("p (s d) -> p s d", s=2).unsqueeze(1)
                            .broadcast_to((P, HL, 2, DH // 2)), ALU.mult).then_inc(s["rot_dve"], 1)
                        if c == 0:
                            dve.wait_ge(s["norm"], t + 1)
                            k = st.did(nc.vector.tensor_scalar(norm[:, t], norm[:, t], 1e-12, None, ALU.max))
                            st.wait(k)
                            nc.vector.reciprocal(rn[:, t], norm[:, t]).then_inc(s["rn"], 1)

                for t in range(NT):
                    rotate(t)

                def shift_scores(u):
                    t, e = divmod(u, 2)
                    if u == 0:
                        dve.wait_ge(s["rn"], NT)
                    if u >= 2:
                        dve.wait_ge(s["probs"], 4 * (u - 1))
                    dve.wait_ge(s["scored"], u + 1)
                    for c in range(4):
                        nc.vector.tensor_tensor_reduce(
                            out=sc[:, u % 2, c, :], in0=bank[u % 2][:, c * P:(c + 1) * P], in1=w.mask_l[:, t % TPB, :],
                            scale=rn[:, t, 0, 2 * c + e:2 * c + e + 1], scalar=3e38, op0=ALU.add, op1=ALU.min,
                            accum_out=neg_max[:, u, c:c + 1]).then_inc(s["shifted_scores"], 1)

                def turned_probs(u):
                    dve.wait_ge(s["pT_ps"], u + 1)
                    if u >= 2:
                        dve.wait_ge(s["pv"], u - 1)
                    nc.vector.tensor_copy(pT[:, u % 2].rearrange("p c q -> p (c q)"), bank[2 + u % 2][:]).then_inc(s["pT"], 1)

                def normalise(u):
                    t, e = divmod(u, 2)
                    dve.wait_ge(s["pv"], u + 1)
                    src = bank[4 + u % 2][:, 0:4 * (DH + 1)].rearrange("p (c d) -> p c d", c=4)
                    k = st.did(nc.vector.reciprocal(rsum[:, u, :], src[:, :, DH]))
                    st.wait(k)
                    nc.vector.tensor_tensor(
                        o[:, t, :].rearrange("p (c e d) -> p c e d", c=4, e=2)[:, :, e, :], src[:, :, 0:DH],
                        rsum[:, u, :].unsqueeze(2).broadcast_to((P, 4, DH)), ALU.mult).then_inc(s["o_sb"], 1)

                def residual(t):
                    dve.wait_ge(s["wo"], t + 1)
                    nc.vector.tensor_tensor(w.y[:, t, :], w.y[:, t, :], bank[7][:, 0:D], ALU.add).then_inc(s["y_attn"], 1)

                def statistics(b):
                    dve.wait_ge(s["y_attn"], TPB * (b + 1))
                    for i in range(TPB):
                        t = b * TPB + i
                        st.did(nc.vector.bn_stats(w.stats[:, t, 0, :], w.y[:, t, 0:HALF]))
                    dve.wait_ge(s["shifted"], b + 1)
                    for i in range(TPB):
                        t = b * TPB + i
                        k = st.did(nc.vector.bn_stats(w.stats[:, t, 1, :], bank[b][:, i * HALF:(i + 1) * HALF]))
                    st.wait(k)
                    for i in range(TPB):
                        t = b * TPB + i
                        nc.vector.bn_aggr(w.mean_var[:, t, :], w.stats[:, t].rearrange("p a b -> p (a b)")
                                          ).then_inc(s["var_ready"], 1)

                def normed(b):
                    ts = slice(b * TPB, (b + 1) * TPB)
                    if b == 0:
                        dve.wait_ge(s["rot_pool"], 2 * NT)
                    dve.wait_ge(s["std_ready"], b + 1)
                    k = st.did(nc.vector.reciprocal(w.rstd[:, ts], w.std[:, ts]))
                    st.wait(k)
                    for i in range(TPB):
                        t = b * TPB + i
                        for c, src in ((0, w.y[:, t, 0:HALF]), (1, bank[b][:, i * HALF:(i + 1) * HALF])):
                            nc.vector.tensor_scalar(n[:, t, c * HALF:(c + 1) * HALF], src, w.mean_var[:, t, 0:1],
                                                    w.rstd[:, t:t + 1], ALU.subtract, ALU.mult).then_inc(s["normed"], 1)

                def gate_in(t):
                    if t == 0:
                        dve.wait_ge(s["pad"], 2)
                    if t >= 2:
                        dve.wait_ge(s["gelu"], t - 1)
                        dve.wait_ge(s["gated"], t - 1)
                    dve.wait_ge(s["w1"], 2 * t + 1)
                    nc.vector.tensor_tensor(gin[:, t % 2, :], bank[3 + 2 * (t % 2)][:, 0:HID], b1[:, HID:2 * HID],
                                            ALU.add).then_inc(s["gated_in"], 1)
                    dve.wait_ge(s["w1"], 2 * t + 2)
                    nc.vector.tensor_tensor(ain[:, t % 2, :], bank[2 + 2 * (t % 2)][:, 0:HID], b1[:, 0:HID],
                                            ALU.add).then_inc(s["gated_in"], 1)

                def gate(t):
                    dve.wait_ge(s["gelu"], t + 1)
                    dve.wait_ge(s["gated_in"], 2 * t + 2)
                    if t >= 2:
                        dve.wait_ge(s["gT_ps"], t - 1)
                    nc.vector.tensor_tensor(gated[:, t % 2, 0:HID], ain[:, t % 2, :], gel[:, t % 2, :],
                                            ALU.mult).then_inc(s["gated"], 1)

                def update(t):
                    if t == 0:
                        dve.wait_ge(s["y_bias"], 1)
                    dve.wait_ge(s["w2"], t + 1)
                    nc.vector.tensor_tensor(w.y[:, t, :], yb[:, t, :], bank[7][:, 0:D], ALU.add).then_inc(s["y_new"], 1)

                for i in range(NU + 4):
                    if i < NU:
                        shift_scores(i)
                    if 1 <= i <= NU:
                        turned_probs(i - 1)
                    if 2 <= i <= NU + 1:
                        normalise(i - 2)
                    if i >= 5 and i % 2 == 1:
                        residual((i - 5) // 2)
                    if i == 8:
                        statistics(0)
                    if i == 9:
                        normed(0)
                statistics(1)
                gate_in(0)
                normed(1)
                gate_in(1)
                gate(0)
                gate(1)
                gate_in(2)
                update(0)
                gate(2)
                gate_in(3)
                update(1)
                gate(3)
                update(2)
                update(3)

            @block.gpsimd
            def _(pool):
                nc.gpsimd.memset(hT[HALF:P, :, 0:1], 0.0).then_inc(s["edge_zero"], 1)
                pool.wait_ge(s["edge_zero"], 1)
                nc.gpsimd.memset(v[:, :, :, :, DH:DH + 1], 1.0).then_inc(s["ones"], 1)
                nc.gpsimd.memset(gated[:, :, HID:], 0.0).then_inc(s["pad"], 1)
                nc.gpsimd.tensor_copy(b1[:], w.b1_l[:, bass.ds(layer, 1), :].rearrange("p l n -> p (l n)")).then_inc(s["pool"], 1)
                nc.gpsimd.tensor_copy(lgb[:], w.ln_gb[:, :, bass.ds(layer, 1)]).then_inc(s["pool"], 1)
                pool.wait_ge(s["pool"], 2)
                nc.gpsimd.memset(yb[:], 0.0).then_inc(s["pad"], 1)
                for t in range(NT):
                    for c in range(2):
                        pool.wait_ge(s["rot_dve"], 2 * t + c + 1)
                        if t >= 2:
                            pool.wait_ge(s["qT_ps"] if c == 0 else s["kT_ps"], t - 1)
                        dst = qk[:, t % 2, 0, :] if c == 0 else kr[:, t % 2, :]
                        ins = nc.gpsimd.tensor_tensor(dst, r1[:, t % 2, c, :], r2[:, t % 2, c, :], ALU.add)
                        if c == 0:
                            ins.then_inc(s["rot_pool"], 1)
                            continue
                        ins.then_inc(s["pool"], 1)
                        pool.wait_ge(s["pool"], 3 + t)
                        pool.wait_ge(s["rn"], t + 1)
                        nc.gpsimd.tensor_tensor(
                            qk[:, t % 2, 1, :].rearrange("p (h d) -> p h d", h=HL),
                            kr[:, t % 2, :].rearrange("p (h d) -> p h d", h=HL),
                            rn[:, t, 1, :].unsqueeze(2).broadcast_to((P, HL, DH)), ALU.mult).then_inc(s["rot_pool"], 1)
                pool.wait_ge(s["y_attn"], NT)
                pool.wait_ge(s["pad"], 2)
                nc.gpsimd.tensor_tensor(yb[:], w.y[:], w.b2_l[:, bass.ds(layer, 1), :].broadcast_to((P, NT, D)),
                                        ALU.add).then_inc(s["y_bias"], 1)
        clear(nc, s)


def attention_b(nc, w, pair):
    with ExitStack() as ctx:
        def sb(name, shape):
            return ctx.enter_context(nc.sbuf_tensor("b_" + name, shape, F32))

        s = signals(nc, ctx, "b", "dve x_new var_ready std_ready normed xT_ps xT proj v_ps high low v_sum vd hidden_ps hidden "
                                  "encoded enc_sb turned_ps turned norms nT_ps diag spread weights wT_ps wT vw_ps vw out_ps x_out var2 std2 "
                                  "pool xbo")
        table = sb("table", [P, 1])
        xn, xT = sb("xn", [P, NT, D]), sb("xT", [P, NT * P])
        split = ctx.enter_context(nc.sbuf_tensor("b_split", [P, 2 * GB, NT * P], F32R))
        v_sum, v_mean = sb("v_sum", [P, NB]), sb("v_mean", [P, NB])
        vd = sb("vd", [P, NB, HB])
        hidden = sb("hidden", [P, 8, NT * P])
        UN = 2 * HB
        SET = 4
        SETS = UN // SET
        code = sb("code", [P, 2, NT * P])
        q1 = sb("q1", [P, NT, SET, 2 * NQ])
        e1, e2, e3 = sb("e1", [P, NT, SET, NQ]), sb("e2", [P, NT, SET, NQ]), sb("e3", [P, NT, SET, NQ])
        norms = sb("norms", [P, NT, UN])
        bounds = sb("bounds", [HB, 3, NB])
        kz = sb("kz", [HB, NB, T])
        diag = sb("diag", [HB, 3, NB, HB])
        prod = sb("prod", [P, NT, 2, HB])
        zero, quot = sb("zero", [P, NT, 2, HB]), sb("quot", [P, NT, 2, HB])
        wgt = sb("wgt", [P, NT, HB])
        wT, vw = sb("wT", [HB, NT, P]), sb("vw", [HB, NB, D])
        mix = sb("mix", [P, 2, HB])
        bank = [ctx.enter_context(nc.psum_tensor(f"b_bank{i}", [P, 512], F32)) for i in range(8)]

        with nc.Block() as block:
            @block.tensor
            def _(pe):
                keep_clock(pe, w, bank[0], 4)
                pe.wait_ge(s["normed"], NT)
                for t in range(NT):
                    pe.transpose(bank[3][:, t * P:(t + 1) * P], xn[:, t, :], w.ident[:]).then_inc(s["xT_ps"], 1)
                pe.wait_ge(s["xT"], 1)
                for p in range(2 * GB):
                    pe.matmul(bank[4 + p][:], w.wqk_b[:, p].rearrange("p a b -> p (a b)"), xT[:],
                              start=True, stop=True).then_inc(s["proj"], 1)
                pe.matmul(bank[3][:], w.wv_b[:], xT[:], start=True, stop=True).then_inc(s["v_ps"], 1)

                def hide(v):
                    p, h = divmod(v, HB // GB)
                    if h == 0:
                        pe.wait_ge(s["low"], p + 1)
                        if p < 2:
                            pe.wait_ge(s["high"], p + 1)
                    if v >= 3:
                        pe.wait_ge(s["hidden"], v - 2)
                    for part in range(2):
                        ins = pe.matmul(bank[v % 3][:], w.w1_b[:, part, h, :], split[:, p, :],
                                        start=(part == 0), stop=(part == 1))
                    ins.then_inc(s["hidden_ps"], 1)

                def encode(g):
                    pe.wait_ge(s["hidden"], SET * (g + 1))
                    if g < 2:
                        pe.wait_ge(s["low"], g + 1)
                    else:
                        pe.wait_ge(s["enc_sb"], g - 1)
                    for i in range(SET):
                        ins = pe.matmul(bank[4 + g % 2][32 * i:32 * i + 32, :], w.w2_b[:], hidden[:, (SET * g + i) % 8, :],
                                        start=True, stop=True)
                    ins.then_inc(s["encoded"], 1)

                def turn(g):
                    pe.wait_ge(s["enc_sb"], g + 1)
                    if g < 2:
                        pe.wait_ge(s["low"], g + 3)
                    else:
                        pe.wait_ge(s["turned"], g - 1)
                    for t in range(NT):
                        ins = pe.transpose(bank[6 + g % 2][:, t * P:(t + 1) * P], code[:, g % 2, t * P:(t + 1) * P], w.ident[:])
                    ins.then_inc(s["turned_ps"], 1)

                def values_out():
                    pe.wait_ge(s["vd"], 1)
                    for b in range(NB):
                        ins = pe.matmul(bank[3][0:HB, b * D:(b + 1) * D], vd[:, b, :], w.wo_b[:], start=True, stop=True)
                    ins.then_inc(s["vw_ps"], 1)

                def turn_norms():
                    pe.wait_ge(s["norms"], SETS // 2)
                    pe.wait_ge(s["vw"], 1)
                    for t in range(NT):
                        ins = pe.transpose(bank[3][0:HB, t * P:(t + 1) * P], norms[:, t, 0:HB], w.ident[:])
                    ins.then_inc(s["nT_ps"], 1)

                def spread_bounds():
                    pe.wait_ge(s["diag"], 1)
                    pe.matmul(bank[3][:, 0:3 * NB * HB], w.ones_t[0:HB, :], diag[:].rearrange("p c b h -> p (c b h)"),
                              start=True, stop=True).then_inc(s["spread"], 1)

                for g in range(SETS + 2):
                    if g < SETS:
                        for i in range(SET):
                            hide(SET * g + i)
                    if 2 <= g:
                        turn(g - 2)
                    if 1 <= g <= SETS:
                        encode(g - 1)
                    if g == 3:
                        values_out()
                    if g == 6:
                        turn_norms()
                    if g == 8:
                        spread_bounds()
                keep_clock(pe, w, bank[0], 2)
                pe.wait_ge(s["weights"], 1)
                for t in range(NT):
                    ins = pe.transpose(bank[0][0:HB, t * P:(t + 1) * P], wgt[:, t, :], w.ident[:])
                ins.then_inc(s["wT_ps"], 1)
                keep_clock(pe, w, bank[4], 1)
                pe.wait_ge(s["wT"], 1)
                pe.wait_ge(s["vw"], 1)
                for t in range(NT):
                    ins = pe.matmul(bank[1][:, t * D:(t + 1) * D], wT[:, t, :], vw[:, t // TPB, :], start=True, stop=True)
                ins.then_inc(s["out_ps"], 1)
                keep_clock(pe, w, bank[4], 4)

            @block.scalar
            def _(act):
                act.wait_ge(s["var_ready"], NT)
                nc.scalar.activation(w.std[:], w.mean_var[:, :, 1], ACT.Sqrt, bias=w.eps_t[:, 0:1]).then_inc(s["std_ready"], 1)
                nc.scalar.activation(table[:], w.eps_t[:], ACT.Tanh)
                act.wait_ge(s["xT_ps"], NT)
                nc.scalar.copy(xT[:], bank[3][:]).then_inc(s["xT"], 1)

                def high(p):
                    act.wait_ge(s["proj"], p + 1)
                    nc.scalar.activation(split[:, p, :], bank[4 + p][:], ACT.Identity,
                                         bias=w.bqk_b[:, p:p + 1]).then_inc(s["high"], 1)

                high(0)
                for v in range(UN):
                    act.wait_ge(s["hidden_ps"], v + 1)
                    if v >= 8:
                        act.wait_ge(s["encoded"], v // SET - 1)
                    nc.scalar.activation(hidden[:, v % 8, :], bank[v % 3][:], ACT.Tanh,
                                         bias=w.b1_b[:, 0:1]).then_inc(s["hidden"], 1)
                    if v == 1:
                        high(1)
                    if v == 4 * SET - 1:
                        act.wait_ge(s["vw_ps"], 1)
                        nc.scalar.copy(vw[:].rearrange("p b n -> p (b n)"), bank[3][0:HB, 0:NB * D]).then_inc(s["vw"], 1)
                act.wait_ge(s["wT_ps"], 1)
                nc.scalar.copy(wT[:].rearrange("p t k -> p (t k)"), bank[0][0:HB, :]).then_inc(s["wT"], 1)
                act.wait_ge(s["var2"], NT)
                nc.scalar.activation(w.std[:], w.mean_var[:, :, 1], ACT.Sqrt, bias=w.eps_t[:, 0:1]).then_inc(s["std2"], 1)

            @block.gpsimd
            def _(pool):
                nc.gpsimd.tensor_copy(mix[:].rearrange("p c h -> p (c h)"),
                                      w.mix_b[:, bass.ds(pair, 1)].rearrange("p o c h -> p (o c h)")).then_inc(s["pool"], 1)
                pool.wait_ge(s["x_new"], 1)
                pool.wait_ge(s["normed"], NT)
                nc.gpsimd.tensor_tensor(w.x[:], w.x[:], w.bo_b[:].unsqueeze(1).broadcast_to((P, NT, D)),
                                        ALU.add).then_inc(s["xbo"], 1)

            @block.vector
            def _(dve):
                st = Steps(dve, s["dve"])

                def then(instruction):
                    st.wait(st.did(instruction))

                nc.vector.tensor_tensor(w.x[:], w.x[:], w.y[:], ALU.add).then_inc(s["x_new"], 1)
                dve.wait_ge(s["x_new"], 1)
                layer_norm_stats(nc, dve, st, w, range(NT), w.x, s, s["var_ready"])
                dve.wait_ge(s["std_ready"], 1)
                then(nc.vector.reciprocal(w.rstd[:], w.std[:]))
                for t in range(NT):
                    nc.vector.tensor_scalar(xn[:, t, :], w.x[:, t, :], w.mean_var[:, t, 0:1], w.rstd[:, t:t + 1],
                                            ALU.subtract, ALU.mult).then_inc(s["normed"], 1)

                def low(p):
                    if p < 2:
                        dve.wait_ge(s["high"], p + 1)
                    else:
                        dve.wait_ge(s["proj"], p + 1)
                        then(nc.vector.tensor_scalar(split[:, p, :], bank[4 + p][:], w.bqk_b[:, p:p + 1], None, ALU.add))
                    at = split[HALF:P, p, :]
                    nc.vector.scalar_tensor_tensor(out=at, in0=bank[4 + p][HALF:P, :], scalar=w.bqk_b[HALF:P, p:p + 1],
                                                   in1=at.bitcast(F32), op0=ALU.add, op1=ALU.subtract).then_inc(s["low"], 1)

                low(0)
                dve.wait_ge(s["v_ps"], 1)
                nc.vector.tensor_reduce(v_sum[:], bank[3][:].rearrange("p (b k) -> p b k", b=NB), AX.X, ALU.add)\
                    .then_inc(s["v_sum"], 1)
                low(1)
                low(2)
                low(3)
                dve.wait_ge(s["v_sum"], 1)
                then(nc.vector.tensor_scalar(v_mean[:], v_sum[:], 1.0 / T, w.bv_b[:], ALU.mult, ALU.add))
                for b in range(NB):
                    ins = nc.vector.tensor_scalar(vd[:, b, :], w.head_of[:], v_mean[:, b:b + 1], None, ALU.mult)
                    if b < NB - 1:
                        st.did(ins)
                ins.then_inc(s["vd"], 1)
                dve.wait_ge(s["pool"], 1)

                def codes(g):
                    dve.wait_ge(s["encoded"], g + 1)
                    if g >= 2:
                        dve.wait_ge(s["turned_ps"], g - 1)
                    nc.vector.tensor_copy(code[:, g % 2, :], bank[4 + g % 2][:]).then_inc(s["enc_sb"], 1)

                def squared_norms(g):
                    dve.wait_ge(s["turned_ps"], g + 1)
                    if g >= 1:
                        dve.wait_ge(s["norms"], g)
                    b2 = w.b2_b[:].unsqueeze(1).unsqueeze(1).broadcast_to((P, NT, SET, 2 * NQ))
                    nc.vector.tensor_tensor(q1[:], bank[6 + g % 2][:].rearrange("p (t i n) -> p t i n", t=NT, i=SET)[:, :, :, 0:2 * NQ],
                                            b2, ALU.add).then_inc(s["turned"], 1)
                    dve.wait_ge(s["turned"], g + 1)
                    h = SET * g % HB
                    cos, sin = (mix[:, c, h:h + SET].unsqueeze(1).unsqueeze(3) for c in range(2))
                    st.did(nc.vector.tensor_tensor(e1[:], q1[:, :, :, 0:NQ], cos.broadcast_to((P, NT, SET, NQ)), ALU.mult))
                    for b in range(NB):
                        mine, other = slice(b * TPB, (b + 1) * TPB), slice((1 - b) * TPB, (2 - b) * TPB)
                        k = st.did(nc.vector.tensor_tensor(e2[:, mine], q1[:, other, :, NQ:2 * NQ],
                                                           sin.broadcast_to((P, TPB, SET, NQ)), ALU.mult))
                    st.wait(k)
                    then(nc.vector.tensor_tensor(e3[:], e1[:], e2[:], ALU.add))
                    then(nc.vector.tensor_tensor(e1[:], e3[:], e3[:], ALU.mult))
                    nc.vector.tensor_reduce(norms[:, :, SET * g:SET * (g + 1)], e1[:], AX.X, ALU.add).then_inc(s["norms"], 1)

                def key_bounds():
                    dve.wait_ge(s["nT_ps"], 1)
                    keys = bank[3][0:HB, :].rearrange("p (b k) -> p b k", b=NB)
                    st.did(nc.vector.tensor_reduce(bounds[:, 0, :], keys, AX.X, ALU.min))
                    st.did(nc.vector.tensor_reduce(bounds[:, 1, :], keys, AX.X, ALU.max))
                    then(nc.vector.tensor_scalar(kz[:], keys, 0.0, None, ALU.mult))
                    then(nc.vector.tensor_reduce(bounds[:, 2, :], kz[:], AX.X, ALU.add))
                    for c in range(3):
                        for b in range(NB):
                            ins = nc.vector.tensor_scalar(diag[:, c, b, :], w.ident[0:HB, 0:HB], bounds[:, c, b:b + 1], None, ALU.mult)
                            if (c, b) != (2, NB - 1):
                                st.did(ins)
                    ins.then_inc(s["diag"], 1)

                for g in range(SETS + 1):
                    if g < SETS:
                        codes(g)
                    if g >= 1:
                        squared_norms(g - 1)
                    if g == 5:
                        key_bounds()
                dve.wait_ge(s["norms"], SETS)
                dve.wait_ge(s["spread"], 1)
                spread = bank[3][:, 0:3 * NB * HB].rearrange("p (c b h) -> p c b h", c=3, b=NB)
                for b in range(NB):
                    for c in range(2):
                        queries = norms[:, b * TPB:(b + 1) * TPB, HB:UN]
                        k = st.did(nc.vector.tensor_tensor(prod[:, b * TPB:(b + 1) * TPB, c, :], queries,
                                                           spread[:, c, b, :].unsqueeze(1).broadcast_to((P, TPB, HB)), ALU.mult))
                st.wait(k)
                then(nc.vector.tensor_scalar(zero[:], prod[:], 0.0, 3e38, ALU.is_equal, ALU.mult))
                then(nc.vector.tensor_scalar(zero[:], zero[:], 3e38, 0.0, ALU.mult, ALU.mult))
                then(nc.vector.scalar_tensor_tensor(out=quot[:], in0=prod[:], scalar=0.0, in1=zero[:], op0=ALU.mult, op1=ALU.add))
                then(nc.vector.scalar_tensor_tensor(out=wgt[:], in0=quot[:, :, 0, :], scalar=1.0, in1=quot[:, :, 1, :],
                                                    op0=ALU.add, op1=ALU.add))
                for b in range(NB):
                    ts = slice(b * TPB, (b + 1) * TPB)
                    ins = nc.vector.tensor_tensor(wgt[:, ts, :], wgt[:, ts, :],
                                                  spread[:, 2, b, :].unsqueeze(1).broadcast_to((P, TPB, HB)), ALU.add)
                    if b < NB - 1:
                        st.did(ins)
                ins.then_inc(s["weights"], 1)
                dve.wait_ge(s["out_ps"], 1)
                dve.wait_ge(s["xbo"], 1)
                nc.vector.tensor_tensor(w.x[:], w.x[:], bank[1][:].rearrange("p (t n) -> p t n", t=NT), ALU.add).then_inc(s["x_out"], 1)
                dve.wait_ge(s["x_out"], 1)
                layer_norm_stats(nc, dve, st, w, range(NT), w.x, s, s["var2"])
                dve.wait_ge(s["std2"], 1)
                then(nc.vector.reciprocal(w.rstd[:], w.std[:]))
                for t in range(NT):
                    st.did(nc.vector.tensor_scalar(w.y[:, t, :], w.x[:, t, :], w.mean_var[:, t, 0:1], w.rstd[:, t:t + 1],
                                                   ALU.subtract, ALU.mult))
        clear(nc, s)


def store(nc, w, pair, x, out):
    with ExitStack() as ctx:
        s = signals(nc, ctx, "store", "summed stored loaded")
        result = ctx.enter_context(nc.sbuf_tensor("result", [P, NT, D], F32))
        bank = ctx.enter_context(nc.psum_tensor("store_bank", [P, 512], F32))
        with nc.Block() as block:
            @block.tensor
            def _(pe):
                keep_clock(pe, w, bank, 4)

            @block.vector
            def _(dve):
                nc.vector.tensor_tensor(result[:], w.x[:], w.y[:], ALU.add).then_inc(s["summed"], 1)

            @block.scalar
            def _(act):
                act.wait_ge(s["summed"], 1)
                act.dma_start(w.x[:], pairs_of_tiles(x)[:, 1:PAIRS + 1][:, bass.ds(pair, 1), :, :]).then_inc(s["loaded"], 16)
                act.wait_ge(s["loaded"], 16)

            @block.sync
            def _(sp):
                sp.wait_ge(s["summed"], 1)
                sp.dma_start(pairs_of_tiles(out)[:, bass.ds(pair, 1), :, :], result[:]).then_inc(s["stored"], 16)
                sp.wait_ge(s["stored"], 16)
        clear(nc, s)


def turned_inputs(inputs):
    return {
        "ln_g_by_feature": np.ascontiguousarray(np.asarray(inputs["L0_ffn_ln_g"]).T),
        "ln_b_by_feature": np.ascontiguousarray(np.asarray(inputs["L0_ffn_ln_b"]).T),
        "x_and_one_pair_more": np.concatenate([np.asarray(inputs["L0_attn_a_x"]), np.asarray(inputs["L0_attn_a_x"])[:NB]]),
        "bq_by_group": np.ascontiguousarray(np.asarray(inputs["L0_attn_b_bq"]).reshape(GB, D // GB).T),
        "bk_by_group": np.ascontiguousarray(np.asarray(inputs["L0_attn_b_bk"]).reshape(GB, D // GB).T),
        "w2_transposed": np.ascontiguousarray(np.asarray(inputs["L0_attn_b_w2"]).T),
        "angles_by_pair": np.ascontiguousarray(np.asarray(inputs["L0_attn_b_rot"])[:, 0:NQ // 2, 0].T),
    }


INPUTS = ["L0_attn_a_Wq", "L0_attn_a_Wk", "L0_attn_a_Wv", "L0_attn_a_Wo",
          "L0_attn_a_polarity_direction", "L0_attn_a_gtp_gamma", "L0_attn_b_wq", "L0_attn_b_wk", "L0_attn_b_wv", "L0_attn_b_bv", "L0_attn_b_wo", "L0_attn_b_bo", "L0_attn_b_w1",
          "L0_attn_b_b1", "L0_attn_b_b2", "L0_attn_b_hadamard", "L0_ffn_wqkv",
          "L0_ffn_q_scale", "L0_ffn_k_scale", "L0_ffn_wo", "L0_ffn_w1", "L0_ffn_b1",
          "L0_ffn_w2", "L0_ffn_b2"]


def kernel(**inputs):
    import concourse.bacc as bacc
    from concourse.bass_utils import run_bass_kernel_spmd

    nc = bacc.Bacc("TRN2", target_bir_lowering=False, num_devices=1)
    arrays, a, consts = {}, {}, {}
    for name, array in {**{n: np.ascontiguousarray(inputs[n]) for n in INPUTS}, **turned_inputs(inputs)}.items():
        arrays[f"in_{name}"] = array
        a[name] = nc.dram_tensor(f"in_{name}", array.shape, mybir.dt.from_np(array.dtype), kind="ExternalInput").ap()
    for name, array in shape_constants().items():
        arrays[f"const_{name}"] = array
        consts[name] = nc.dram_tensor(f"const_{name}", array.shape, F32, kind="ExternalInput").ap()
    out = nc.dram_tensor("out_0", (BATCH, T, D), F32, kind="ExternalOutput").ap()
    build(nc, a, consts, out)
    result = run_bass_kernel_spmd(nc, [arrays], core_ids=[0])
    return result.results[0]["out_0"]
```
